# Optimizing a Trainium2 kernel written in Bass

```python
import numpy as np
import jax
import jax.numpy as jnp

def _softmax(x, axis=-1):
    return jax.nn.softmax(x, axis=axis)

def _gelu(x):
    return jax.nn.gelu(x, approximate=True)

def _silu(x):
    return jax.nn.silu(x)

def _sigmoid(x):
    return jax.nn.sigmoid(x)

def _layernorm(x, axis=-1, eps=1e-05):
    m = jnp.mean(x, axis=axis, keepdims=True)
    v = jnp.var(x, axis=axis, keepdims=True)
    return (x - m) / jnp.sqrt(v + eps)

def _scatter_add(tgt, idx, src, axis=0):
    return tgt.at[idx].add(src)

def _segment_sum(src, seg, n):
    return jax.ops.segment_sum(src, seg, n)
kernel_name = 'mk_decoder_preln_d1_seqx_r4_b42679'

def setup_inputs(seed: int=0):
    np.random.seed(seed)
    _w = jnp.asarray

    def _rec_inputs():
        import jax
        import jax.numpy as jnp
        _rk = jax.random.key(seed)
        x = 7.22e-05 + 1 * jax.random.normal(jax.random.fold_in(_rk, 1), (32, 100, 256), jnp.float32)
        _lenS = 100 - jax.random.randint(jax.random.fold_in(_rk, 7), (32,), 0, max(1, 100 // 4) + 1, jnp.int32)
        _lenS2 = 361 - jax.random.randint(jax.random.fold_in(_rk, 8), (32,), 0, max(1, 361 // 4) + 1, jnp.int32)
        _ctx_1024P = jax.random.normal(jax.random.fold_in(_rk, 11), (32, 16, 256), jnp.float32)
        _ctx_1024c = jax.random.dirichlet(jax.random.fold_in(_rk, 511), 0.3 * jnp.ones((16,), jnp.float32), (32, 361))
        _ctx_1024t = jnp.einsum('bsk,bkd->bsd', _ctx_1024c, _ctx_1024P)
        _ctx_1024t = _ctx_1024t * jax.lax.rsqrt(jnp.mean(jnp.square(_ctx_1024t)) + 1e-12) * 0.953939
        ctx_1024 = 4.13588e-05 + 0.999923 * (_ctx_1024t + 0.3 * jax.random.normal(jax.random.fold_in(_rk, 611), (32, 361, 256), jnp.float32))
        return (x, ctx_1024)
    x, ctx_1024 = _rec_inputs()

    def _L0_attn_setup():
        import jax, jax.numpy as jnp
        import numpy as np
        D_MODEL = 256
        N_HEADS = 16
        D_K = D_MODEL // N_HEADS
        THETA = 10000.0

        def _rope(x, pos):
            half = D_K // 2
            inv_freq = THETA ** (-jnp.arange(0, half, dtype=jnp.float32) * 2.0 / D_K)
            ang = pos[:, None].astype(jnp.float32) * inv_freq[None, :]
            cos, sin = (jnp.cos(ang), jnp.sin(ang))
            x1, x2 = (x[..., 0::2], x[..., 1::2])
            r1 = x1 * cos - x2 * sin
            r2 = x1 * sin + x2 * cos
            out = jnp.stack([r1, r2], axis=-1).reshape(x.shape)
            return out
        key = jax.random.key(seed)
        ks = jax.random.split(key, 5)
        b, s = (4, 512)
        sc = 1.0 / np.sqrt(D_MODEL)
        return {'x': jax.random.normal(ks[0], (b, s, D_MODEL), dtype=jnp.float32), 'Wq': jax.random.normal(ks[1], (D_MODEL, D_MODEL), dtype=jnp.float32) * sc, 'Wk': jax.random.normal(ks[2], (D_MODEL, D_MODEL), dtype=jnp.float32) * sc, 'Wv': jax.random.normal(ks[3], (D_MODEL, D_MODEL), dtype=jnp.float32) * sc, 'Wo': jax.random.normal(ks[4], (D_MODEL, D_MODEL), dtype=jnp.float32) * sc}
    _L0_attn_all = _L0_attn_setup()
    _L0_attn_in = {k: v for k, v in _L0_attn_all.items() if k in ('Wq', 'Wk', 'Wv', 'Wo')}
    del _L0_attn_all

    def _L0_xattn_setup():
        import jax, jax.numpy as jnp
        import numpy as np
        D_MODEL = 256
        N_HEADS = 16
        HEAD_DIM = D_MODEL // N_HEADS
        SCALE = HEAD_DIM ** (-0.5)
        key = jax.random.key(seed)
        ks = jax.random.split(key, 11)
        B, L = (4, 512)
        s = 1.0 / np.sqrt(D_MODEL)
        inp = {'queries': jax.random.normal(ks[0], (B, L, D_MODEL), jnp.float32), 'keys': jax.random.normal(ks[1], (B, L, D_MODEL), jnp.float32), 'values': jax.random.normal(ks[2], (B, L, D_MODEL), jnp.float32), 'Wq': jax.random.normal(ks[3], (D_MODEL, D_MODEL), jnp.float32) * s, 'bq': jnp.zeros((D_MODEL,), jnp.float32), 'Wk': jax.random.normal(ks[4], (D_MODEL, D_MODEL), jnp.float32) * s, 'bk': jnp.zeros((D_MODEL,), jnp.float32), 'Wv': jax.random.normal(ks[5], (D_MODEL, D_MODEL), jnp.float32) * s, 'bv': jnp.zeros((D_MODEL,), jnp.float32), 'Wo': jax.random.normal(ks[6], (D_MODEL, D_MODEL), jnp.float32) * s, 'bo': jnp.zeros((D_MODEL,), jnp.float32)}
        return inp
    _L0_xattn_all = _L0_xattn_setup()
    _L0_xattn_in = {k: v for k, v in _L0_xattn_all.items() if k in ('Wq', 'bq', 'Wk', 'bk', 'Wv', 'bv', 'Wo', 'bo')}
    del _L0_xattn_all

    def _L0_ffn_setup():
        import jax, jax.numpy as jnp
        import numpy as np
        B, SEQ, DIM = (2, 1024, 256)
        E, S = (8, 128)
        HID = 4 * DIM
        SCALE = DIM ** 0.5

        def rmsnorm(x, gamma):
            n = jnp.linalg.norm(x, axis=-1, keepdims=True)
            return x / jnp.maximum(n, 1e-12) * SCALE * gamma
        key = jax.random.key(seed)
        ks = jax.random.split(key, 4)
        w_init = lambda k, shape: jax.random.normal(k, shape, dtype=jnp.float32) * 0.02
        return {'x': jax.random.normal(ks[0], (B, SEQ, DIM), dtype=jnp.float32), 'norm_gamma': jnp.ones((DIM,), jnp.float32), 'slot_norm_gamma': jnp.ones((DIM,), jnp.float32), 'slot_embeds': jax.random.normal(ks[1], (E, S, DIM), dtype=jnp.float32), 'w1': w_init(ks[2], (E, DIM, HID)), 'b1': jnp.zeros((E, HID), jnp.float32), 'w2': w_init(ks[3], (E, HID, DIM)), 'b2': jnp.zeros((E, DIM), jnp.float32)}
    _L0_ffn_all = _L0_ffn_setup()
    _L0_ffn_in = {k: v for k, v in _L0_ffn_all.items() if k in ('norm_gamma', 'slot_norm_gamma', 'slot_embeds', 'w1', 'b1', 'w2', 'b2')}
    del _L0_ffn_all
    return {'x': x, 'ctx_1024': ctx_1024, 'L0_attn_Wq': _L0_attn_in['Wq'], 'L0_attn_Wk': _L0_attn_in['Wk'], 'L0_attn_Wv': _L0_attn_in['Wv'], 'L0_attn_Wo': _L0_attn_in['Wo'], 'L0_xattn_Wq': _L0_xattn_in['Wq'], 'L0_xattn_bq': _L0_xattn_in['bq'], 'L0_xattn_Wk': _L0_xattn_in['Wk'], 'L0_xattn_bk': _L0_xattn_in['bk'], 'L0_xattn_Wv': _L0_xattn_in['Wv'], 'L0_xattn_bv': _L0_xattn_in['bv'], 'L0_xattn_Wo': _L0_xattn_in['Wo'], 'L0_xattn_bo': _L0_xattn_in['bo'], 'L0_ffn_norm_gamma': _L0_ffn_in['norm_gamma'], 'L0_ffn_slot_norm_gamma': _L0_ffn_in['slot_norm_gamma'], 'L0_ffn_slot_embeds': _L0_ffn_in['slot_embeds'], 'L0_ffn_w1': _L0_ffn_in['w1'], 'L0_ffn_b1': _L0_ffn_in['b1'], 'L0_ffn_w2': _L0_ffn_in['w2'], 'L0_ffn_b2': _L0_ffn_in['b2']}

def reference(x, ctx_1024, L0_attn_Wq, L0_attn_Wk, L0_attn_Wv, L0_attn_Wo, L0_xattn_Wq, L0_xattn_bq, L0_xattn_Wk, L0_xattn_bk, L0_xattn_Wv, L0_xattn_bv, L0_xattn_Wo, L0_xattn_bo, L0_ffn_norm_gamma, L0_ffn_slot_norm_gamma, L0_ffn_slot_embeds, L0_ffn_w1, L0_ffn_b1, L0_ffn_w2, L0_ffn_b2):
    import jax
    import jax.numpy as jnp

    def _L0_attn_ref(x, Wq, Wk, Wv, Wo):
        import jax, jax.numpy as jnp
        import numpy as np
        D_MODEL = 256
        N_HEADS = 16
        D_K = D_MODEL // N_HEADS
        THETA = 10000.0

        def _rope(x, pos):
            half = D_K // 2
            inv_freq = THETA ** (-jnp.arange(0, half, dtype=jnp.float32) * 2.0 / D_K)
            ang = pos[:, None].astype(jnp.float32) * inv_freq[None, :]
            cos, sin = (jnp.cos(ang), jnp.sin(ang))
            x1, x2 = (x[..., 0::2], x[..., 1::2])
            r1 = x1 * cos - x2 * sin
            r2 = x1 * sin + x2 * cos
            out = jnp.stack([r1, r2], axis=-1).reshape(x.shape)
            return out
        b, s, _ = x.shape
        pos = jnp.arange(s)

        def split_heads(t):
            return t.reshape(b, s, N_HEADS, D_K).transpose(0, 2, 1, 3).reshape(b * N_HEADS, s, D_K)
        q = split_heads(x @ Wq.T)
        k = split_heads(x @ Wk.T)
        v = split_heads(x @ Wv.T)
        q = _rope(q, pos)
        k = _rope(k, pos)
        score = jnp.einsum('bqd,bkd->bqk', q, k)
        causal = jnp.tril(jnp.ones((s, s), dtype=bool))
        score = jnp.where(causal[None], score, -jnp.inf)
        attn = jax.nn.softmax(score / jnp.sqrt(jnp.float32(D_K)), axis=-1)
        out = jnp.einsum('bqk,bkd->bqd', attn, v)
        out = out.reshape(b, N_HEADS, s, D_K).transpose(0, 2, 1, 3).reshape(b, s, D_MODEL)
        return out @ Wo.T

    def _L0_xattn_ref(queries, keys, values, Wq, bq, Wk, bk, Wv, bv, Wo, bo):
        import jax, jax.numpy as jnp
        import numpy as np
        D_MODEL = 256
        N_HEADS = 16
        HEAD_DIM = D_MODEL // N_HEADS
        SCALE = HEAD_DIM ** (-0.5)
        B, L, _ = queries.shape
        S = keys.shape[1]
        q = (queries @ Wq + bq).reshape(B, L, N_HEADS, HEAD_DIM).transpose(0, 2, 1, 3)
        k = (keys @ Wk + bk).reshape(B, S, N_HEADS, HEAD_DIM).transpose(0, 2, 1, 3)
        v = (values @ Wv + bv).reshape(B, S, N_HEADS, HEAD_DIM).transpose(0, 2, 1, 3)
        scores = jnp.einsum('bhld,bhsd->bhls', q, k) * SCALE
        weights = jax.nn.softmax(scores, axis=-1)
        out = jnp.einsum('bhls,bhsd->bhld', weights, v)
        out = out.transpose(0, 2, 1, 3).reshape(B, L, D_MODEL)
        out = out @ Wo + bo
        return out

    def _L0_ffn_ref(x, norm_gamma, slot_norm_gamma, slot_embeds, w1, b1, w2, b2):
        import jax, jax.numpy as jnp
        import numpy as np
        B, SEQ, DIM = (2, 1024, 256)
        E, S = (8, 128)
        HID = 4 * DIM
        SCALE = DIM ** 0.5

        def rmsnorm(x, gamma):
            n = jnp.linalg.norm(x, axis=-1, keepdims=True)
            return x / jnp.maximum(n, 1e-12) * SCALE * gamma
        xn = rmsnorm(x, norm_gamma)
        sn = rmsnorm(slot_embeds, slot_norm_gamma)
        logits = jnp.einsum('bnd,esd->bnes', xn, sn)
        dispatch = jax.nn.softmax(logits, axis=1)
        b, n, e, s = logits.shape
        combine = jax.nn.softmax(logits.reshape(b, n, e * s), axis=-1)
        slots = jnp.einsum('bnd,bnes->besd', xn, dispatch)
        h = jnp.einsum('besd,edh->besh', slots, w1) + b1[None, :, None, :]
        h = jax.nn.gelu(h, approximate=False)
        eo = jnp.einsum('besh,ehd->besd', h, w2) + b2[None, :, None, :]
        eo = eo.reshape(b, e * s, DIM)
        out = jnp.einsum('bmd,bnm->bnd', eo, combine)
        return out
    x = x + _L0_attn_ref(_layernorm(x, axis=-1), L0_attn_Wq, L0_attn_Wk, L0_attn_Wv, L0_attn_Wo)
    x = x + _L0_xattn_ref(_layernorm(x, axis=-1), ctx_1024, ctx_1024, L0_xattn_Wq, L0_xattn_bq, L0_xattn_Wk, L0_xattn_bk, L0_xattn_Wv, L0_xattn_bv, L0_xattn_Wo, L0_xattn_bo)
    x = x + _L0_ffn_ref(_layernorm(x, axis=-1), L0_ffn_norm_gamma, L0_ffn_slot_norm_gamma, L0_ffn_slot_embeds, L0_ffn_w1, L0_ffn_b1, L0_ffn_w2, L0_ffn_b2)
    return x

_drawn_inputs = setup_inputs


def setup_inputs(seed=0):
    import zlib

    import numpy as np

    out = dict(_drawn_inputs(seed))
    spreads = {'L0_xattn_bq': (0.0, 0.379),
     'L0_xattn_bk': (0.0, 0.8),
     'L0_xattn_bv': (0.0, 0.1),
     'L0_xattn_bo': (0.0, 0.1),
     'L0_ffn_norm_gamma': (1.0, 0.2),
     'L0_ffn_slot_norm_gamma': (1.0, 0.2),
     'L0_ffn_b1': (0.0, 0.273),
     'L0_ffn_b2': (0.0, 0.1)}
    factors = {}
    for name, (base, spread) in spreads.items():
        noise = np.random.default_rng([zlib.crc32(name.encode()), seed]).standard_normal(out[name].shape)
        drawn = base * np.exp(spread * noise) if base else spread * noise
        out[name] = jnp.asarray(drawn.astype(out[name].dtype))
    for name, factor in factors.items():
        out[name] = (out[name] * factor).astype(out[name].dtype)
    return out
```

```python
from contextlib import ExitStack

import numpy as np

import concourse.bass as bass
from concourse import mybir

ALU = mybir.AluOpType
ACT = mybir.ActivationFunctionType
F32 = mybir.dt.float32
F32R = mybir.dt.float32r
BF16 = mybir.dt.bfloat16
X = mybir.AxisListType.X
ALL_MAX = bass.bass_isa.ReduceOp.max

B, S, D = 32, 100, 256
SC = 361
H, DK = 16, 16
P = 128
DC = D // P
ROWS = 4
HP = H // ROWS
KEYS = [121, 120, 120]
KEY0 = [0, 121, 241]
ER = 3
VA = DK + 1
E, HID = 8, 1024
HC = HID // P
GB = 4
G = B // GB
M3 = [7, 8, 6]
EPS = 1e-5


def head_of(row, hp):
    return 8 * (hp // 2) + 2 * row + hp % 2


class Stages:

    def __init__(self, engine, stages, count):
        lags = [lag for _, lag in stages]
        least, deepest = min(lags), max(lags)
        begin = deepest + 1 + (deepest + 1) % 2
        end = count + least - (count + least) % 2

        def step(i, turn):
            for stage, lag in stages:
                b = i - lag
                if not isinstance(b, int) or 0 <= b < count:
                    stage(b, (turn - lag) % 2)

        for i in range(least, begin):
            step(i, i)
        with engine.Fori(begin // 2, end // 2) as pair:
            step(2 * pair, 0)
            step(2 * pair + 1, 1)
        for i in range(end, count + deepest):
            step(i, i)


def later(b, n=1):
    return not isinstance(b, int) or b >= n


def norm_statistics(nc, x_all, mv, rstd, stats, name, first):
    with ExitStack() as ctx:
        sem = lambda n: ctx.enter_context(nc.semaphore(f"{name}_{n}"))
        stats_done, aggr_done, eps_added, root_done, rstd_done = (
            sem(n) for n in ("stats_done", "aggr_done", "eps_added", "root_done", "rstd_done"))
        block = ctx.enter_context(nc.Block())

        @block.vector
        def _(dve):
            if first:
                with dve.Fori(0, B) as b:
                    dve.bn_stats(stats[:, b, :], x_all[:, b, :]).then_inc(stats_done, 1)
                dve.wait_ge(stats_done, B)
            for b in range(B):
                dve.bn_aggr(mv[:, b, :], stats[:, b, :]).then_inc(aggr_done, 1)
            dve.wait_ge(aggr_done, B)
            dve.tensor_scalar(rstd[:], mv[:, :, 1], EPS, None, ALU.add).then_inc(eps_added, 1)
            dve.wait_ge(root_done, 1)
            dve.reciprocal(rstd[:], rstd[:]).then_inc(rstd_done, 1)
            dve.wait_ge(rstd_done, 1)

        @block.scalar
        def _(act):
            act.wait_ge(eps_added, 1)
            act.activation(rstd[:], rstd[:], ACT.Sqrt).then_inc(root_done, 1)


def self_attention(nc, x_all, mv, rstd, stats, ident, wqkv_dram, wo_dram, cos_dram, sin_dram, mask_dram):
    with ExitStack() as ctx:
        sb = lambda n, shape, dt=F32: ctx.enter_context(nc.sbuf_tensor(f"sa_{n}", shape, dt))
        pb = lambda n, shape: ctx.enter_context(nc.psum_tensor(f"sa_{n}", shape, F32))
        sem = lambda n: ctx.enter_context(nc.semaphore(f"sa_{n}"))

        w_qkv = sb("w_qkv", [P, DC, 3 * D])
        w_o = sb("w_o", [P, DC, D])
        cos_t = sb("cos_t", [S, 2 * D])
        sin_t = sb("sin_t", [S, 2 * D])
        mask = sb("mask", [S, S])
        xn = sb("xn", [S, D])
        xnT = sb("xnT", [P, DC, S])
        t_cos = sb("t_cos", [S, 2 * D])
        t_sin = sb("t_sin", [S, 2 * D])
        q_split = sb("q_split", [S, HP, ROWS, 2 * DK])
        k_rot = sb("k_rot", [S, D])
        qT = sb("qT", [P, HP, S])
        kT = sb("kT", [P, DC, S])
        v_aug = sb("v_aug", [S, 3, H, VA])
        e = sb("e", [S, ROWS, HP, S])
        mx = sb("mx", [S, H])
        eT = sb("eT", [S, ROWS, HP, S])
        rsum = sb("rsum", [S, H])
        o = sb("o", [S, D])
        oT = sb("oT", [P, DC, S])

        p_a = pb("p_a", [P, 512])
        p_b = pb("p_b", [P, 512])
        p_t0 = pb("p_t0", [P, 512])
        p_t1 = pb("p_t1", [P, 512])
        p_s = pb("p_s", [P, ROWS, 512])
        p_t = [p_t0, p_t1]

        loaded = sem("loaded")
        cleared = sem("cleared")
        xn_ready = sem("xn_ready")
        xnT_made = sem("xnT_made")
        xnT_ready = sem("xnT_ready")
        qk_made = sem("qk_made")
        v_made = sem("v_made")
        v_ready = sem("v_ready")
        rot_terms = sem("rot_terms")
        rotated = sem("rotated")
        qT_made = sem("qT_made")
        kT_made = sem("kT_made")
        qT_ready = sem("qT_ready")
        kT_ready = sem("kT_ready")
        s_made = sem("s_made")
        masked = sem("masked")
        max_ready = sem("max_ready")
        shifted = sem("shifted")
        e_ready = sem("e_ready")
        eT_made = sem("eT_made")
        eT_ready = sem("eT_ready")
        pv_made = sem("pv_made")
        rsum_ready = sem("rsum_ready")
        o_ready = sem("o_ready")
        oT_made = sem("oT_made")
        oT_ready = sem("oT_ready")
        out_made = sem("out_made")
        x_added = sem("x_added")
        stats_kept = sem("stats_kept")

        block = ctx.enter_context(nc.Block())

        @block.sync
        def _(sp):
            sp.dma_start(w_qkv[:], wqkv_dram).then_inc(loaded, 16)
            sp.dma_start(w_o[:], wo_dram).then_inc(loaded, 16)
            sp.dma_start(cos_t[:], cos_dram).then_inc(loaded, 16)
            sp.dma_start(sin_t[:], sin_dram).then_inc(loaded, 16)
            sp.dma_start(mask[:], mask_dram).then_inc(loaded, 16)
            sp.wait_ge(loaded, 80)

        @block.tensor
        def _(pe):
            pe.wait_ge(loaded, 80)

            def transpose_xn(b, slot):
                pe.wait_ge(xn_ready, b + 1)
                if later(b):
                    pe.wait_ge(qT_ready, b)
                for c in range(DC):
                    mm = pe.transpose(p_a[:, c * S:(c + 1) * S], xn[:, c * P:(c + 1) * P], ident[0:S, 0:S])
                mm.then_inc(xnT_made, 1)

            def transpose_e(b, slot):
                for j in range(ROWS):
                    if j == 0:
                        pe.wait_ge(e_ready, b + 1)
                    if j >= 2:
                        pe.wait_ge(eT_ready, ROWS * b + j - 1)
                    elif j == 0 and later(b):
                        pe.wait_ge(x_added, b)
                    elif j == 1 and later(b):
                        pe.wait_ge(oT_ready, b)
                    for hp in range(HP):
                        mm = pe.transpose(p_t[j % 2][0:S, hp * S:(hp + 1) * S], e[:, j, hp, :], ident[0:S, 0:S])
                    mm.then_inc(eT_made, 1)

            def project_qkv(b, slot):
                pe.wait_ge(xnT_ready, b + 1)
                if later(b):
                    pe.wait_ge(kT_ready, b)
                for c in range(DC):
                    mm = pe.matmul(p_b[0:S, :], xnT[:, c, :], w_qkv[:, c, 0:2 * D], start=c == 0, stop=c == DC - 1)
                mm.then_inc(qk_made, 1)
                for c in range(DC):
                    mm = pe.matmul(p_a[0:S, 0:D], xnT[:, c, :], w_qkv[:, c, 2 * D:3 * D],
                                   start=c == 0, stop=c == DC - 1)
                mm.then_inc(v_made, 1)

            def scores(b, slot):
                pe.wait_ge(qT_ready, b + 1)
                pe.wait_ge(kT_ready, b + 1)
                if later(b):
                    pe.wait_ge(masked, ROWS * b)
                for hp in range(HP):
                    for j in range(ROWS):
                        mm = pe.matmul(p_s[0:S, j, hp * S:(hp + 1) * S], qT[32 * j:32 * j + 32, hp, :],
                                       kT[32 * j:32 * j + 32, hp // 2, :], start=True, stop=True)
                mm.then_inc(s_made, 1)

            def weigh_values(b, slot):
                pe.wait_ge(eT_ready, ROWS * (b + 1))
                pe.wait_ge(v_ready, b + 1)
                for j in range(ROWS):
                    for hp in range(HP):
                        h = head_of(j, hp)
                        mm = pe.matmul(p_t0[0:S, h * VA:(h + 1) * VA], eT[:, j, hp, :], v_aug[:, b % 3, h, :],
                                       start=True, stop=True)
                mm.then_inc(pv_made, 1)

            def transpose_qk(b, slot):
                pe.wait_ge(rotated, 3 * b + 3)
                pe.wait_ge(v_ready, b + 1)
                for hp in range(HP):
                    mm = pe.transpose(p_a[:, hp * S:(hp + 1) * S],
                                      q_split[:, hp, :, :].rearrange("s r f -> s (r f)"), ident[0:S, 0:S])
                mm.then_inc(qT_made, 1)
                for c in range(DC):
                    mm = pe.transpose(p_b[:, c * S:(c + 1) * S], k_rot[:, c * P:(c + 1) * P], ident[0:S, 0:S])
                mm.then_inc(kT_made, 1)

            def transpose_o(b, slot):
                pe.wait_ge(o_ready, b + 1)
                for c in range(DC):
                    mm = pe.transpose(p_t1[:, c * S:(c + 1) * S], o[:, c * P:(c + 1) * P], ident[0:S, 0:S])
                mm.then_inc(oT_made, 1)

            def project_out(b, slot):
                pe.wait_ge(oT_ready, b + 1)
                for c in range(DC):
                    mm = pe.matmul(p_t0[0:S, 0:D], oT[:, c, :], w_o[:, c, :], start=c == 0, stop=c == DC - 1)
                mm.then_inc(out_made, 1)

            Stages(pe, [
                (transpose_xn, 0),
                (transpose_e, 2),
                (scores, 1),
                (project_qkv, 0),
                (weigh_values, 2),
                (transpose_qk, 0),
                (transpose_o, 2),
                (project_out, 2),
            ], B)

        @block.vector
        def _(dve):
            dve.memset(q_split[:], 0.0).then_inc(cleared, 1)
            dve.memset(v_aug[:], 1.0).then_inc(cleared, 1)
            dve.wait_ge(cleared, 2)
            dve.wait_ge(loaded, 80)

            def normalise(b, slot):
                if later(b):
                    dve.wait_ge(xnT_made, b)
                dve.tensor_scalar(xn[:], x_all[:, b, :], mv[:, b, 0:1], rstd[:, bass.ds(b, 1)],
                                  ALU.subtract, ALU.mult).then_inc(xn_ready, 1)

            def rotate(b, slot):
                dve.wait_ge(qk_made, b + 1)
                if later(b):
                    dve.wait_ge(rotated, 3 * b)
                dve.tensor_tensor(t_cos[:], p_b[0:S, :], cos_t[:], ALU.mult).then_inc(rot_terms, 1)
                dve.tensor_tensor(t_sin[:, 0::2], p_b[0:S, 1::2], sin_t[:, 0::2], ALU.mult).then_inc(rot_terms, 1)
                dve.tensor_tensor(t_sin[:, 1::2], p_b[0:S, 0::2], sin_t[:, 1::2], ALU.mult).then_inc(rot_terms, 1)
                dve.wait_ge(rot_terms, 3 * b + 3)
                if later(b):
                    dve.wait_ge(kT_made, b)
                parts = lambda t: t[:, 0:D].rearrange("s (f r p d) -> s f r p d", f=2, r=ROWS, p=2)
                split = q_split[:, :, :, :].rearrange("s (f p) r d -> s f p r d", p=2)
                for par in range(2):
                    dve.tensor_tensor(split[:, :, par, :, par * DK:(par + 1) * DK], parts(t_cos)[:, :, :, par, :],
                                      parts(t_sin)[:, :, :, par, :], ALU.add).then_inc(rotated, 1)
                dve.tensor_tensor(k_rot[:], t_cos[:, D:2 * D], t_sin[:, D:2 * D], ALU.add).then_inc(rotated, 1)

            def mask_scores(b, slot):
                dve.wait_ge(s_made, b + 1)
                if later(b):
                    dve.wait_ge(eT_made, ROWS * b)
                for j in range(ROWS):
                    dve.tensor_tensor(e[:, j, :, :], p_s[0:S, j, 0:HP * S].rearrange("q (h k) -> q h k", h=HP),
                                            mask[:, :].unsqueeze(1).broadcast_to([S, HP, S]),
                                      ALU.add).then_inc(masked, 1)
                dve.wait_ge(masked, ROWS * (b + 1))
                dve.tensor_reduce(mx[:], e[:].rearrange("q r h k -> q (r h) k"), X, ALU.max).then_inc(max_ready, 1)

            def divide(b, slot):
                dve.wait_ge(pv_made, b + 1)
                if later(b):
                    dve.wait_ge(o_ready, b)
                pv = p_t0[0:S, 0:H * VA].rearrange("q (h d) -> q h d", h=H)
                dve.reciprocal(rsum[:], pv[:, :, DK]).then_inc(rsum_ready, 1)
                dve.wait_ge(rsum_ready, b + 1)
                dve.tensor_tensor(o[:].rearrange("q (h d) -> q h d", h=H), pv[:, :, 0:DK],
                                  rsum[:].unsqueeze(2).broadcast_to([S, H, DK]), ALU.mult).then_inc(o_ready, 1)

            def add_to_x(b, slot):
                dve.wait_ge(out_made, b + 1)
                dve.tensor_tensor(x_all[:, b, :], p_t0[0:S, 0:D], x_all[:, b, :], ALU.add).then_inc(x_added, 1)
                dve.wait_ge(x_added, b + 1)
                dve.bn_stats(stats[:, b, :], x_all[:, b, :]).then_inc(stats_kept, 1)

            Stages(dve, [
                (mask_scores, 1),
                (rotate, 0),
                (divide, 2),
                (add_to_x, 2),
                (normalise, -1),
            ], B)

        @block.scalar
        def _(act):
            act.wait_ge(cleared, 2)

            def copy_xnT(b, slot):
                act.wait_ge(xnT_made, b + 1)
                if later(b):
                    act.wait_ge(v_made, b)
                act.copy(xnT[:].rearrange("p c s -> p (c s)"), p_a[:, 0:DC * S]).then_inc(xnT_ready, 1)

            def copy_eT(b, slot):
                for j in range(ROWS):
                    act.wait_ge(eT_made, ROWS * b + j + 1)
                    if j == 0 and later(b):
                        act.wait_ge(pv_made, b)
                    act.copy(eT[:, j, :, :].rearrange("k h q -> k (h q)"),
                             p_t[j % 2][0:S, 0:HP * S]).then_inc(eT_ready, 1)

            def copy_v(b, slot):
                act.wait_ge(v_made, b + 1)
                if later(b, 3):
                    act.wait_ge(pv_made, b - 2)
                act.copy(v_aug[:, b % 3, :, 0:DK], p_a[0:S, 0:D].rearrange("k (h d) -> k h d", h=H)).then_inc(v_ready, 1)

            def copy_qkT(b, slot):
                act.wait_ge(qT_made, b + 1)
                if later(b):
                    act.wait_ge(s_made, b)
                act.copy(qT[:].rearrange("p h s -> p (h s)"), p_a[:, 0:HP * S]).then_inc(qT_ready, 1)
                act.wait_ge(kT_made, b + 1)
                act.copy(kT[:].rearrange("p c s -> p (c s)"), p_b[:, 0:DC * S]).then_inc(kT_ready, 1)

            def copy_oT(b, slot):
                act.wait_ge(oT_made, b + 1)
                if later(b):
                    act.wait_ge(out_made, b)
                act.copy(oT[:].rearrange("p c s -> p (c s)"), p_t1[:, 0:DC * S]).then_inc(oT_ready, 1)

            def exponentiate(b, slot):
                act.wait_ge(shifted, b + 1)
                flat = e[:].rearrange("q r h k -> q (r h k)")
                act.activation(flat, flat, ACT.Exp, scale=DK ** -0.5).then_inc(e_ready, 1)

            Stages(act, [
                (copy_xnT, 0),
                (copy_eT, 2),
                (copy_v, 0),
                (copy_qkT, 0),
                (copy_oT, 2),
                (exponentiate, 1),
            ], B)

        @block.gpsimd
        def _(pool):
            def shift(b, slot):
                pool.wait_ge(max_ready, b + 1)
                rows = e[:].rearrange("q r h k -> q (r h) k")
                pool.tensor_tensor(rows, rows, mx[:].unsqueeze(2).broadcast_to([S, H, S]),
                                   ALU.subtract).then_inc(shifted, 1)

            Stages(pool, [(shift, 1)], B)


def cross_attention(nc, x_all, mv, rstd, stats, ident, ident16, ctx_dram, w, shift_mask_dram):
    with ExitStack() as ctx:
        sb = lambda n, shape, dt=F32: ctx.enter_context(nc.sbuf_tensor(f"xa_{n}", shape, dt))
        pb = lambda n, shape, dt=F32: ctx.enter_context(nc.psum_tensor(f"xa_{n}", shape, dt))
        sem = lambda n: ctx.enter_context(nc.semaphore(f"xa_{n}"))

        w_q = sb("w_q", [P, DC, D])
        w_k = sb("w_k", [P, DC, D])
        w_v = sb("w_v", [P, DC, D])
        w_o = sb("w_o", [P, DC, D])
        b_q = sb("b_q", [S, D])
        b_k = sb("b_k", [P, DC])
        b_v = sb("b_v", [S, D])
        b_o = sb("b_o", [S, D])
        shift_mask = sb("shift_mask", [P, HP, S])
        ones = sb("ones", [P, KEYS[0]], BF16)
        context = sb("context", [P, 2, DC, SC])
        xn = sb("xn", [S, D])
        xnT = sb("xnT", [P, DC, S])
        q_split = sb("q_split", [S, HP, ROWS, 2 * DK])
        qT = sb("qT", [P, 2, HP, S])
        kT = sb("kT", [P, 2, DC, SC])
        v_aug = sb("v_aug", [KEYS[0], 2, len(KEYS), H, VA])
        nmax = sb("nmax", [S, HP, ROWS])
        nmax2 = sb("nmax2", [S, ROWS, 2 * DK], BF16)
        shift = sb("shift", [P, HP, S], BF16)
        eT = sb("eT", [KEYS[0], ER, HP, S])
        rsum = sb("rsum", [S, H])
        o = sb("o", [S, D])
        oT = sb("oT", [P, DC, S])

        p_m = pb("p_m", [P, 512])
        p_o = pb("p_o", [P, 512])
        p_e = [pb(f"p_e{i}", [P, 512]) for i in range(2)]
        p_s = pb("p_s", [P, ROWS, 512])

        loaded = sem("loaded")
        cleared = sem("cleared")
        context_in = [sem("context_in0"), sem("context_in1")]
        xn_ready = sem("xn_ready")
        xnT_made = sem("xnT_made")
        xnT_ready = sem("xnT_ready")
        q_made = sem("q_made")
        q_ready = sem("q_ready")
        qT_made = sem("qT_made")
        qT_ready = sem("qT_ready")
        k_made = sem("k_made")
        k_ready = sem("k_ready")
        v_made = sem("v_made")
        v_ready = sem("v_ready")
        s_made = sem("s_made")
        max_ready = sem("max_ready")
        high_ready = sem("high_ready")
        low_ready = sem("low_ready")
        maxT_made = sem("maxT_made")
        shift_ready = sem("shift_ready")
        sT_made = sem("sT_made")
        e_ready = sem("e_ready")
        pv_unit = sem("pv_unit")
        rsum_ready = sem("rsum_ready")
        divided = sem("divided")
        o_ready = sem("o_ready")
        oT_made = sem("oT_made")
        oT_ready = sem("oT_ready")
        out_made = sem("out_made")
        x_added = sem("x_added")
        bo_added = sem("bo_added")
        stats_kept = sem("stats_kept")

        block = ctx.enter_context(nc.Block())
        NK = len(KEYS)
        UNITS = ROWS * NK
        N_LOADS = 9

        @block.sync
        def _(sp):
            for dst, src in ((w_q, w["w_q"]), (w_k, w["w_k"]), (w_v, w["w_v"]), (w_o, w["w_o"]),
                             (b_k, w["b_k"]), (shift_mask, shift_mask_dram)):
                sp.dma_start(dst[:], src).then_inc(loaded, 16)
            for dst, src in ((b_q, w["b_q"]), (b_v, w["b_v"]), (b_o, w["b_o"])):
                sp.dma_start(dst[:], src.partition_broadcast(S)).then_inc(loaded, 16)

            def load_context(b, slot):
                if later(b, 2):
                    sp.wait_ge(v_made, NK * (b - 1))
                sp.dma_start(context[:, slot], ctx_dram[b]).then_inc(context_in[slot], 16)

            Stages(sp, [(load_context, 0)], B)
            sp.wait_ge(loaded, 16 * N_LOADS)

        def in_turn(b):
            return b // 2 + 1

        @block.tensor
        def _(pe):
            pe.wait_ge(loaded, 16 * N_LOADS)

            def transpose_xn(b, slot):
                pe.wait_ge(xn_ready, b + 1)
                if later(b, 2):
                    pe.wait_ge(x_added, b - 1)
                elif later(b):
                    pe.wait_ge(v_ready, NK)
                for c in range(DC):
                    mm = pe.transpose(p_m[:, c * S:(c + 1) * S], xn[:, c * P:(c + 1) * P], ident[0:S, 0:S])
                mm.then_inc(xnT_made, 1)

            def project_q(b, slot):
                pe.wait_ge(xnT_ready, b + 1)
                for c in range(DC):
                    mm = pe.matmul(p_m[0:S, 0:D], xnT[:, c, :], w_q[:, c, :], start=c == 0, stop=c == DC - 1)
                mm.then_inc(q_made, 1)

            def transpose_q(b, slot):
                pe.wait_ge(q_ready, 2 * (b + 1))
                for hp in range(HP):
                    mm = pe.transpose(p_m[:, hp * S:(hp + 1) * S],
                                      q_split[:, hp, :, :].rearrange("s r f -> s (r f)"), ident[0:S, 0:S])
                mm.then_inc(qT_made, 1)

            def transpose_max(b, slot):
                pe.wait_ge(low_ready, b + 1)
                pe.wait_ge(qT_ready, qT_before(b))
                if isinstance(b, int) and b == B - 1:
                    pe.wait_ge(x_added, b)
                pe.transpose(p_m[:, :].bitcast(BF16)[:, 0:S], nmax2[:].rearrange("s r f -> s (r f)"),
                             ident16[0:S, 0:S]).then_inc(maxT_made, 1)

            def qT_before(b):
                if isinstance(b, int):
                    return min(b + 2, B)
                return b + 2

            def project_k(b, slot, c):
                pe.wait_ge(context_in[slot], 16 * in_turn(b))
                if c == 0:
                    pe.wait_ge(qT_ready, b + 1)
                    if later(b):
                        pe.wait_ge(shift_ready, b)
                else:
                    pe.wait_ge(k_ready, DC * b + c)
                for d in range(DC):
                    mm = pe.matmul(p_m[:, 0:SC], w_k[:, d, c * P:(c + 1) * P], context[:, slot, d, :],
                                   start=d == 0, stop=d == DC - 1)
                mm.then_inc(k_made, 1)

            def project_v(b, slot, n):
                if n == 0:
                    pe.wait_ge(k_ready, DC * (b + 1))
                else:
                    pe.wait_ge(v_ready, NK * b + n)
                for d in range(DC):
                    mm = pe.matmul(p_m[0:KEYS[n], 0:D], context[:, slot, d, KEY0[n]:KEY0[n] + KEYS[n]], w_v[:, d, :],
                                   start=d == 0, stop=d == DC - 1)
                mm.then_inc(v_made, 1)

            def scores(b, slot, hp):
                if hp == 0:
                    pe.wait_ge(k_ready, DC * (b + 1))
                    if later(b):
                        pe.wait_ge(max_ready, HP * b)
                else:
                    pe.wait_ge(max_ready, HP * b + hp)
                for j in range(ROWS):
                    mm = pe.matmul(p_s[0:S, j, 0:SC], qT[32 * j:32 * j + 32, slot, hp, :],
                                   kT[32 * j:32 * j + 32, slot, hp // 2, :], start=True, stop=True)
                mm.then_inc(s_made, 1)

            def scores_t(b, slot, u):
                j, n = divmod(u, NK)
                rows = slice(32 * j, 32 * j + 32)
                if u == 0:
                    pe.wait_ge(shift_ready, b + 1)
                if u >= 2:
                    pe.wait_ge(e_ready, UNITS * b + u - 1)
                elif later(b):
                    pe.wait_ge(e_ready, UNITS * b - 1 + u)
                nk = KEYS[n]
                pe.matmul(p_e[u % 2][0:nk, 0:HP * S], ones[rows, 0:nk], shift[rows].rearrange("h r q -> h (r q)"),
                          start=True, stop=False, skip_group_check=True)
                for half in range(DC):
                    mm = pe.matmul(p_e[u % 2][0:nk, half * 2 * S:(half + 1) * 2 * S],
                                   kT[rows, slot, half, KEY0[n]:KEY0[n] + nk],
                                   qT[rows, slot, 2 * half:2 * half + 2, :].rearrange("f h q -> f (h q)"),
                                   start=False, stop=True, skip_group_check=True)
                mm.then_inc(sT_made, 1)

            def weigh_values(b, slot, u):
                j, n = divmod(u, NK)
                pe.wait_ge(e_ready, UNITS * b + u + 1)
                if u == 0:
                    pe.wait_ge(v_ready, NK * (b + 1))
                    if later(b):
                        pe.wait_ge(divided, b)
                for hp in range(HP):
                    h = head_of(j, hp)
                    mm = pe.matmul(p_o[0:S, h * VA:(h + 1) * VA], eT[0:KEYS[n], u % ER, hp, :],
                                   v_aug[0:KEYS[n], slot, n, h, :], start=u == 0 and hp == 0, stop=n == NK - 1,
                                   skip_group_check=True)
                mm.then_inc(pv_unit, 1)

            def transpose_o(b, slot):
                pe.wait_ge(o_ready, b + 1)
                if isinstance(b, int) and b == B - 1:
                    pe.wait_ge(v_ready, NK * B)
                else:
                    pe.wait_ge(v_ready, NK * (b + 2))
                for c in range(DC):
                    mm = pe.transpose(p_m[:, c * S:(c + 1) * S], o[:, c * P:(c + 1) * P], ident[0:S, 0:S])
                mm.then_inc(oT_made, 1)

            def project_out(b, slot):
                pe.wait_ge(oT_ready, b + 1)
                for c in range(DC):
                    mm = pe.matmul(p_m[0:S, 0:D], oT[:, c, :], w_o[:, c, :], start=c == 0, stop=c == DC - 1)
                mm.then_inc(out_made, 1)

            part = lambda f, *a: (lambda b, slot: f(b, slot, *a))
            st = lambda u: (part(scores_t, u), 1)
            pv = lambda u: (part(weigh_values, u), 1)
            sc = lambda hp: (part(scores, hp), 0)
            Stages(pe, [
                (transpose_xn, 0), (project_q, 0), (transpose_q, 0), (transpose_max, 1),
                (part(project_k, 0), 0),
                st(0), st(1), (part(project_k, 1), 0),
                pv(0), st(2), pv(1), st(3), (part(project_v, 0), 0),
                pv(2), st(4), sc(0), pv(3), st(5), (part(project_v, 1), 0),
                pv(4), st(6), sc(1), pv(5), st(7), (part(project_v, 2), 0),
                pv(6), st(8), sc(2), pv(7), st(9),
                pv(8), st(10), sc(3), pv(9), st(11), pv(10), pv(11),
                (transpose_o, 1), (project_out, 1),
            ], B)

        @block.vector
        def _(dve):
            dve.memset(q_split[:], 0.0).then_inc(cleared, 1)
            dve.memset(v_aug[:], 1.0).then_inc(cleared, 1)
            dve.memset(nmax2[:], 0.0).then_inc(cleared, 1)
            dve.memset(ones[:], 1.0).then_inc(cleared, 1)
            dve.wait_ge(cleared, 4)
            dve.wait_ge(loaded, 16 * N_LOADS)

            def normalise(b, slot):
                if later(b):
                    dve.wait_ge(xnT_made, b)
                dve.tensor_scalar(xn[:], x_all[:, b, :], mv[:, b, 0:1], rstd[:, bass.ds(b, 1)],
                                  ALU.subtract, ALU.mult).then_inc(xn_ready, 1)

            def split_q(b, slot):
                dve.wait_ge(q_made, b + 1)
                if later(b):
                    dve.wait_ge(qT_made, b)
                parts = lambda t: t.rearrange("s (f r p d) -> s f r p d", f=2, r=ROWS, p=2)
                split = q_split[:, :, :, :].rearrange("s (f p) r d -> s f p r d", p=2)
                for par in range(2):
                    dve.tensor_tensor(split[:, :, par, :, par * DK:(par + 1) * DK], parts(p_m[0:S, 0:D])[:, :, :, par, :],
                                      parts(b_q[:, :])[:, :, :, par, :], ALU.add).then_inc(q_ready, 1)

            def find_max(b, slot, hp):
                dve.wait_ge(s_made, HP * b + hp + 1)
                dve.tensor_reduce(nmax[:, hp, :], p_s[0:S, :, 0:SC], X, ALU.max, negate=True).then_inc(max_ready, 1)

            def split_max(b, slot):
                dve.wait_ge(max_ready, HP * (b + 1))
                if later(b):
                    dve.wait_ge(maxT_made, b)
                most = nmax[:].rearrange("q h r -> q r h")
                high, low = nmax2[:, :, 0:HP], nmax2[:, :, HP:2 * HP]
                dve.tensor_copy(high, most).then_inc(high_ready, 1)
                dve.wait_ge(high_ready, b + 1)
                dve.tensor_tensor(low, most, high, ALU.subtract).then_inc(low_ready, 1)

            def make_shift(b, slot):
                dve.wait_ge(maxT_made, b + 1)
                if later(b):
                    dve.wait_ge(sT_made, UNITS * b)
                dve.tensor_tensor(shift[:], p_m[:, :].bitcast(BF16)[:, 0:S].unsqueeze(1).broadcast_to([P, HP, S]),
                                  shift_mask[:], ALU.mult).then_inc(shift_ready, 1)

            def divide(b, slot):
                dve.wait_ge(pv_unit, UNITS * (b + 1))
                if later(b):
                    dve.wait_ge(oT_made, b)
                pv = p_o[0:S, 0:H * VA].rearrange("q (h d) -> q h d", h=H)
                dve.reciprocal(rsum[:], pv[:, :, DK]).then_inc(rsum_ready, 1)
                dve.wait_ge(rsum_ready, b + 1)
                dve.tensor_tensor(o[:].rearrange("q (h d) -> q h d", h=H), pv[:, :, 0:DK],
                                  rsum[:].unsqueeze(2).broadcast_to([S, H, DK]), ALU.mult).then_inc(divided, 1)
                dve.wait_ge(divided, b + 1)
                dve.tensor_tensor(o[:], o[:], b_v[:], ALU.add).then_inc(o_ready, 1)

            def add_to_x(b, slot):
                dve.wait_ge(out_made, b + 1)
                dve.tensor_tensor(x_all[:, b, :], p_m[0:S, 0:D], x_all[:, b, :], ALU.add).then_inc(x_added, 1)
                dve.wait_ge(x_added, b + 1)
                dve.tensor_tensor(x_all[:, b, :], x_all[:, b, :], b_o[:], ALU.add).then_inc(bo_added, 1)
                dve.wait_ge(bo_added, b + 1)
                dve.bn_stats(stats[:, b, :], x_all[:, b, :]).then_inc(stats_kept, 1)

            part = lambda f, *a: (lambda b, slot: f(b, slot, *a))
            Stages(dve, [
                (split_q, 0), (make_shift, 1),
                *[(part(find_max, hp), 0) for hp in range(HP)],
                (split_max, 0),
                (divide, 1), (add_to_x, 1), (normalise, -1),
            ], B)

        @block.scalar
        def _(act):
            act.wait_ge(cleared, 4)
            act.wait_ge(loaded, 16 * N_LOADS)

            def copy_xnT(b, slot):
                act.wait_ge(xnT_made, b + 1)
                act.copy(xnT[:].rearrange("p c s -> p (c s)"), p_m[:, 0:DC * S]).then_inc(xnT_ready, 1)

            def copy_qT(b, slot):
                act.wait_ge(qT_made, b + 1)
                act.activation(qT[:, slot].rearrange("p h s -> p (h s)"), p_m[:, 0:HP * S], ACT.Copy,
                               scale=DK ** -0.5).then_inc(qT_ready, 1)

            def copy_k(b, slot, c):
                act.wait_ge(k_made, DC * b + c + 1)
                act.activation(kT[:, slot, c, :], p_m[:, 0:SC], ACT.Identity, bias=b_k[:, c:c + 1]).then_inc(k_ready, 1)

            def copy_v(b, slot, n):
                act.wait_ge(v_made, NK * b + n + 1)
                act.copy(v_aug[0:KEYS[n], slot, n, :, 0:DK],
                         p_m[0:KEYS[n], 0:D].rearrange("k (h d) -> k h d", h=H)).then_inc(v_ready, 1)

            def exponentiate(b, slot, u):
                act.wait_ge(sT_made, UNITS * b + u + 1)
                if u >= ER:
                    act.wait_ge(pv_unit, UNITS * b + u + 1 - ER)
                elif later(b):
                    act.wait_ge(pv_unit, UNITS * b + u + 1 - ER)
                nk = KEYS[u % NK]
                act.activation(eT[0:nk, u % ER].rearrange("k h q -> k (h q)"), p_e[u % 2][0:nk, 0:HP * S],
                               ACT.Exp).then_inc(e_ready, 1)

            def copy_oT(b, slot):
                act.wait_ge(oT_made, b + 1)
                act.copy(oT[:].rearrange("p c s -> p (c s)"), p_m[:, 0:DC * S]).then_inc(oT_ready, 1)

            part = lambda f, *a: (lambda b, slot: f(b, slot, *a))
            ex = lambda u: (part(exponentiate, u), 1)
            Stages(act, [
                (copy_xnT, 0), (copy_qT, 0), (part(copy_k, 0), 0),
                ex(0), ex(1), (part(copy_k, 1), 0), ex(2), ex(3), (part(copy_v, 0), 0),
                ex(4), ex(5), (part(copy_v, 1), 0), ex(6), ex(7), (part(copy_v, 2), 0),
                ex(8), ex(9), ex(10), ex(11), (copy_oT, 1),
            ], B)


def route(nc, x_all, mv, rstd, ident, p, xnT_hi, xnT_lo, inv_sum, scratch):
    with ExitStack() as ctx:
        sb = lambda n, shape, dt=F32: ctx.enter_context(nc.sbuf_tensor(f"rt_{n}", shape, dt))
        pb = lambda n, shape, dt=F32: ctx.enter_context(nc.psum_tensor(f"rt_{n}", shape, dt))
        sem = lambda n: ctx.enter_context(nc.semaphore(f"rt_{n}"))

        gamma = sb("gamma", [S, D])
        slot_gamma = sb("slot_gamma", [P, D])
        slots = sb("slots", [P, E, D])
        squares = sb("squares", [P, D])
        norm = sb("norm", [P, E])
        sn = sb("sn", [P, E, D])
        snT_hi = sb("snT_hi", [P, DC, E * P], F32R)
        snT_lo = sb("snT_lo", [P, DC, E * P], F32R)
        scale = sb("scale", [S, B])
        scaled = sb("scaled", [S, D])
        xn = sb("xn", [S, 2, D])
        cur_hi = sb("cur_hi", [P, DC, S], F32R)
        cur_lo = sb("cur_lo", [P, DC, S], F32R)
        nmax = sb("nmax", [S, B])
        nmaxT = sb("nmaxT", [B, S])
        weights = sb("weights", [S, E * P])
        total = sb("total", [S, B])

        p_t = pb("p_t", [P, 512])
        p_sn = [pb(f"p_sn{i}", [P, 512]) for i in range(2)]
        p_l = pb("p_l", [P, 2, 512])

        loaded = sem("loaded")
        squared = sem("squared")
        steps = sem("steps")
        rooted = sem("rooted")
        sn_ready = sem("sn_ready")
        snT_made = sem("snT_made")
        snT_rounded = sem("snT_rounded")
        snT_left = sem("snT_left")
        sn_kept = sem("sn_kept")
        scaled_ready = sem("scaled_ready")
        xn_ready = sem("xn_ready")
        xn_kept = [sem("xn_kept0"), sem("xn_kept1")]
        xnT_made = sem("xnT_made")
        xnT_rounded = sem("xnT_rounded")
        xnT_left = sem("xnT_left")
        xnT_kept = sem("xnT_kept")
        logits_made = sem("logits_made")
        max_ready = sem("max_ready")
        exp_done = sem("exp_done")
        inv_ready = sem("inv_ready")
        maxT_made = sem("maxT_made")
        maxT_ready = sem("maxT_ready")
        max_kept = sem("max_kept")
        block = ctx.enter_context(nc.Block())

        @block.sync
        def _(sp):
            sp.dma_start(slots[:], p["slots"]).then_inc(loaded, 16)
            sp.dma_start(gamma[:], p["gamma"].partition_broadcast(S)).then_inc(loaded, 16)
            sp.dma_start(slot_gamma[:], p["slot_gamma"].partition_broadcast(P)).then_inc(loaded, 16)

            sp.wait_ge(snT_rounded, DC * E)
            sp.dma_start(scratch["snT_hi"].bitcast(F32), snT_hi[:].bitcast(F32)).then_inc(sn_kept, 16)
            sp.wait_ge(snT_left, DC * E)
            sp.dma_start(scratch["snT_lo"].bitcast(F32), snT_lo[:].bitcast(F32)).then_inc(sn_kept, 16)

            def keep_xn(b, slot):
                sp.wait_ge(xn_ready, b + 1)
                sp.dma_start(scratch["xn"][b], xn[:, slot]).then_inc(xn_kept[slot], 16)

            Stages(sp, [(keep_xn, 0)], B)
            sp.wait_ge(maxT_ready, 1)
            sp.dma_start(scratch["nmax"], nmaxT[:]).then_inc(max_kept, 16)
            sp.wait_ge(max_kept, 16)
            sp.wait_ge(sn_kept, 32)
            sp.wait_ge(xn_kept[0], 16 * (B // 2))
            sp.wait_ge(xn_kept[1], 16 * (B // 2))

        @block.tensor
        def _(pe):
            pe.wait_ge(sn_ready, E)
            for e in range(E):
                for c in range(DC):
                    n = DC * e + c
                    if n >= 2:
                        pe.wait_ge(snT_left, n - 1)
                    pe.transpose(p_sn[n % 2][:, 0:P], sn[:, e, c * P:(c + 1) * P], ident[:]).then_inc(snT_made, 1)
            pe.wait_ge(snT_left, DC * E)

            def transpose_xn(b, slot):
                pe.wait_ge(xn_ready, b + 1)
                if later(b):
                    pe.wait_ge(xnT_left, b)
                for c in range(DC):
                    mm = pe.transpose(p_t[:, c * S:(c + 1) * S], xn[:, slot, c * P:(c + 1) * P], ident[0:S, 0:S])
                mm.then_inc(xnT_made, 1)

            def logits(b, slot):
                pe.wait_ge(xnT_rounded, b + 1)
                pe.wait_ge(xnT_left, b + 1)
                if later(b):
                    pe.wait_ge(exp_done, b)
                for half in range(2):
                    cols = slice(half * 512, half * 512 + 512)
                    n = 0
                    for c in range(DC):
                        for a, w in ((cur_hi, snT_hi), (cur_lo, snT_hi), (cur_hi, snT_lo)):
                            mm = pe.matmul(p_l[0:S, half, :], a[:, c, :], w[:, c, cols], start=n == 0, stop=n == 3 * DC - 1)
                            n += 1
                mm.then_inc(logits_made, 1)

            Stages(pe, [(transpose_xn, 0), (logits, 1)], B)
            pe.wait_ge(max_ready, B)
            pe.wait_ge(xnT_left, B)
            pe.transpose(p_t[0:B, 0:S], nmax[:], ident[0:S, 0:S]).then_inc(maxT_made, 1)

        @block.vector
        def _(dve):
            dve.wait_ge(squared, E)
            dve.wait_ge(rooted, 1)
            dve.tensor_scalar(norm[:], norm[:], 1e-12, None, ALU.max).then_inc(steps, 1)
            dve.wait_ge(steps, 1)
            dve.reciprocal(norm[:], norm[:]).then_inc(steps, 1)
            dve.wait_ge(steps, 2)
            dve.tensor_scalar(norm[:], norm[:], float(D) ** 0.5, None, ALU.mult).then_inc(steps, 1)
            dve.wait_ge(steps, 3)
            for e in range(E):
                dve.scalar_tensor_tensor(out=sn[:, e, :], in0=slots[:, e, :], scalar=norm[:, e:e + 1], in1=slot_gamma[:],
                                         op0=ALU.mult, op1=ALU.mult).then_inc(sn_ready, 1)
            for n in range(DC * E):
                dve.wait_ge(snT_rounded, n + 1)
                e, c = divmod(n, DC)
                cols = slice(e * P, (e + 1) * P)
                dve.tensor_tensor(snT_lo[:, c, cols], p_sn[n % 2][:, 0:P], snT_hi[:, c, cols].bitcast(F32),
                                  ALU.subtract).then_inc(snT_left, 1)

            dve.tensor_tensor(scale[:], mv[:, :, 1], rstd[:], ALU.mult).then_inc(steps, 1)
            dve.wait_ge(steps, 4)
            dve.tensor_tensor(scale[:], scale[:], rstd[:], ALU.mult).then_inc(steps, 1)
            dve.wait_ge(steps, 5)
            dve.tensor_scalar(scale[:], scale[:], float(D), None, ALU.mult).then_inc(steps, 1)
            dve.wait_ge(rooted, 2)
            dve.tensor_scalar(scale[:], scale[:], 1e-12, None, ALU.max).then_inc(steps, 1)
            dve.wait_ge(steps, 7)
            dve.reciprocal(scale[:], scale[:]).then_inc(steps, 1)
            dve.wait_ge(steps, 8)
            dve.tensor_tensor(scale[:], scale[:], rstd[:], ALU.mult).then_inc(steps, 1)
            dve.wait_ge(steps, 9)
            dve.tensor_scalar(scale[:], scale[:], float(D) ** 0.5, None, ALU.mult).then_inc(steps, 1)
            dve.wait_ge(steps, 10)

            def normalise(b, slot):
                if later(b):
                    dve.wait_ge(xn_ready, b)
                if later(b, 2):
                    dve.wait_ge(xn_kept[slot], 16 * (b // 2))
                    dve.wait_ge(xnT_made, b - 1)
                dve.tensor_scalar(scaled[:], x_all[:, b, :], mv[:, b, 0:1], scale[:, bass.ds(b, 1)],
                                  ALU.subtract, ALU.mult).then_inc(scaled_ready, 1)
                dve.wait_ge(scaled_ready, b + 1)
                dve.tensor_tensor(xn[:, slot], scaled[:], gamma[:], ALU.mult).then_inc(xn_ready, 1)

            def leave_xnT(b, slot):
                dve.wait_ge(xnT_rounded, b + 1)
                if later(b):
                    dve.wait_ge(xnT_kept, 2 * b)
                    dve.wait_ge(logits_made, b)
                dve.tensor_tensor(cur_lo[:].rearrange("p c s -> p (c s)"), p_t[:, 0:DC * S],
                                  cur_hi[:].rearrange("p c s -> p (c s)").bitcast(F32), ALU.subtract).then_inc(xnT_left, 1)

            def find_max(b, slot):
                dve.wait_ge(logits_made, b + 1)
                dve.tensor_reduce(nmax[:, bass.ds(b, 1)], p_l[0:S].rearrange("s a n -> s (a n)"), X, ALU.max,
                                  negate=True).then_inc(max_ready, 1)

            Stages(dve, [(normalise, -1), (leave_xnT, 0), (find_max, 1)], B)
            dve.wait_ge(maxT_made, 1)
            dve.tensor_copy(nmaxT[:], p_t[0:B, 0:S]).then_inc(maxT_ready, 1)
            dve.wait_ge(exp_done, B)
            dve.reciprocal(inv_sum[:], total[:]).then_inc(inv_ready, 1)
            dve.wait_ge(inv_ready, 1)

        @block.scalar
        def _(act):
            act.wait_ge(loaded, 48)
            for e in range(E):
                if e:
                    act.wait_ge(squared, e)
                act.activation(squares[:], slots[:, e, :], ACT.Square, accum_out=norm[:, e:e + 1]).then_inc(squared, 1)
            act.wait_ge(squared, E)
            act.activation(norm[:], norm[:], ACT.Sqrt).then_inc(rooted, 1)
            for n in range(DC * E):
                act.wait_ge(snT_made, n + 1)
                e, c = divmod(n, DC)
                act.copy(snT_hi[:, c, e * P:(e + 1) * P], p_sn[n % 2][:, 0:P]).then_inc(snT_rounded, 1)
            act.wait_ge(steps, 6)
            act.activation(scale[:], scale[:], ACT.Sqrt).then_inc(rooted, 1)

            def round_xnT(b, slot):
                act.wait_ge(xnT_made, b + 1)
                if later(b):
                    act.wait_ge(xnT_kept, 2 * b)
                    act.wait_ge(logits_made, b)
                act.copy(cur_hi[:].rearrange("p c s -> p (c s)"), p_t[:, 0:DC * S]).then_inc(xnT_rounded, 1)

            def exponentiate(b, slot):
                act.wait_ge(max_ready, b + 1)
                if later(b):
                    act.wait_ge(exp_done, b)
                act.activation(weights[:], p_l[0:S].rearrange("s a n -> s (a n)"), ACT.Exp,
                               bias=nmax[:, bass.ds(b, 1)], accum_out=total[:, bass.ds(b, 1)]).then_inc(exp_done, 1)

            Stages(act, [(round_xnT, 0), (exponentiate, 1)], B)

        @block.gpsimd
        def _(pool):
            def keep_xnT(b, slot):
                pool.wait_ge(xnT_rounded, b + 1)
                pool.tensor_copy(xnT_hi[:, :, bass.ds(b * S, S)], cur_hi[:]).then_inc(xnT_kept, 1)
                pool.wait_ge(xnT_left, b + 1)
                pool.tensor_copy(xnT_lo[:, :, bass.ds(b * S, S)], cur_lo[:]).then_inc(xnT_kept, 1)

            Stages(pool, [(keep_xnT, 0)], B)
            pool.wait_ge(xnT_kept, 2 * B)


def experts(nc, x_all, ident, p, xnT_hi, xnT_lo, inv_sum, scratch):
    with ExitStack() as ctx:
        sb = lambda n, shape, dt=F32: ctx.enter_context(nc.sbuf_tensor(f"ex_{n}", shape, dt))
        pb = lambda n, shape, dt=F32: ctx.enter_context(nc.psum_tensor(f"ex_{n}", shape, dt))
        sem = lambda n: ctx.enter_context(nc.semaphore(f"ex_{n}"))
        N = GB * S
        R = GB * P

        w1_raw = sb("w1_raw", [P, DC, HID])
        w2_raw = sb("w2_raw", [P, HC, D])
        w1_hi = sb("w1_hi", [P, DC, HID], F32R)
        w1_lo = sb("w1_lo", [P, DC, HID], F32R)
        w2_hi = sb("w2_hi", [P, HC, D], F32R)
        w2_lo = sb("w2_lo", [P, HC, D], F32R)
        b1 = sb("b1", [P, E, HC])
        b2 = sb("b2", [P, E, D])
        snT_hi = sb("snT_hi", [P, DC, P], F32R)
        snT_lo = sb("snT_lo", [P, DC, P], F32R)
        nmax = sb("nmax", [P, N])
        xn = sb("xn", [S, GB, D])
        over = sb("over", [P, GB])
        dispatch = sb("dispatch", [P, GB, S])
        dsum = sb("dsum", [P, GB])
        dispatchT = sb("dispatchT", [S, GB, P])
        lag_c = sb("lag_c", [P, N])
        combine = sb("combine", [P, GB, S])
        slots_hi = sb("slots_hi", [P, DC, R], F32R)
        slots_lo = sb("slots_lo", [P, DC, R], F32R)
        h = sb("h", [P, 2, R])
        h_hi = sb("h_hi", [P, HC, R], F32R)
        h_lo = sb("h_lo", [P, HC, R], F32R)
        eo = sb("eo", [P, GB, D])

        p_h = [pb(f"p_h{i}", [P, 512]) for i in range(3)]
        p_e = [pb(f"p_e{i}", [P, 512]) for i in range(2)]
        p_c = pb("p_c", [P, 512])
        p_l = pb("p_l", [P, 512])
        p_x = pb("p_x", [P, 512])

        loaded = sem("loaded")
        w1_in = sem("w1_in")
        w2_in = sem("w2_in")
        sn_in = sem("sn_in")
        nmax_in = sem("nmax_in")
        xn_in = sem("xn_in")
        w1_split = sem("w1_split")
        w1_lost = sem("w1_lost")
        w2_split = sem("w2_split")
        w2_lost = sem("w2_lost")
        l_made = sem("l_made")
        over_ready = sem("over_ready")
        d_shifted = sem("d_shifted")
        c_shifted = sem("c_shifted")
        d_exp = sem("d_exp")
        dsum_ready = sem("dsum_ready")
        d_ready = sem("d_ready")
        dT_made = sem("dT_made")
        dT_ready = sem("dT_ready")
        c_ready = sem("c_ready")
        slots_made = sem("slots_made")
        slots_rounded = sem("slots_rounded")
        slots_left = sem("slots_left")
        h_made = sem("h_made")
        h_ready = sem("h_ready")
        h_rounded = sem("h_rounded")
        h_left = sem("h_left")
        e_made = sem("e_made")
        e_ready = sem("e_ready")
        c_made = sem("c_made")
        x_added = sem("x_added")

        block = ctx.enter_context(nc.Block())

        def over_units(engine, unit):
            unit(0, 0, 0, 1)
            with engine.Fori(1, G - 1) as g:
                unit(0, g, 0, g + 1)
            unit(0, G - 1, 1, 0)
            with engine.Fori(1, E - 1) as e:
                with engine.Fori(0, G - 1) as g:
                    unit(e, g, e, g + 1)
                unit(e, G - 1, e + 1, 0)
            with engine.Fori(0, G - 1) as g:
                unit(E - 1, g, E - 1, g + 1)
            unit(E - 1, G - 1, None, None)

        @block.sync
        def _(sp):
            sp.dma_start(b1[:], p["b1"]).then_inc(loaded, 16)
            sp.dma_start(b2[:].rearrange("p e d -> p (e d)"), p["b2"].partition_broadcast(P)).then_inc(loaded, 16)

            def load_expert(e):
                if later(e):
                    sp.wait_ge(l_made, G * e)
                sp.dma_start(snT_hi[:].bitcast(F32), scratch["snT_hi"][:, :, bass.ds(e * P, P)].bitcast(F32)).then_inc(sn_in, 16)
                sp.dma_start(snT_lo[:].bitcast(F32), scratch["snT_lo"][:, :, bass.ds(e * P, P)].bitcast(F32)).then_inc(sn_in, 16)

            def load_weights(e):
                if later(e):
                    sp.wait_ge(w1_split, e)
                    sp.wait_ge(w1_lost, e)
                sp.dma_start(w1_raw[:], p["w1"][e]).then_inc(w1_in, 16)
                if later(e):
                    sp.wait_ge(w2_split, e)
                    sp.wait_ge(w2_lost, e)
                sp.dma_start(w2_raw[:], p["w2"][e]).then_inc(w2_in, 16)

            def load_tokens(e, g):
                u = e * G + g
                if later(u):
                    sp.wait_ge(c_shifted, u)
                sp.dma_start(nmax[:].rearrange("p (b s) -> p b s", b=GB),
                             scratch["nmax"][bass.ds(g * GB, GB), :].partition_broadcast(P)).then_inc(nmax_in, 16)
                if later(u):
                    sp.wait_ge(slots_made, DC * u)
                sp.dma_start(xn[:], scratch["xn_units"][:, bass.ds(g * GB, GB), :]).then_inc(xn_in, 16)

            load_expert(0)
            load_tokens(0, 0)
            load_weights(0)

            def unit(e, g, e2, g2):
                if isinstance(g, int) and g == 0:
                    load_weights(e + 1)
                if isinstance(g2, int) and g2 == 0:
                    load_expert(e2)
                load_tokens(e2, g2)

            unit(0, 0, 0, 1)
            with sp.Fori(1, G - 1) as g:
                unit(0, g, 0, g + 1)
            unit(0, G - 1, 1, 0)
            with sp.Fori(1, E - 1) as e:
                load_weights(e + 1)
                with sp.Fori(0, G - 1) as g:
                    unit(e, g, e, g + 1)
                unit(e, G - 1, e + 1, 0)
            with sp.Fori(0, G - 1) as g:
                unit(E - 1, g, E - 1, g + 1)
            sp.wait_ge(loaded, 32)

        @block.tensor
        def _(pe):
            def logits(e, g):
                u = e * G + g
                pe.wait_ge(sn_in, 32 * (e + 1))
                if later(u):
                    pe.wait_ge(slots_left, DC * u)
                    pe.wait_ge(slots_rounded, DC * u)
                n = 0
                for c in range(DC):
                    for a, t in ((snT_hi, xnT_hi), (snT_lo, xnT_hi), (snT_hi, xnT_lo)):
                        mm = pe.matmul(p_l[:, 0:N], a[:, c, :], t[:, c, bass.ds(g * N, N)], start=n == 0, stop=n == 3 * DC - 1)
                        n += 1
                mm.then_inc(l_made, 1)

            def transpose_dispatch(e, g):
                u = e * G + g
                pe.wait_ge(d_ready, u + 1)
                pe.wait_ge(c_shifted, u + 1)
                for b in range(GB):
                    mm = pe.transpose(p_l[0:S, b * P:(b + 1) * P], dispatch[:, b, :], ident[:])
                mm.then_inc(dT_made, 1)

            def fill_slots(e, g, c):
                u = e * G + g
                if c == 0:
                    pe.wait_ge(dT_ready, u + 1)
                    pe.wait_ge(xn_in, 16 * (u + 1))
                    if later(u):
                        pe.wait_ge(slots_left, DC * (u - 1) + 1)
                to = p_x if c == 0 else p_l
                for b in range(GB):
                    mm = pe.matmul(to[:, b * P:(b + 1) * P], xn[:, b, c * P:(c + 1) * P], dispatchT[:, b, :],
                                   start=True, stop=True)
                mm.then_inc(slots_made, 1)

            def layer_1(e, g, m):
                u = e * G + g
                if m == 0:
                    pe.wait_ge(slots_left, DC * (u + 1))
                    pe.wait_ge(slots_rounded, DC * (u + 1))
                    pe.wait_ge(w1_split, e + 1)
                    pe.wait_ge(w1_lost, e + 1)
                if m >= 3:
                    pe.wait_ge(h_ready, HC * u + m - 2)
                elif later(u):
                    pe.wait_ge(h_ready, HC * (u - 1) + M3[m])
                cols = slice(m * P, (m + 1) * P)
                n = 0
                for c in range(DC):
                    for w, a in ((w1_hi, slots_hi), (w1_lo, slots_hi), (w1_hi, slots_lo)):
                        mm = pe.matmul(p_h[m % 3][:, 0:R], w[:, c, cols], a[:, c, :], start=n == 0, stop=n == 3 * DC - 1)
                        n += 1
                mm.then_inc(h_made, 1)

            def layer_2(e, g, b):
                u = e * G + g
                if b == 0:
                    pe.wait_ge(w2_split, e + 1)
                    pe.wait_ge(w2_lost, e + 1)
                if b >= 2:
                    pe.wait_ge(e_ready, GB * u + b - 1)
                elif later(u):
                    pe.wait_ge(e_ready, GB * u + b - 1)
                rows = slice(b * P, (b + 1) * P)
                for m in range(HC):
                    if b == 0:
                        pe.wait_ge(h_left, HC * u + m + 1)
                    for n, (a, w) in enumerate(((h_hi, w2_hi), (h_lo, w2_hi), (h_hi, w2_lo))):
                        mm = pe.matmul(p_e[b % 2][:, 0:D], a[:, m, rows], w[:, m, :], start=m == 0 and n == 0,
                                       stop=m == HC - 1 and n == 2)
                mm.then_inc(e_made, 1)

            def combine_batch(e, g, b):
                u = e * G + g
                pe.wait_ge(e_ready, GB * u + b + 1)
                if b == 0:
                    pe.wait_ge(c_ready, u + 1)
                if b > 0 or later(u):
                    pe.wait_ge(x_added, GB * u + b)
                pe.matmul(p_c[0:S, 0:D], combine[:, b, :], eo[:, b, :], start=True, stop=True).then_inc(c_made, 1)

            def unit(e, g, e2, g2):
                more = e2 is not None
                if more:
                    logits(e2, g2)
                for m in range(HC):
                    layer_1(e, g, m)
                if more:
                    transpose_dispatch(e2, g2)
                layer_2(e, g, 0)
                if more:
                    fill_slots(e2, g2, 0)
                layer_2(e, g, 1)
                combine_batch(e, g, 0)
                if more:
                    fill_slots(e2, g2, 1)
                layer_2(e, g, 2)
                combine_batch(e, g, 1)
                layer_2(e, g, 3)
                combine_batch(e, g, 2)
                combine_batch(e, g, 3)

            def first():
                logits(0, 0)
                transpose_dispatch(0, 0)
                fill_slots(0, 0, 0)
                fill_slots(0, 0, 1)

            first()
            over_units(pe, unit)

        @block.vector
        def _(dve):
            dve.wait_ge(loaded, 32)

            def shift(e, g):
                u = e * G + g
                dve.wait_ge(l_made, u + 1)
                rows = p_l[:, 0:N].rearrange("p (b s) -> p b s", b=GB)
                dve.tensor_reduce(over[:], rows, X, ALU.max).then_inc(over_ready, 1)
                dve.wait_ge(over_ready, u + 1)
                if later(u):
                    dve.wait_ge(dT_made, u)
                dve.tensor_tensor(dispatch[:], rows, over[:].unsqueeze(2).broadcast_to([P, GB, S]),
                                  ALU.subtract).then_inc(d_shifted, 1)
                dve.wait_ge(nmax_in, 16 * (u + 1))
                if later(u):
                    dve.wait_ge(c_ready, u)
                dve.tensor_tensor(lag_c[:], p_l[:, 0:N], nmax[:], ALU.add).then_inc(c_shifted, 1)

            def sum_dispatch(e, g):
                u = e * G + g
                dve.wait_ge(d_exp, u + 1)
                dve.tensor_reduce(dsum[:], dispatch[:], X, ALU.add).then_inc(dsum_ready, 1)
                dve.wait_ge(dsum_ready, 2 * u + 1)
                dve.reciprocal(dsum[:], dsum[:]).then_inc(dsum_ready, 1)
                dve.wait_ge(dsum_ready, 2 * u + 2)
                dve.tensor_tensor(dispatch[:], dispatch[:], dsum[:].unsqueeze(2).broadcast_to([P, GB, S]),
                                  ALU.mult).then_inc(d_ready, 1)

            def leave_slots(e, g, c):
                u = e * G + g
                dve.wait_ge(slots_rounded, DC * u + c + 1)
                frm = p_x if c == 0 else p_l
                dve.tensor_tensor(slots_lo[:, c, :], frm[:, 0:R], slots_hi[:, c, :].bitcast(F32),
                                  ALU.subtract).then_inc(slots_left, 1)

            def leave_h(e, g, m):
                u = e * G + g
                dve.wait_ge(h_rounded, HC * u + m + 1)
                dve.tensor_tensor(h_lo[:, m, :], h[:, m % 2, :], h_hi[:, m, :].bitcast(F32), ALU.subtract).then_inc(h_left, 1)

            def leave_w(e, raw, hi, lo, split, lost):
                dve.wait_ge(split, e + 1)
                dve.tensor_tensor(lo[:].rearrange("p a b -> p (a b)"), raw[:].rearrange("p a b -> p (a b)"),
                                  hi[:].rearrange("p a b -> p (a b)").bitcast(F32), ALU.subtract).then_inc(lost, 1)

            def add_bias(e, g, b):
                u = e * G + g
                dve.wait_ge(e_made, GB * u + b + 1)
                if later(u):
                    dve.wait_ge(c_made, GB * (u - 1) + b + 1)
                dve.tensor_tensor(eo[:, b, :], p_e[b % 2][:, 0:D], b2[:, bass.ds(e, 1), :].squeeze(1) if not isinstance(e, int) else b2[:, e, :],
                                  ALU.add).then_inc(e_ready, 1)

            def add_to_x(e, g, b):
                u = e * G + g
                dve.wait_ge(c_made, GB * u + b + 1)
                at = g * GB + b
                dve.scalar_tensor_tensor(out=x_all[:, at, :], in0=p_c[0:S, 0:D], scalar=inv_sum[:, bass.ds(at, 1)],
                                         in1=x_all[:, at, :], op0=ALU.mult, op1=ALU.add).then_inc(x_added, 1)

            def unit(e, g, e2, g2):
                more = e2 is not None
                if more:
                    shift(e2, g2)
                for m in range(HC):
                    leave_h(e, g, m)
                    if m == 2 and more:
                        sum_dispatch(e2, g2)
                if isinstance(g2, int) and g2 == 0:
                    leave_w(e2, w1_raw, w1_hi, w1_lo, w1_split, w1_lost)
                add_bias(e, g, 0)
                if more:
                    leave_slots(e2, g2, 0)
                add_bias(e, g, 1)
                add_to_x(e, g, 0)
                if more:
                    leave_slots(e2, g2, 1)
                add_bias(e, g, 2)
                add_to_x(e, g, 1)
                add_bias(e, g, 3)
                add_to_x(e, g, 2)
                add_to_x(e, g, 3)
                if isinstance(g2, int) and g2 == 0:
                    leave_w(e2, w2_raw, w2_hi, w2_lo, w2_split, w2_lost)

            def first():
                shift(0, 0)
                sum_dispatch(0, 0)
                leave_w(0, w1_raw, w1_hi, w1_lo, w1_split, w1_lost)
                leave_w(0, w2_raw, w2_hi, w2_lo, w2_split, w2_lost)
                leave_slots(0, 0, 0)
                leave_slots(0, 0, 1)

            first()
            over_units(dve, unit)

        @block.scalar
        def _(act):
            act.wait_ge(loaded, 32)

            def exp_dispatch(e, g):
                u = e * G + g
                act.wait_ge(d_shifted, u + 1)
                act.activation(dispatch[:], dispatch[:], ACT.Exp).then_inc(d_exp, 1)

            def copy_dispatch(e, g):
                u = e * G + g
                act.wait_ge(dT_made, u + 1)
                if later(u):
                    act.wait_ge(slots_made, DC * u)
                act.copy(dispatchT[:].rearrange("s b p -> s (b p)"), p_l[0:S, 0:R]).then_inc(dT_ready, 1)

            def exp_combine(e, g):
                u = e * G + g
                act.wait_ge(c_shifted, u + 1)
                if later(u):
                    act.wait_ge(c_made, GB * u)
                act.activation(combine[:].rearrange("p b s -> p (b s)"), lag_c[:], ACT.Exp).then_inc(c_ready, 1)

            def round_slots(e, g, c):
                u = e * G + g
                act.wait_ge(slots_made, DC * u + c + 1)
                if c == 0 and later(u):
                    act.wait_ge(h_made, HC * u)
                act.copy(slots_hi[:, c, :], (p_x if c == 0 else p_l)[:, 0:R]).then_inc(slots_rounded, 1)

            def gelu(e, g, m):
                u = e * G + g
                act.wait_ge(h_made, HC * u + m + 1)
                if m >= 2 or later(u):
                    act.wait_ge(h_left, HC * u + m - 1)
                act.activation(h[:, m % 2, :], p_h[m % 3][:, 0:R], ACT.Gelu, bias=b1[:, e, m:m + 1]).then_inc(h_ready, 1)
                act.wait_ge(h_ready, HC * u + m + 1)
                if m == 0 and later(u):
                    act.wait_ge(e_made, GB * u)
                act.copy(h_hi[:, m, :], h[:, m % 2, :]).then_inc(h_rounded, 1)

            def split_w(e, raw, hi, arrived, split):
                act.wait_ge(arrived, 16 * (e + 1))
                act.copy(hi[:].rearrange("p a b -> p (a b)"), raw[:].rearrange("p a b -> p (a b)")).then_inc(split, 1)

            def unit(e, g, e2, g2):
                more = e2 is not None
                exp_combine(e, g)
                if more:
                    exp_dispatch(e2, g2)
                for m in range(HC):
                    gelu(e, g, m)
                if more:
                    copy_dispatch(e2, g2)
                    if isinstance(g2, int) and g2 == 0:
                        split_w(e2, w1_raw, w1_hi, w1_in, w1_split)
                    round_slots(e2, g2, 0)
                    round_slots(e2, g2, 1)
                    if isinstance(g2, int) and g2 == 0:
                        act.wait_ge(e_made, GB * (e * G + g) + GB)
                        split_w(e2, w2_raw, w2_hi, w2_in, w2_split)

            def first():
                exp_dispatch(0, 0)
                copy_dispatch(0, 0)
                split_w(0, w1_raw, w1_hi, w1_in, w1_split)
                split_w(0, w2_raw, w2_hi, w2_in, w2_split)
                round_slots(0, 0, 0)
                round_slots(0, 0, 1)

            first()
            over_units(act, unit)


def decoder_layer(nc, x, wqkv, wo, cos, sin, causal, ident_f32, ident_bf16, ctx_t, shift_mask, xw_q, xw_k, xw_v, xw_o,
                  xb_q, xb_k, xb_v, xb_o, gamma, slot_gamma, slots, w1, w2, b1, b2, out):
    with ExitStack() as ctx:
        sb = lambda n, shape, dt=F32: ctx.enter_context(nc.sbuf_tensor(n, shape, dt))
        dram = lambda n, shape, dt=F32: nc.dram_tensor(n, shape, dt, kind="Internal").ap()
        x_all = sb("x_all", [S, B, D])
        mv = sb("mv", [S, B, 2])
        rstd = sb("rstd", [S, B])
        stats = sb("stats", [S, B, 6])
        ident = sb("ident", [P, P])
        ident16 = sb("ident16", [P, P], BF16)
        x_in = ctx.enter_context(nc.semaphore("x_in"))
        x_out = ctx.enter_context(nc.semaphore("x_out"))

        with nc.Block() as block:
            @block.sync
            def _(sp):
                sp.dma_start(x_all[:], x.rearrange("b s d -> s b d")).then_inc(x_in, 16)
                sp.dma_start(ident[:], ident_f32).then_inc(x_in, 16)
                sp.dma_start(ident16[:], ident_bf16).then_inc(x_in, 16)
                sp.wait_ge(x_in, 48)

        norm_statistics(nc, x_all, mv, rstd, stats, "ln1", True)
        self_attention(nc, x_all, mv, rstd, stats, ident, wqkv, wo, cos, sin, causal)
        norm_statistics(nc, x_all, mv, rstd, stats, "ln2", False)
        cross_attention(nc, x_all, mv, rstd, stats, ident, ident16, ctx_t,
                        dict(w_q=xw_q, w_k=xw_k, w_v=xw_v, w_o=xw_o, b_q=xb_q, b_k=xb_k, b_v=xb_v, b_o=xb_o), shift_mask)
        norm_statistics(nc, x_all, mv, rstd, stats, "ln3", False)

        ffn = dict(gamma=gamma, slot_gamma=slot_gamma, slots=slots, w1=w1, w2=w2, b1=b1, b2=b2)
        xn = dram("xn_tokens", (B, S, D))
        scratch = dict(snT_hi=dram("sn_t_hi", (P, DC, E * P), F32R), snT_lo=dram("sn_t_lo", (P, DC, E * P), F32R),
                       xn=xn, xn_units=xn.rearrange("b s d -> s b d"), nmax=dram("token_nmax", (B, S)))
        xnT_hi = sb("xnT_hi", [P, DC, B * S], F32R)
        xnT_lo = sb("xnT_lo", [P, DC, B * S], F32R)
        inv_sum = sb("inv_sum", [S, B])
        route(nc, x_all, mv, rstd, ident, ffn, xnT_hi, xnT_lo, inv_sum, scratch)
        experts(nc, x_all, ident, ffn, xnT_hi, xnT_lo, inv_sum, scratch)

        with nc.Block() as block:
            @block.sync
            def _(sp):
                sp.dma_start(out.rearrange("b s d -> s b d"), x_all[:]).then_inc(x_out, 16)
                sp.wait_ge(x_out, 16)


def constants():
    inv_freq = (np.float32(10000.0) ** (-np.arange(DK // 2, dtype=np.float32) * np.float32(2.0) / DK)).astype(np.float32)
    angle = np.arange(S, dtype=np.float32)[:, None] * inv_freq[None, :]
    cos, sin = np.cos(angle).astype(np.float32), np.sin(angle).astype(np.float32)
    shift_mask = np.zeros((ROWS, 2 * DK, HP, S), np.float32)
    for hp in range(HP):
        shift_mask[:, [hp, HP + hp], hp] = 1.0
    return dict(
        cos=np.tile(np.repeat(cos, 2, axis=1), (1, 2 * H)),
        sin=np.tile(np.stack([-sin, sin], axis=-1).reshape(S, DK), (1, 2 * H)),
        causal=np.where(np.tril(np.ones((S, S), bool)), 0.0, -3e38).astype(np.float32),
        ident_f32=np.eye(P, dtype=np.float32),
        ident_bf16=np.eye(P).astype(mybir.dt.np(BF16)),
        shift_mask=shift_mask.reshape(P, HP, S))


def kernel(**inputs):
    import concourse.bacc as _bacc
    from concourse.bass_utils import run_bass_kernel_spmd as _run

    given = {name: np.asarray(a) for name, a in inputs.items()}
    attn = lambda n: given["L0_attn_" + n]
    xattn = lambda n: given["L0_xattn_" + n]
    ffn = lambda n: given["L0_ffn_" + n]
    rows = lambda w: w.reshape(DC, P, -1).transpose(1, 0, 2)

    arrays = dict(
        x=given["x"],
        wqkv=rows(np.concatenate([attn("Wq").T, attn("Wk").T, attn("Wv").T], axis=1)),
        wo=rows(attn("Wo").T),
        ctx_t=given["ctx_1024"].transpose(0, 2, 1).reshape(B, DC, P, SC).transpose(0, 2, 1, 3),
        xw_q=rows(xattn("Wq")), xw_k=rows(xattn("Wk")), xw_v=rows(xattn("Wv")), xw_o=rows(xattn("Wo")),
        xb_q=xattn("bq"), xb_k=xattn("bk").reshape(DC, P).T, xb_v=xattn("bv"), xb_o=xattn("bo"),
        gamma=ffn("norm_gamma"), slot_gamma=ffn("slot_norm_gamma"), slots=ffn("slot_embeds").transpose(1, 0, 2),
        w1=ffn("w1").reshape(E, DC, P, HID).transpose(0, 2, 1, 3),
        w2=ffn("w2").reshape(E, HC, P, D).transpose(0, 2, 1, 3),
        b1=ffn("b1").reshape(E, HC, P).transpose(2, 0, 1), b2=ffn("b2").reshape(-1),
        **constants())

    nc = _bacc.Bacc("TRN2", target_bir_lowering=False, num_devices=1)
    feeds, args = {}, {}
    for name, a in arrays.items():
        feeds[f"in_{name}_dram"] = a = np.ascontiguousarray(a)
        args[name] = nc.dram_tensor(f"in_{name}_dram", a.shape, mybir.dt.from_np(a.dtype), kind="ExternalInput").ap()
    out = nc.dram_tensor("out_0_dram", (B, S, D), F32, kind="ExternalOutput").ap()
    decoder_layer(nc, out=out, **args)
    return _run(nc, [feeds], core_ids=[0]).results[0]["out_0_dram"]
```

```python
from contextlib import ExitStack

import numpy as np

import concourse.bass as bass
from concourse import mybir

ALU = mybir.AluOpType
ACT = mybir.ActivationFunctionType
F32 = mybir.dt.float32
F32R = mybir.dt.float32r
BF16 = mybir.dt.bfloat16
X = mybir.AxisListType.X
ALL_MAX = bass.bass_isa.ReduceOp.max

B, S, D = 32, 100, 256
SC = 361
SCP = 362
H, DK = 16, 16
P = 128
DC = D // P
ROWS = 4
HP = H // ROWS
KEYS = [121, 120, 120]
KEY0 = [0, 121, 241]
ER = 3
VA = DK + 1
E, HID = 8, 1024
HC = HID // P
GB = 4
G = B // GB
M3 = [7, 8, 6]
EPS = 1e-5


def head_of(row, hp):
    return 8 * (hp // 2) + 2 * row + hp % 2


class Stages:

    def __init__(self, engine, stages, count):
        lags = [lag for _, lag in stages]
        least, deepest = min(lags), max(lags)
        begin = deepest + 1 + (deepest + 1) % 2
        end = count + least - (count + least) % 2

        def step(i, turn):
            for stage, lag in stages:
                b = i - lag
                if not isinstance(b, int) or 0 <= b < count:
                    stage(b, (turn - lag) % 2)

        for i in range(least, begin):
            step(i, i)
        with engine.Fori(begin // 2, end // 2) as pair:
            step(2 * pair, 0)
            step(2 * pair + 1, 1)
        for i in range(end, count + deepest):
            step(i, i)


def later(b, n=1):
    return not isinstance(b, int) or b >= n


def norm_statistics(nc, x_all, mv, rstd, stats, name, first):
    with ExitStack() as ctx:
        sem = lambda n: ctx.enter_context(nc.semaphore(f"{name}_{n}"))
        stats_done, aggr_done, eps_added, root_done, rstd_done = (
            sem(n) for n in ("stats_done", "aggr_done", "eps_added", "root_done", "rstd_done"))
        block = ctx.enter_context(nc.Block())

        @block.vector
        def _(dve):
            if first:
                with dve.Fori(0, B) as b:
                    dve.bn_stats(stats[:, b, :], x_all[:, b, :]).then_inc(stats_done, 1)
                dve.wait_ge(stats_done, B)
            for b in range(B):
                dve.bn_aggr(mv[:, b, :], stats[:, b, :]).then_inc(aggr_done, 1)
            dve.wait_ge(aggr_done, B)
            dve.tensor_scalar(rstd[:], mv[:, :, 1], EPS, None, ALU.add).then_inc(eps_added, 1)
            dve.wait_ge(root_done, 1)
            dve.reciprocal(rstd[:], rstd[:]).then_inc(rstd_done, 1)
            dve.wait_ge(rstd_done, 1)

        @block.scalar
        def _(act):
            act.wait_ge(eps_added, 1)
            act.activation(rstd[:], rstd[:], ACT.Sqrt).then_inc(root_done, 1)


def self_attention(nc, x_all, mv, rstd, stats, ident, wqkv_dram, wo_dram, cos_dram, sin_dram, mask_dram):
    with ExitStack() as ctx:
        sb = lambda n, shape, dt=F32: ctx.enter_context(nc.sbuf_tensor(f"sa_{n}", shape, dt))
        pb = lambda n, shape: ctx.enter_context(nc.psum_tensor(f"sa_{n}", shape, F32))
        sem = lambda n: ctx.enter_context(nc.semaphore(f"sa_{n}"))

        w_qkv = sb("w_qkv", [P, DC, 3 * D])
        w_o = sb("w_o", [P, DC, D])
        cos_t = sb("cos_t", [S, 2 * D])
        sin_t = sb("sin_t", [S, 2 * D])
        mask = sb("mask", [S, S])
        xn = sb("xn", [S, D])
        xnT = sb("xnT", [P, DC, S])
        t_cos = sb("t_cos", [S, 2 * D])
        t_sin = sb("t_sin", [S, 2 * D])
        q_split = sb("q_split", [S, HP, ROWS, 2 * DK])
        k_rot = sb("k_rot", [S, D])
        qT = sb("qT", [P, HP, S])
        kT = sb("kT", [P, DC, S])
        v_aug = sb("v_aug", [S, 3, H, VA])
        e = sb("e", [S, ROWS, HP, S])
        mx = sb("mx", [S, H])
        eT = sb("eT", [S, ROWS, HP, S])
        rsum = sb("rsum", [S, H])
        o = sb("o", [S, D])
        oT = sb("oT", [P, DC, S])

        p_a = pb("p_a", [P, 512])
        p_b = pb("p_b", [P, 512])
        p_t0 = pb("p_t0", [P, 512])
        p_t1 = pb("p_t1", [P, 512])
        p_s = pb("p_s", [P, ROWS, 512])
        p_t = [p_t0, p_t1]

        loaded = sem("loaded")
        cleared = sem("cleared")
        xn_ready = sem("xn_ready")
        xnT_made = sem("xnT_made")
        xnT_ready = sem("xnT_ready")
        qk_made = sem("qk_made")
        v_made = sem("v_made")
        v_ready = sem("v_ready")
        rot_terms = sem("rot_terms")
        rotated = sem("rotated")
        qT_made = sem("qT_made")
        kT_made = sem("kT_made")
        qT_ready = sem("qT_ready")
        kT_ready = sem("kT_ready")
        s_made = sem("s_made")
        masked = sem("masked")
        max_ready = sem("max_ready")
        shifted = sem("shifted")
        e_ready = sem("e_ready")
        eT_made = sem("eT_made")
        eT_ready = sem("eT_ready")
        pv_made = sem("pv_made")
        rsum_ready = sem("rsum_ready")
        o_ready = sem("o_ready")
        oT_made = sem("oT_made")
        oT_ready = sem("oT_ready")
        out_made = sem("out_made")
        x_added = sem("x_added")
        stats_kept = sem("stats_kept")

        block = ctx.enter_context(nc.Block())

        @block.sync
        def _(sp):
            sp.dma_start(w_qkv[:], wqkv_dram).then_inc(loaded, 16)
            sp.dma_start(w_o[:], wo_dram).then_inc(loaded, 16)
            sp.dma_start(cos_t[:], cos_dram).then_inc(loaded, 16)
            sp.dma_start(sin_t[:], sin_dram).then_inc(loaded, 16)
            sp.dma_start(mask[:], mask_dram).then_inc(loaded, 16)
            sp.wait_ge(loaded, 80)

        @block.tensor
        def _(pe):
            pe.wait_ge(loaded, 80)

            def transpose_xn(b, slot):
                pe.wait_ge(xn_ready, b + 1)
                if later(b):
                    pe.wait_ge(qT_ready, b)
                for c in range(DC):
                    mm = pe.transpose(p_a[:, c * S:(c + 1) * S], xn[:, c * P:(c + 1) * P], ident[0:S, 0:S])
                mm.then_inc(xnT_made, 1)

            def transpose_e(b, slot):
                for j in range(ROWS):
                    if j == 0:
                        pe.wait_ge(e_ready, b + 1)
                    if j >= 2:
                        pe.wait_ge(eT_ready, ROWS * b + j - 1)
                    elif j == 0 and later(b):
                        pe.wait_ge(x_added, b)
                    elif j == 1 and later(b):
                        pe.wait_ge(oT_ready, b)
                    for hp in range(HP):
                        mm = pe.transpose(p_t[j % 2][0:S, hp * S:(hp + 1) * S], e[:, j, hp, :], ident[0:S, 0:S])
                    mm.then_inc(eT_made, 1)

            def project_qkv(b, slot):
                pe.wait_ge(xnT_ready, b + 1)
                if later(b):
                    pe.wait_ge(kT_ready, b)
                for c in range(DC):
                    mm = pe.matmul(p_b[0:S, :], xnT[:, c, :], w_qkv[:, c, 0:2 * D], start=c == 0, stop=c == DC - 1)
                mm.then_inc(qk_made, 1)
                for c in range(DC):
                    mm = pe.matmul(p_a[0:S, 0:D], xnT[:, c, :], w_qkv[:, c, 2 * D:3 * D],
                                   start=c == 0, stop=c == DC - 1)
                mm.then_inc(v_made, 1)

            def scores(b, slot):
                pe.wait_ge(qT_ready, b + 1)
                pe.wait_ge(kT_ready, b + 1)
                if later(b):
                    pe.wait_ge(masked, ROWS * b)
                for hp in range(HP):
                    for j in range(ROWS):
                        mm = pe.matmul(p_s[0:S, j, hp * S:(hp + 1) * S], qT[32 * j:32 * j + 32, hp, :],
                                       kT[32 * j:32 * j + 32, hp // 2, :], start=True, stop=True)
                mm.then_inc(s_made, 1)

            def weigh_values(b, slot):
                pe.wait_ge(eT_ready, ROWS * (b + 1))
                pe.wait_ge(v_ready, b + 1)
                for j in range(ROWS):
                    for hp in range(HP):
                        h = head_of(j, hp)
                        mm = pe.matmul(p_t0[0:S, h * VA:(h + 1) * VA], eT[:, j, hp, :], v_aug[:, b % 3, h, :],
                                       start=True, stop=True)
                mm.then_inc(pv_made, 1)

            def transpose_qk(b, slot):
                pe.wait_ge(rotated, 3 * b + 3)
                pe.wait_ge(v_ready, b + 1)
                for hp in range(HP):
                    mm = pe.transpose(p_a[:, hp * S:(hp + 1) * S],
                                      q_split[:, hp, :, :].rearrange("s r f -> s (r f)"), ident[0:S, 0:S])
                mm.then_inc(qT_made, 1)
                for c in range(DC):
                    mm = pe.transpose(p_b[:, c * S:(c + 1) * S], k_rot[:, c * P:(c + 1) * P], ident[0:S, 0:S])
                mm.then_inc(kT_made, 1)

            def transpose_o(b, slot):
                pe.wait_ge(o_ready, b + 1)
                for c in range(DC):
                    mm = pe.transpose(p_t1[:, c * S:(c + 1) * S], o[:, c * P:(c + 1) * P], ident[0:S, 0:S])
                mm.then_inc(oT_made, 1)

            def project_out(b, slot):
                pe.wait_ge(oT_ready, b + 1)
                for c in range(DC):
                    mm = pe.matmul(p_t0[0:S, 0:D], oT[:, c, :], w_o[:, c, :], start=c == 0, stop=c == DC - 1)
                mm.then_inc(out_made, 1)

            Stages(pe, [
                (transpose_xn, 0),
                (transpose_e, 2),
                (scores, 1),
                (project_qkv, 0),
                (weigh_values, 2),
                (transpose_qk, 0),
                (transpose_o, 2),
                (project_out, 2),
            ], B)

        @block.vector
        def _(dve):
            dve.memset(q_split[:], 0.0).then_inc(cleared, 1)
            dve.memset(v_aug[:], 1.0).then_inc(cleared, 1)
            dve.wait_ge(cleared, 2)
            dve.wait_ge(loaded, 80)

            def normalise(b, slot):
                if later(b):
                    dve.wait_ge(xnT_made, b)
                dve.tensor_scalar(xn[:], x_all[:, b, :], mv[:, b, 0:1], rstd[:, bass.ds(b, 1)],
                                  ALU.subtract, ALU.mult).then_inc(xn_ready, 1)

            def rotate(b, slot):
                dve.wait_ge(qk_made, b + 1)
                if later(b):
                    dve.wait_ge(rotated, 3 * b)
                dve.tensor_tensor(t_cos[:], p_b[0:S, :], cos_t[:], ALU.mult).then_inc(rot_terms, 1)
                dve.tensor_tensor(t_sin[:, 0::2], p_b[0:S, 1::2], sin_t[:, 0::2], ALU.mult).then_inc(rot_terms, 1)
                dve.tensor_tensor(t_sin[:, 1::2], p_b[0:S, 0::2], sin_t[:, 1::2], ALU.mult).then_inc(rot_terms, 1)
                dve.wait_ge(rot_terms, 3 * b + 3)
                if later(b):
                    dve.wait_ge(kT_made, b)
                parts = lambda t: t[:, 0:D].rearrange("s (f r p d) -> s f r p d", f=2, r=ROWS, p=2)
                split = q_split[:, :, :, :].rearrange("s (f p) r d -> s f p r d", p=2)
                for par in range(2):
                    dve.tensor_tensor(split[:, :, par, :, par * DK:(par + 1) * DK], parts(t_cos)[:, :, :, par, :],
                                      parts(t_sin)[:, :, :, par, :], ALU.add).then_inc(rotated, 1)
                dve.tensor_tensor(k_rot[:], t_cos[:, D:2 * D], t_sin[:, D:2 * D], ALU.add).then_inc(rotated, 1)

            def mask_scores(b, slot):
                dve.wait_ge(s_made, b + 1)
                if later(b):
                    dve.wait_ge(eT_made, ROWS * b)
                for j in range(ROWS):
                    dve.tensor_tensor(e[:, j, :, :], p_s[0:S, j, 0:HP * S].rearrange("q (h k) -> q h k", h=HP),
                                            mask[:, :].unsqueeze(1).broadcast_to([S, HP, S]),
                                      ALU.add).then_inc(masked, 1)
                dve.wait_ge(masked, ROWS * (b + 1))
                dve.tensor_reduce(mx[:], e[:].rearrange("q r h k -> q (r h) k"), X, ALU.max).then_inc(max_ready, 1)

            def divide(b, slot):
                dve.wait_ge(pv_made, b + 1)
                if later(b):
                    dve.wait_ge(o_ready, b)
                pv = p_t0[0:S, 0:H * VA].rearrange("q (h d) -> q h d", h=H)
                dve.reciprocal(rsum[:], pv[:, :, DK]).then_inc(rsum_ready, 1)
                dve.wait_ge(rsum_ready, b + 1)
                dve.tensor_tensor(o[:].rearrange("q (h d) -> q h d", h=H), pv[:, :, 0:DK],
                                  rsum[:].unsqueeze(2).broadcast_to([S, H, DK]), ALU.mult).then_inc(o_ready, 1)

            def add_to_x(b, slot):
                dve.wait_ge(out_made, b + 1)
                dve.tensor_tensor(x_all[:, b, :], p_t0[0:S, 0:D], x_all[:, b, :], ALU.add).then_inc(x_added, 1)
                dve.wait_ge(x_added, b + 1)
                dve.bn_stats(stats[:, b, :], x_all[:, b, :]).then_inc(stats_kept, 1)

            Stages(dve, [
                (mask_scores, 1),
                (rotate, 0),
                (divide, 2),
                (add_to_x, 2),
                (normalise, -1),
            ], B)

        @block.scalar
        def _(act):
            act.wait_ge(cleared, 2)

            def copy_xnT(b, slot):
                act.wait_ge(xnT_made, b + 1)
                if later(b):
                    act.wait_ge(v_made, b)
                act.copy(xnT[:].rearrange("p c s -> p (c s)"), p_a[:, 0:DC * S]).then_inc(xnT_ready, 1)

            def copy_eT(b, slot):
                for j in range(ROWS):
                    act.wait_ge(eT_made, ROWS * b + j + 1)
                    if j == 0 and later(b):
                        act.wait_ge(pv_made, b)
                    act.copy(eT[:, j, :, :].rearrange("k h q -> k (h q)"),
                             p_t[j % 2][0:S, 0:HP * S]).then_inc(eT_ready, 1)

            def copy_v(b, slot):
                act.wait_ge(v_made, b + 1)
                if later(b, 3):
                    act.wait_ge(pv_made, b - 2)
                act.copy(v_aug[:, b % 3, :, 0:DK], p_a[0:S, 0:D].rearrange("k (h d) -> k h d", h=H)).then_inc(v_ready, 1)

            def copy_qkT(b, slot):
                act.wait_ge(qT_made, b + 1)
                if later(b):
                    act.wait_ge(s_made, b)
                act.copy(qT[:].rearrange("p h s -> p (h s)"), p_a[:, 0:HP * S]).then_inc(qT_ready, 1)
                act.wait_ge(kT_made, b + 1)
                act.copy(kT[:].rearrange("p c s -> p (c s)"), p_b[:, 0:DC * S]).then_inc(kT_ready, 1)

            def copy_oT(b, slot):
                act.wait_ge(oT_made, b + 1)
                if later(b):
                    act.wait_ge(out_made, b)
                act.copy(oT[:].rearrange("p c s -> p (c s)"), p_t1[:, 0:DC * S]).then_inc(oT_ready, 1)

            def exponentiate(b, slot):
                act.wait_ge(shifted, b + 1)
                flat = e[:].rearrange("q r h k -> q (r h k)")
                act.activation(flat, flat, ACT.Exp, scale=DK ** -0.5).then_inc(e_ready, 1)

            Stages(act, [
                (copy_xnT, 0),
                (copy_eT, 2),
                (copy_v, 0),
                (copy_qkT, 0),
                (copy_oT, 2),
                (exponentiate, 1),
            ], B)

        @block.gpsimd
        def _(pool):
            def shift(b, slot):
                pool.wait_ge(max_ready, b + 1)
                rows = e[:].rearrange("q r h k -> q (r h) k")
                pool.tensor_tensor(rows, rows, mx[:].unsqueeze(2).broadcast_to([S, H, S]),
                                   ALU.subtract).then_inc(shifted, 1)

            Stages(pool, [(shift, 1)], B)


def cross_attention(nc, x_all, mv, rstd, stats, ident, ident16, ctx_dram, w, shift_mask_dram):
    with ExitStack() as ctx:
        sb = lambda n, shape, dt=F32: ctx.enter_context(nc.sbuf_tensor(f"xa_{n}", shape, dt))
        pb = lambda n, shape, dt=F32: ctx.enter_context(nc.psum_tensor(f"xa_{n}", shape, dt))
        sem = lambda n: ctx.enter_context(nc.semaphore(f"xa_{n}"))
        NT = H // HP
        NK = len(KEYS)
        UNITS = NT * NK
        V2 = 2 * DK

        names = ("w_q", "w_k", "w_v", "w_o")
        widths = dict(w_q=NT * P, w_k=NT * P, w_v=D, w_o=D)
        raw = sb("raw", [P, DC, NT * P])
        w_hi = {n: sb(f"{n}_hi", [P, DC, widths[n]], F32R) for n in names}
        w_lo = {n: sb(f"{n}_lo", [P, DC, widths[n]], F32R) for n in names}
        b_q = sb("b_q", [P, NT])
        b_k = sb("b_k", [P, NT])
        b_v = sb("b_v", [S, D])
        b_o = sb("b_o", [S, D])
        is_low = sb("is_low", [P, 1])
        low_b_k = sb("low_b_k", [P, NT])
        shift_mask = sb("shift_mask", [P, HP, S])
        ones = sb("ones", [P, KEYS[0]], BF16)
        context = sb("context", [P, 2, DC, SCP])
        ctx_hi = sb("ctx_hi", [P, DC, SCP], F32R)
        ctx_lo = sb("ctx_lo", [P, DC, SCP], F32R)
        xn = sb("xn", [S, D])
        xnT_hi = sb("xnT_hi", [P, DC, S], F32R)
        xnT_lo = sb("xnT_lo", [P, DC, S], F32R)
        q_full = sb("q_full", [P, NT, S])
        q_hi = sb("q_hi", [P, NT, S], F32R)
        q_lo = sb("q_lo", [P, NT, S], F32R)
        qm_hi = sb("qm_hi", [P, 2, NT, HP, S], F32R)
        qm_lo = sb("qm_lo", [P, 2, NT, HP, S], F32R)
        k_low = sb("k_low", [P, 2, SCP], F32R)
        kT = sb("kT", [P, 2, NT, SCP], F32R)
        v_aug = sb("v_aug", [KEYS[0], 2, NK, H, V2])
        nmax = sb("nmax", [S, NT, HP])
        nmax2 = sb("nmax2", [S, NT, V2], BF16)
        shift = sb("shift", [P, HP, S], BF16)
        eT = sb("eT", [KEYS[0], ER, HP, S])
        o_raw = sb("o_raw", [P, NT, S])
        rsum = sb("rsum", [S, H])
        o = sb("o", [S, D])
        oT_hi = sb("oT_hi", [P, DC, S], F32R)
        oT_lo = sb("oT_lo", [P, DC, S], F32R)

        p_s = [pb(f"p_s{i}", [P, 512]) for i in range(2)]
        p_e = [pb(f"p_e{i}", [P, 512]) for i in range(2)]
        p_o = pb("p_o", [P, 512])
        p_k = [pb(f"p_k{i}", [P, 512]) for i in range(2)]
        p_x = pb("p_x", [P, 512])

        loaded = sem("loaded")
        cleared = sem("cleared")
        raw_in = sem("raw_in")
        w_rounded = sem("w_rounded")
        w_left = sem("w_left")
        biases = sem("biases")
        context_in = [sem("context_in0"), sem("context_in1")]
        ctx_rounded = sem("ctx_rounded")
        ctx_left = sem("ctx_left")
        xn_ready = sem("xn_ready")
        xnT_made = sem("xnT_made")
        xnT_rounded = sem("xnT_rounded")
        xnT_left = sem("xnT_left")
        q_made = sem("q_made")
        q_ready = sem("q_ready")
        q_rounded = sem("q_rounded")
        q_left = sem("q_left")
        q_hi_placed = [sem("q_hi_placed0"), sem("q_hi_placed1")]
        q_lo_placed = [sem("q_lo_placed0"), sem("q_lo_placed1")]
        k_made = sem("k_made")
        k_rounded = sem("k_rounded")
        k_ready = sem("k_ready")
        v_made = sem("v_made")
        v_ready = sem("v_ready")
        s_made = sem("s_made")
        max_ready = sem("max_ready")
        high_ready = sem("high_ready")
        low_ready = sem("low_ready")
        maxT_made = sem("maxT_made")
        shift_ready = sem("shift_ready")
        sT_made = sem("sT_made")
        e_ready = sem("e_ready")
        pv_unit = sem("pv_unit")
        o_raw_ready = sem("o_raw_ready")
        back_made = sem("back_made")
        rsum_ready = sem("rsum_ready")
        divided = sem("divided")
        o_ready = sem("o_ready")
        oT_made = sem("oT_made")
        oT_rounded = sem("oT_rounded")
        oT_left = sem("oT_left")
        out_made = sem("out_made")
        x_added = sem("x_added")
        bo_added = sem("bo_added")
        stats_kept = sem("stats_kept")

        block = ctx.enter_context(nc.Block())
        N_LOADS = 6
        N_CLEARED = 5

        def in_turn(b):
            return b // 2 + 1

        def at_most(b, n):
            return min(b + n, B) if isinstance(b, int) else b + n

        @block.sync
        def _(sp):
            for i, n in enumerate(names):
                if i:
                    sp.wait_ge(w_left, i)
                    sp.wait_ge(w_rounded, i)
                sp.dma_start(raw[:, :, 0:widths[n]], w[n]).then_inc(raw_in, 16)
                if i == 0:
                    for dst, src in ((b_q, w["b_q"]), (b_k, w["b_k"]), (is_low, w["is_low"]), (shift_mask, shift_mask_dram)):
                        sp.dma_start(dst[:], src).then_inc(loaded, 16)
                    for dst, src in ((b_v, w["b_v"]), (b_o, w["b_o"])):
                        sp.dma_start(dst[:], src.partition_broadcast(S)).then_inc(loaded, 16)
            sp.wait_ge(cleared, N_CLEARED)

            def load_context(b, slot):
                if later(b, 2):
                    sp.wait_ge(ctx_left, b - 1)
                    sp.wait_ge(ctx_rounded, b - 1)
                sp.dma_start(context[:, slot], ctx_dram[b]).then_inc(context_in[slot], 16)

            def place_q(b, slot):
                if later(b, 2):
                    sp.wait_ge(sT_made, UNITS * (b - 1))
                sp.wait_ge(q_rounded, b + 1)
                for a in range(HP):
                    rows = slice(32 * a, 32 * a + 32)
                    sp.dma_start(qm_hi[rows, slot, :, a, :].bitcast(F32), q_hi[rows].bitcast(F32)).then_inc(q_hi_placed[slot], 16)
                sp.wait_ge(q_left, b + 1)
                for a in range(HP):
                    rows = slice(32 * a, 32 * a + 32)
                    sp.dma_start(qm_lo[rows, slot, :, a, :].bitcast(F32), q_lo[rows].bitcast(F32)).then_inc(q_lo_placed[slot], 16)

            Stages(sp, [(load_context, -2), (place_q, -1)], B)

        @block.tensor
        def _(pe):
            def transpose_xn(b, slot):
                pe.wait_ge(xn_ready, b + 1)
                if later(b):
                    pe.wait_ge(q_ready, b)
                if later(b, 2):
                    pe.wait_ge(shift_ready, b - 1)
                if later(b, 3):
                    pe.wait_ge(x_added, b - 2)
                for c in range(DC):
                    mm = pe.transpose(p_x[:, c * S:(c + 1) * S], xn[:, c * P:(c + 1) * P], ident[0:S, 0:S])
                mm.then_inc(xnT_made, 1)

            def project_q(b, slot):
                pe.wait_ge(xnT_rounded, b + 1)
                pe.wait_ge(xnT_left, b + 1)
                for t in range(NT):
                    cols = slice(t * P, (t + 1) * P)
                    n = 0
                    for c in range(DC):
                        for a, x in ((w_hi["w_q"], xnT_hi), (w_lo["w_q"], xnT_hi), (w_hi["w_q"], xnT_lo)):
                            mm = pe.matmul(p_x[:, t * S:(t + 1) * S], a[:, c, cols], x[:, c, :],
                                           start=n == 0, stop=n == 3 * DC - 1)
                            n += 1
                mm.then_inc(q_made, 1)

            def transpose_max(b, slot):
                pe.wait_ge(low_ready, b + 1)
                pe.wait_ge(q_ready, at_most(b, 2))
                if later(b, 2):
                    pe.wait_ge(x_added, b - 1)
                pe.transpose(p_x[:, :].bitcast(BF16)[:, 0:S], nmax2[:].rearrange("s r f -> s (r f)"),
                             ident16[0:S, 0:S]).then_inc(maxT_made, 1)

            def project_k(b, slot, t):
                if t == 0:
                    pe.wait_ge(ctx_rounded, b + 1)
                    pe.wait_ge(ctx_left, b + 1)
                if t >= 2:
                    pe.wait_ge(k_ready, NT * b + t - 1)
                elif later(b):
                    pe.wait_ge(v_ready, NK * b - 1 + t)
                cols = slice(t * P, (t + 1) * P)
                n = 0
                for d in range(DC):
                    for a, x in ((w_hi["w_k"], ctx_hi), (w_lo["w_k"], ctx_hi), (w_hi["w_k"], ctx_lo)):
                        mm = pe.matmul(p_k[(slot + t) % 2][:, 0:SCP], a[:, d, cols], x[:, d, :],
                                       start=n == 0, stop=n == 3 * DC - 1)
                        n += 1
                mm.then_inc(k_made, 1)

            def project_v(b, slot, j):
                if j < 2:
                    pe.wait_ge(k_ready, NT * b + NT - 1 + j)
                else:
                    pe.wait_ge(v_ready, NK * b + 1)
                keys = slice(KEY0[j], KEY0[j] + KEYS[j])
                n = 0
                for d in range(DC):
                    for a, x in ((ctx_hi, w_hi["w_v"]), (ctx_lo, w_hi["w_v"]), (ctx_hi, w_lo["w_v"])):
                        mm = pe.matmul(p_k[(slot + NT + j) % 2][0:KEYS[j], 0:D], a[:, d, keys], x[:, d, :],
                                       start=n == 0, stop=n == 3 * DC - 1)
                        n += 1
                mm.then_inc(v_made, 1)

            def scores(b, slot, h):
                if h == 0:
                    pe.wait_ge(q_hi_placed[slot], HP * 16 * in_turn(b))
                if h % HP == 0:
                    pe.wait_ge(k_ready, NT * b + h // HP + 1)
                if h >= 2:
                    pe.wait_ge(max_ready, H * b + h - 1)
                elif later(b):
                    pe.wait_ge(max_ready, H * b + h - 1)
                t, a = divmod(h, HP)
                pe.matmul(p_s[h % 2][0:S, 0:SCP], qm_hi[:, slot, t, a, :], kT[:, slot, t, :],
                          start=True, stop=True).then_inc(s_made, 1)

            def scores_t(b, slot, u):
                t, n = divmod(u, NK)
                if u == 0:
                    pe.wait_ge(shift_ready, b + 1)
                    pe.wait_ge(q_lo_placed[slot], HP * 16 * in_turn(b))
                if u >= 2 or later(b):
                    pe.wait_ge(e_ready, UNITS * b + u - 1)
                keys = slice(KEY0[n], KEY0[n] + KEYS[n])
                rows = slice(32 * t, 32 * t + 32)
                to = p_e[u % 2][0:KEYS[n], 0:HP * S]
                pe.matmul(to, ones[rows, 0:KEYS[n]], shift[rows].rearrange("h r q -> h (r q)"), start=True, stop=False)
                for q in (qm_hi, qm_lo):
                    mm = pe.matmul(to, kT[:, slot, t, keys], q[:, slot, t].rearrange("p a s -> p (a s)"),
                                   start=False, stop=q is qm_lo)
                mm.then_inc(sT_made, 1)

            def weigh_values(b, slot, u):
                t, n = divmod(u, NK)
                pe.wait_ge(e_ready, UNITS * b + u + 1)
                if u == 0:
                    pe.wait_ge(v_ready, NK * (b + 1))
                    if later(b):
                        pe.wait_ge(o_raw_ready, b)
                for a in range(HP):
                    mm = pe.matmul(p_o[32 * a:32 * a + 32, t * S:(t + 1) * S], v_aug[0:KEYS[n], slot, n, HP * t + a, :],
                                   eT[0:KEYS[n], u % ER, a, :], start=u == 0, stop=n == NK - 1, skip_group_check=True)
                mm.then_inc(pv_unit, 1)

            def transpose_back(b, slot):
                pe.wait_ge(o_raw_ready, b + 1)
                pe.wait_ge(shift_ready, at_most(b, 2))
                if later(b):
                    pe.wait_ge(x_added, b)
                for t in range(NT):
                    mm = pe.transpose(p_x[0:S, t * P:(t + 1) * P], o_raw[:, t, :], ident[:])
                mm.then_inc(back_made, 1)

            def transpose_o(b, slot):
                pe.wait_ge(o_ready, b + 1)
                for c in range(DC):
                    mm = pe.transpose(p_x[:, c * S:(c + 1) * S], o[:, c * P:(c + 1) * P], ident[0:S, 0:S])
                mm.then_inc(oT_made, 1)

            def project_out(b, slot):
                pe.wait_ge(oT_rounded, b + 1)
                pe.wait_ge(oT_left, b + 1)
                n = 0
                for c in range(DC):
                    for a, x in ((oT_hi, w_hi["w_o"]), (oT_lo, w_hi["w_o"]), (oT_hi, w_lo["w_o"])):
                        mm = pe.matmul(p_x[0:S, 0:D], a[:, c, :], x[:, c, :], start=n == 0, stop=n == 3 * DC - 1)
                        n += 1
                mm.then_inc(out_made, 1)

            pe.wait_ge(w_left, len(names))
            pe.wait_ge(cleared, N_CLEARED)
            part = lambda f, *a: (lambda b, slot: f(b, slot, *a))
            st = lambda u: (part(scores_t, u), 1)
            pv = lambda u: (part(weigh_values, u), 1)
            mx = lambda h: (part(scores, h), 0)
            k = lambda t: (part(project_k, t), 0)
            v = lambda j: (part(project_v, j), 0)
            Stages(pe, [
                k(0), (part(weigh_values, UNITS - 1), 2), (transpose_max, 1), k(1), st(0), k(2), mx(0), st(1),
                pv(0), mx(1), (transpose_back, 2), k(3), mx(2), st(2), pv(1), mx(3), v(0), mx(4), st(3), pv(2),
                mx(5), (transpose_o, 2), v(1), mx(6), st(4), pv(3), mx(7), st(5), pv(4), v(2), mx(8),
                (project_out, 2), st(6), pv(5), mx(9), (transpose_xn, -1), mx(10), st(7), pv(6), mx(11), st(8),
                pv(7), mx(12), (project_q, -1), mx(13), st(9), pv(8), mx(14), st(10), pv(9), mx(15), st(11),
                pv(10),
            ], B)

        @block.vector
        def _(dve):
            dve.memset(qm_hi[:].bitcast(F32), 0.0).then_inc(cleared, 1)
            dve.memset(qm_lo[:].bitcast(F32), 0.0).then_inc(cleared, 1)
            dve.memset(v_aug[:], 1.0).then_inc(cleared, 1)
            dve.memset(nmax2[:], 0.0).then_inc(cleared, 1)
            dve.memset(ones[:], 1.0).then_inc(cleared, 1)
            for i, n in enumerate(names):
                dve.wait_ge(w_rounded, i + 1)
                dve.tensor_tensor(w_lo[n][:], raw[:, :, 0:widths[n]], w_hi[n][:].bitcast(F32), ALU.subtract).then_inc(w_left, 1)
            dve.wait_ge(cleared, N_CLEARED)
            dve.wait_ge(loaded, 16 * N_LOADS)
            dve.tensor_scalar(b_q[:], b_q[:], DK ** -0.5, None, ALU.mult).then_inc(biases, 1)
            dve.tensor_scalar(low_b_k[:], b_k[:], is_low[:, 0:1], None, ALU.mult).then_inc(biases, 1)
            dve.wait_ge(biases, 2)

            def normalise(b, slot):
                if later(b):
                    dve.wait_ge(xnT_made, b)
                dve.tensor_scalar(xn[:], x_all[:, b, :], mv[:, b, 0:1], rstd[:, bass.ds(b, 1)],
                                  ALU.subtract, ALU.mult).then_inc(xn_ready, 1)

            def leave_xnT(b, slot):
                dve.wait_ge(xnT_rounded, b + 1)
                if later(b):
                    dve.wait_ge(q_made, b)
                dve.tensor_tensor(xnT_lo[:].rearrange("p c s -> p (c s)"), p_x[:, 0:DC * S],
                                  xnT_hi[:].rearrange("p c s -> p (c s)").bitcast(F32), ALU.subtract).then_inc(xnT_left, 1)

            def bias_q(b, slot):
                dve.wait_ge(q_made, b + 1)
                if later(b):
                    dve.wait_ge(q_left, b)
                dve.scalar_tensor_tensor(out=q_full[:], in0=p_x[:, 0:NT * S].rearrange("p (t s) -> p t s", t=NT),
                                         scalar=DK ** -0.5, in1=b_q[:].unsqueeze(2).broadcast_to([P, NT, S]),
                                         op0=ALU.mult, op1=ALU.add).then_inc(q_ready, 1)

            def leave_q(b, slot):
                dve.wait_ge(q_rounded, b + 1)
                if later(b):
                    dve.wait_ge(q_lo_placed[1 - slot], HP * 16 * in_turn(b - 1))
                dve.tensor_tensor(q_lo[:], q_full[:], q_hi[:].bitcast(F32), ALU.subtract).then_inc(q_left, 1)

            def stack_k(b, slot, t):
                dve.wait_ge(k_rounded, NT * b + t + 1)
                if t == 0 and later(b, 2):
                    dve.wait_ge(sT_made, UNITS * (b - 1))
                dve.scalar_tensor_tensor(out=kT[:, slot, t, :], in0=p_k[(slot + t) % 2][:, 0:SCP], scalar=b_k[:, t:t + 1],
                                         in1=k_low[:, t % 2, :].bitcast(F32), op0=ALU.add,
                                         op1=ALU.subtract).then_inc(k_ready, 1)

            def find_max(b, slot, h):
                dve.wait_ge(s_made, H * b + h + 1)
                if h == 0 and later(b):
                    dve.wait_ge(low_ready, b)
                t, a = divmod(h, HP)
                dve.tensor_reduce(nmax[:, t, a:a + 1], p_s[h % 2][0:S, 0:SC], X, ALU.max, negate=True).then_inc(max_ready, 1)

            def split_max(b, slot):
                dve.wait_ge(max_ready, H * (b + 1))
                if later(b):
                    dve.wait_ge(maxT_made, b)
                high, low = nmax2[:, :, 0:HP], nmax2[:, :, HP:2 * HP]
                dve.tensor_copy(high, nmax[:]).then_inc(high_ready, 1)
                dve.wait_ge(high_ready, b + 1)
                dve.tensor_tensor(low, nmax[:], high, ALU.subtract).then_inc(low_ready, 1)

            def make_shift(b, slot):
                dve.wait_ge(maxT_made, b + 1)
                if later(b):
                    dve.wait_ge(sT_made, UNITS * b)
                dve.tensor_tensor(shift[:], p_x[:, :].bitcast(BF16)[:, 0:S].unsqueeze(1).broadcast_to([P, HP, S]),
                                  shift_mask[:], ALU.mult).then_inc(shift_ready, 1)

            def divide(b, slot):
                dve.wait_ge(back_made, b + 1)
                if later(b):
                    dve.wait_ge(oT_made, b)
                    dve.wait_ge(divided, b)
                pv = p_x[0:S, 0:H * V2].rearrange("q (h d) -> q h d", h=H)
                dve.reciprocal(rsum[:], pv[:, :, DK]).then_inc(rsum_ready, 1)
                dve.wait_ge(rsum_ready, b + 1)
                dve.tensor_tensor(o[:].rearrange("q (h d) -> q h d", h=H), pv[:, :, 0:DK],
                                  rsum[:].unsqueeze(2).broadcast_to([S, H, DK]), ALU.mult).then_inc(divided, 1)
                dve.wait_ge(divided, b + 1)
                dve.tensor_tensor(o[:], o[:], b_v[:], ALU.add).then_inc(o_ready, 1)

            def leave_oT(b, slot):
                dve.wait_ge(oT_rounded, b + 1)
                if later(b):
                    dve.wait_ge(out_made, b)
                dve.tensor_tensor(oT_lo[:].rearrange("p c s -> p (c s)"), p_x[:, 0:DC * S],
                                  oT_hi[:].rearrange("p c s -> p (c s)").bitcast(F32), ALU.subtract).then_inc(oT_left, 1)

            def add_to_x(b, slot):
                dve.wait_ge(out_made, b + 1)
                dve.wait_ge(bo_added, b + 1)
                dve.tensor_tensor(x_all[:, b, :], p_x[0:S, 0:D], x_all[:, b, :], ALU.add).then_inc(x_added, 1)

            def keep_stats(b, slot):
                dve.wait_ge(x_added, b + 1)
                dve.bn_stats(stats[:, b, :], x_all[:, b, :]).then_inc(stats_kept, 1)

            part = lambda f, *a: (lambda b, slot: f(b, slot, *a))
            k = lambda t: (part(stack_k, t), 0)
            mx = lambda h: (part(find_max, h), 0)
            Stages(dve, [
                (make_shift, 1), k(0), k(1), k(2), mx(0), mx(1), (divide, 2), k(3), mx(2), mx(3), mx(4), mx(5),
                (leave_oT, 2), mx(6), mx(7), mx(8), (add_to_x, 2), mx(9), (leave_xnT, -1), mx(10), mx(11), mx(12),
                (bias_q, -1), mx(13), (leave_q, -1), (keep_stats, 2), mx(14), mx(15), (split_max, 0),
                (normalise, -2),
            ], B)

        @block.scalar
        def _(act):
            for i, n in enumerate(names):
                act.wait_ge(raw_in, 16 * (i + 1))
                act.copy(w_hi[n][:], raw[:, :, 0:widths[n]]).then_inc(w_rounded, 1)
            act.wait_ge(cleared, N_CLEARED)
            act.wait_ge(biases, 2)

            def round_context(b, slot):
                act.wait_ge(context_in[slot], 16 * in_turn(b))
                if later(b):
                    act.wait_ge(v_made, NK * b)
                    act.wait_ge(ctx_left, b)
                act.copy(ctx_hi[:], context[:, slot]).then_inc(ctx_rounded, 1)

            def round_xnT(b, slot):
                act.wait_ge(xnT_made, b + 1)
                if later(b):
                    act.wait_ge(q_made, b)
                act.copy(xnT_hi[:].rearrange("p c s -> p (c s)"), p_x[:, 0:DC * S]).then_inc(xnT_rounded, 1)

            def round_q(b, slot):
                act.wait_ge(q_ready, b + 1)
                if later(b):
                    act.wait_ge(q_hi_placed[1 - slot], HP * 16 * in_turn(b - 1))
                act.copy(q_hi[:], q_full[:]).then_inc(q_rounded, 1)

            def round_k(b, slot, t):
                act.wait_ge(k_made, NT * b + t + 1)
                if t >= 2 or later(b):
                    act.wait_ge(k_ready, NT * b + t - 1)
                act.activation(k_low[:, t % 2, :], p_k[(slot + t) % 2][:, 0:SCP], ACT.Identity, bias=low_b_k[:, t:t + 1],
                               scale=is_low[:, 0:1]).then_inc(k_rounded, 1)

            def copy_v(b, slot, j):
                act.wait_ge(v_made, NK * b + j + 1)
                if j == 0 and later(b, 2):
                    act.wait_ge(pv_unit, UNITS * (b - 1))
                act.copy(v_aug[0:KEYS[j], slot, j, :, 0:DK],
                         p_k[(slot + NT + j) % 2][0:KEYS[j], 0:D].rearrange("k (h d) -> k h d", h=H)).then_inc(v_ready, 1)

            def exponentiate(b, slot, u):
                act.wait_ge(sT_made, UNITS * b + u + 1)
                if u >= ER or later(b):
                    act.wait_ge(pv_unit, UNITS * b + u + 1 - ER)
                nk = KEYS[u % NK]
                act.activation(eT[0:nk, u % ER].rearrange("k h q -> k (h q)"), p_e[u % 2][0:nk, 0:HP * S],
                               ACT.Exp).then_inc(e_ready, 1)

            def copy_o_raw(b, slot):
                act.wait_ge(pv_unit, UNITS * (b + 1))
                if later(b):
                    act.wait_ge(back_made, b)
                act.copy(o_raw[:].rearrange("p t s -> p (t s)"), p_o[:, 0:NT * S]).then_inc(o_raw_ready, 1)

            def round_oT(b, slot):
                act.wait_ge(oT_made, b + 1)
                if later(b):
                    act.wait_ge(out_made, b)
                act.copy(oT_hi[:].rearrange("p c s -> p (c s)"), p_x[:, 0:DC * S]).then_inc(oT_rounded, 1)

            part = lambda f, *a: (lambda b, slot: f(b, slot, *a))
            ex = lambda u: (part(exponentiate, u), 1)
            k = lambda t: (part(round_k, t), 0)
            v = lambda j: (part(copy_v, j), 0)
            Stages(act, [
                k(0), (copy_o_raw, 2), k(1), ex(0), k(2), ex(1), k(3), ex(2), v(0), ex(3), (round_oT, 2), v(1),
                ex(4), ex(5), v(2), ex(6), (round_xnT, -1), ex(7), (round_context, -1), ex(8), (round_q, -1),
                ex(9), ex(10), ex(11),
            ], B)

        @block.gpsimd
        def _(pool):
            def leave_context(b, slot):
                pool.wait_ge(ctx_rounded, b + 1)
                if later(b):
                    pool.wait_ge(v_made, NK * b)
                pool.tensor_tensor(ctx_lo[:], context[:, slot], ctx_hi[:].bitcast(F32), ALU.subtract).then_inc(ctx_left, 1)

            def add_bias_to_x(b, slot):
                pool.wait_ge(xn_ready, b + 1)
                pool.tensor_tensor(x_all[:, b, :], x_all[:, b, :], b_o[:], ALU.add).then_inc(bo_added, 1)

            pool.wait_ge(loaded, 16 * N_LOADS)
            Stages(pool, [(add_bias_to_x, 0), (leave_context, -1)], B)


def route(nc, x_all, mv, rstd, ident, p, xnT_hi, xnT_lo, inv_sum, scratch):
    with ExitStack() as ctx:
        sb = lambda n, shape, dt=F32: ctx.enter_context(nc.sbuf_tensor(f"rt_{n}", shape, dt))
        pb = lambda n, shape, dt=F32: ctx.enter_context(nc.psum_tensor(f"rt_{n}", shape, dt))
        sem = lambda n: ctx.enter_context(nc.semaphore(f"rt_{n}"))

        gamma = sb("gamma", [S, D])
        slot_gamma = sb("slot_gamma", [P, D])
        slots = sb("slots", [P, E, D])
        squares = sb("squares", [P, D])
        norm = sb("norm", [P, E])
        sn = sb("sn", [P, E, D])
        snT_hi = sb("snT_hi", [P, DC, E * P], F32R)
        snT_lo = sb("snT_lo", [P, DC, E * P], F32R)
        scale = sb("scale", [S, B])
        scaled = sb("scaled", [S, D])
        xn = sb("xn", [S, 2, D])
        cur_hi = sb("cur_hi", [P, DC, S], F32R)
        cur_lo = sb("cur_lo", [P, DC, S], F32R)
        nmax = sb("nmax", [S, B])
        nmaxT = sb("nmaxT", [B, S])
        weights = sb("weights", [S, E * P])
        total = sb("total", [S, B])

        p_t = pb("p_t", [P, 512])
        p_sn = [pb(f"p_sn{i}", [P, 512]) for i in range(2)]
        p_l = pb("p_l", [P, 2, 512])

        loaded = sem("loaded")
        squared = sem("squared")
        steps = sem("steps")
        rooted = sem("rooted")
        sn_ready = sem("sn_ready")
        snT_made = sem("snT_made")
        snT_rounded = sem("snT_rounded")
        snT_left = sem("snT_left")
        sn_kept = sem("sn_kept")
        scaled_ready = sem("scaled_ready")
        xn_ready = sem("xn_ready")
        xn_kept = [sem("xn_kept0"), sem("xn_kept1")]
        xnT_made = sem("xnT_made")
        xnT_rounded = sem("xnT_rounded")
        xnT_left = sem("xnT_left")
        xnT_kept = sem("xnT_kept")
        logits_made = sem("logits_made")
        max_ready = sem("max_ready")
        exp_done = sem("exp_done")
        inv_ready = sem("inv_ready")
        maxT_made = sem("maxT_made")
        maxT_ready = sem("maxT_ready")
        max_kept = sem("max_kept")
        block = ctx.enter_context(nc.Block())

        @block.sync
        def _(sp):
            sp.dma_start(slots[:], p["slots"]).then_inc(loaded, 16)
            sp.dma_start(gamma[:], p["gamma"].partition_broadcast(S)).then_inc(loaded, 16)
            sp.dma_start(slot_gamma[:], p["slot_gamma"].partition_broadcast(P)).then_inc(loaded, 16)

            sp.wait_ge(snT_rounded, DC * E)
            sp.dma_start(scratch["snT_hi"].bitcast(F32), snT_hi[:].bitcast(F32)).then_inc(sn_kept, 16)
            sp.wait_ge(snT_left, DC * E)
            sp.dma_start(scratch["snT_lo"].bitcast(F32), snT_lo[:].bitcast(F32)).then_inc(sn_kept, 16)

            def keep_xn(b, slot):
                sp.wait_ge(xn_ready, b + 1)
                sp.dma_start(scratch["xn"][b], xn[:, slot]).then_inc(xn_kept[slot], 16)

            Stages(sp, [(keep_xn, 0)], B)
            sp.wait_ge(maxT_ready, 1)
            sp.dma_start(scratch["nmax"], nmaxT[:]).then_inc(max_kept, 16)
            sp.wait_ge(max_kept, 16)
            sp.wait_ge(sn_kept, 32)
            sp.wait_ge(xn_kept[0], 16 * (B // 2))
            sp.wait_ge(xn_kept[1], 16 * (B // 2))

        @block.tensor
        def _(pe):
            pe.wait_ge(sn_ready, E)
            for e in range(E):
                for c in range(DC):
                    n = DC * e + c
                    if n >= 2:
                        pe.wait_ge(snT_left, n - 1)
                    pe.transpose(p_sn[n % 2][:, 0:P], sn[:, e, c * P:(c + 1) * P], ident[:]).then_inc(snT_made, 1)
            pe.wait_ge(snT_left, DC * E)

            def transpose_xn(b, slot):
                pe.wait_ge(xn_ready, b + 1)
                if later(b):
                    pe.wait_ge(xnT_left, b)
                for c in range(DC):
                    mm = pe.transpose(p_t[:, c * S:(c + 1) * S], xn[:, slot, c * P:(c + 1) * P], ident[0:S, 0:S])
                mm.then_inc(xnT_made, 1)

            def logits(b, slot):
                pe.wait_ge(xnT_rounded, b + 1)
                pe.wait_ge(xnT_left, b + 1)
                if later(b):
                    pe.wait_ge(exp_done, b)
                for half in range(2):
                    cols = slice(half * 512, half * 512 + 512)
                    n = 0
                    for c in range(DC):
                        for a, w in ((cur_hi, snT_hi), (cur_lo, snT_hi), (cur_hi, snT_lo)):
                            mm = pe.matmul(p_l[0:S, half, :], a[:, c, :], w[:, c, cols], start=n == 0, stop=n == 3 * DC - 1)
                            n += 1
                mm.then_inc(logits_made, 1)

            Stages(pe, [(transpose_xn, 0), (logits, 1)], B)
            pe.wait_ge(max_ready, B)
            pe.wait_ge(xnT_left, B)
            pe.transpose(p_t[0:B, 0:S], nmax[:], ident[0:S, 0:S]).then_inc(maxT_made, 1)

        @block.vector
        def _(dve):
            dve.wait_ge(squared, E)
            dve.wait_ge(rooted, 1)
            dve.tensor_scalar(norm[:], norm[:], 1e-12, None, ALU.max).then_inc(steps, 1)
            dve.wait_ge(steps, 1)
            dve.reciprocal(norm[:], norm[:]).then_inc(steps, 1)
            dve.wait_ge(steps, 2)
            dve.tensor_scalar(norm[:], norm[:], float(D) ** 0.5, None, ALU.mult).then_inc(steps, 1)
            dve.wait_ge(steps, 3)
            for e in range(E):
                dve.scalar_tensor_tensor(out=sn[:, e, :], in0=slots[:, e, :], scalar=norm[:, e:e + 1], in1=slot_gamma[:],
                                         op0=ALU.mult, op1=ALU.mult).then_inc(sn_ready, 1)
            for n in range(DC * E):
                dve.wait_ge(snT_rounded, n + 1)
                e, c = divmod(n, DC)
                cols = slice(e * P, (e + 1) * P)
                dve.tensor_tensor(snT_lo[:, c, cols], p_sn[n % 2][:, 0:P], snT_hi[:, c, cols].bitcast(F32),
                                  ALU.subtract).then_inc(snT_left, 1)

            dve.tensor_tensor(scale[:], mv[:, :, 1], rstd[:], ALU.mult).then_inc(steps, 1)
            dve.wait_ge(steps, 4)
            dve.tensor_tensor(scale[:], scale[:], rstd[:], ALU.mult).then_inc(steps, 1)
            dve.wait_ge(steps, 5)
            dve.tensor_scalar(scale[:], scale[:], float(D), None, ALU.mult).then_inc(steps, 1)
            dve.wait_ge(rooted, 2)
            dve.tensor_scalar(scale[:], scale[:], 1e-12, None, ALU.max).then_inc(steps, 1)
            dve.wait_ge(steps, 7)
            dve.reciprocal(scale[:], scale[:]).then_inc(steps, 1)
            dve.wait_ge(steps, 8)
            dve.tensor_tensor(scale[:], scale[:], rstd[:], ALU.mult).then_inc(steps, 1)
            dve.wait_ge(steps, 9)
            dve.tensor_scalar(scale[:], scale[:], float(D) ** 0.5, None, ALU.mult).then_inc(steps, 1)
            dve.wait_ge(steps, 10)

            def normalise(b, slot):
                if later(b):
                    dve.wait_ge(xn_ready, b)
                if later(b, 2):
                    dve.wait_ge(xn_kept[slot], 16 * (b // 2))
                    dve.wait_ge(xnT_made, b - 1)
                dve.tensor_scalar(scaled[:], x_all[:, b, :], mv[:, b, 0:1], scale[:, bass.ds(b, 1)],
                                  ALU.subtract, ALU.mult).then_inc(scaled_ready, 1)
                dve.wait_ge(scaled_ready, b + 1)
                dve.tensor_tensor(xn[:, slot], scaled[:], gamma[:], ALU.mult).then_inc(xn_ready, 1)

            def leave_xnT(b, slot):
                dve.wait_ge(xnT_rounded, b + 1)
                if later(b):
                    dve.wait_ge(xnT_kept, 2 * b)
                    dve.wait_ge(logits_made, b)
                dve.tensor_tensor(cur_lo[:].rearrange("p c s -> p (c s)"), p_t[:, 0:DC * S],
                                  cur_hi[:].rearrange("p c s -> p (c s)").bitcast(F32), ALU.subtract).then_inc(xnT_left, 1)

            def find_max(b, slot):
                dve.wait_ge(logits_made, b + 1)
                dve.tensor_reduce(nmax[:, bass.ds(b, 1)], p_l[0:S].rearrange("s a n -> s (a n)"), X, ALU.max,
                                  negate=True).then_inc(max_ready, 1)

            Stages(dve, [(normalise, -1), (leave_xnT, 0), (find_max, 1)], B)
            dve.wait_ge(maxT_made, 1)
            dve.tensor_copy(nmaxT[:], p_t[0:B, 0:S]).then_inc(maxT_ready, 1)
            dve.wait_ge(exp_done, B)
            dve.reciprocal(inv_sum[:], total[:]).then_inc(inv_ready, 1)
            dve.wait_ge(inv_ready, 1)

        @block.scalar
        def _(act):
            act.wait_ge(loaded, 48)
            for e in range(E):
                if e:
                    act.wait_ge(squared, e)
                act.activation(squares[:], slots[:, e, :], ACT.Square, accum_out=norm[:, e:e + 1]).then_inc(squared, 1)
            act.wait_ge(squared, E)
            act.activation(norm[:], norm[:], ACT.Sqrt).then_inc(rooted, 1)
            for n in range(DC * E):
                act.wait_ge(snT_made, n + 1)
                e, c = divmod(n, DC)
                act.copy(snT_hi[:, c, e * P:(e + 1) * P], p_sn[n % 2][:, 0:P]).then_inc(snT_rounded, 1)
            act.wait_ge(steps, 6)
            act.activation(scale[:], scale[:], ACT.Sqrt).then_inc(rooted, 1)

            def round_xnT(b, slot):
                act.wait_ge(xnT_made, b + 1)
                if later(b):
                    act.wait_ge(xnT_kept, 2 * b)
                    act.wait_ge(logits_made, b)
                act.copy(cur_hi[:].rearrange("p c s -> p (c s)"), p_t[:, 0:DC * S]).then_inc(xnT_rounded, 1)

            def exponentiate(b, slot):
                act.wait_ge(max_ready, b + 1)
                if later(b):
                    act.wait_ge(exp_done, b)
                act.activation(weights[:], p_l[0:S].rearrange("s a n -> s (a n)"), ACT.Exp,
                               bias=nmax[:, bass.ds(b, 1)], accum_out=total[:, bass.ds(b, 1)]).then_inc(exp_done, 1)

            Stages(act, [(round_xnT, 0), (exponentiate, 1)], B)

        @block.gpsimd
        def _(pool):
            def keep_xnT(b, slot):
                pool.wait_ge(xnT_rounded, b + 1)
                pool.tensor_copy(xnT_hi[:, :, bass.ds(b * S, S)], cur_hi[:]).then_inc(xnT_kept, 1)
                pool.wait_ge(xnT_left, b + 1)
                pool.tensor_copy(xnT_lo[:, :, bass.ds(b * S, S)], cur_lo[:]).then_inc(xnT_kept, 1)

            Stages(pool, [(keep_xnT, 0)], B)
            pool.wait_ge(xnT_kept, 2 * B)


def experts(nc, x_all, ident, p, xnT_hi, xnT_lo, inv_sum, scratch):
    with ExitStack() as ctx:
        sb = lambda n, shape, dt=F32: ctx.enter_context(nc.sbuf_tensor(f"ex_{n}", shape, dt))
        pb = lambda n, shape, dt=F32: ctx.enter_context(nc.psum_tensor(f"ex_{n}", shape, dt))
        sem = lambda n: ctx.enter_context(nc.semaphore(f"ex_{n}"))
        N = GB * S
        R = GB * P

        w1_raw = sb("w1_raw", [P, DC, HID])
        w2_raw = sb("w2_raw", [P, HC, D])
        w1_hi = sb("w1_hi", [P, DC, HID], F32R)
        w1_lo = sb("w1_lo", [P, DC, HID], F32R)
        w2_hi = sb("w2_hi", [P, HC, D], F32R)
        w2_lo = sb("w2_lo", [P, HC, D], F32R)
        b1 = sb("b1", [P, E, HC])
        b2 = sb("b2", [P, E, D])
        snT_hi = sb("snT_hi", [P, DC, P], F32R)
        snT_lo = sb("snT_lo", [P, DC, P], F32R)
        nmax = sb("nmax", [P, N])
        xn = sb("xn", [S, GB, D])
        over = sb("over", [P, GB])
        dispatch = sb("dispatch", [P, GB, S])
        dsum = sb("dsum", [P, GB])
        dispatchT = sb("dispatchT", [S, GB, P])
        lag_c = sb("lag_c", [P, N])
        combine = sb("combine", [P, GB, S])
        slots_hi = sb("slots_hi", [P, DC, R], F32R)
        slots_lo = sb("slots_lo", [P, DC, R], F32R)
        h = sb("h", [P, 2, R])
        h_hi = sb("h_hi", [P, HC, R], F32R)
        h_lo = sb("h_lo", [P, HC, R], F32R)
        eo = sb("eo", [P, GB, D])

        p_h = [pb(f"p_h{i}", [P, 512]) for i in range(3)]
        p_e = [pb(f"p_e{i}", [P, 512]) for i in range(2)]
        p_c = pb("p_c", [P, 512])
        p_l = pb("p_l", [P, 512])
        p_x = pb("p_x", [P, 512])

        loaded = sem("loaded")
        w1_in = sem("w1_in")
        w2_in = sem("w2_in")
        sn_in = sem("sn_in")
        nmax_in = sem("nmax_in")
        xn_in = sem("xn_in")
        w1_split = sem("w1_split")
        w1_lost = sem("w1_lost")
        w2_split = sem("w2_split")
        w2_lost = sem("w2_lost")
        l_made = sem("l_made")
        over_ready = sem("over_ready")
        d_shifted = sem("d_shifted")
        c_shifted = sem("c_shifted")
        d_exp = sem("d_exp")
        dsum_ready = sem("dsum_ready")
        d_ready = sem("d_ready")
        dT_made = sem("dT_made")
        dT_ready = sem("dT_ready")
        c_ready = sem("c_ready")
        slots_made = sem("slots_made")
        slots_rounded = sem("slots_rounded")
        slots_left = sem("slots_left")
        h_made = sem("h_made")
        h_ready = sem("h_ready")
        h_rounded = sem("h_rounded")
        h_left = sem("h_left")
        e_made = sem("e_made")
        e_ready = sem("e_ready")
        c_made = sem("c_made")
        x_added = sem("x_added")

        block = ctx.enter_context(nc.Block())

        def over_units(engine, unit):
            unit(0, 0, 0, 1)
            with engine.Fori(1, G - 1) as g:
                unit(0, g, 0, g + 1)
            unit(0, G - 1, 1, 0)
            with engine.Fori(1, E - 1) as e:
                with engine.Fori(0, G - 1) as g:
                    unit(e, g, e, g + 1)
                unit(e, G - 1, e + 1, 0)
            with engine.Fori(0, G - 1) as g:
                unit(E - 1, g, E - 1, g + 1)
            unit(E - 1, G - 1, None, None)

        @block.sync
        def _(sp):
            sp.dma_start(b1[:], p["b1"]).then_inc(loaded, 16)
            sp.dma_start(b2[:].rearrange("p e d -> p (e d)"), p["b2"].partition_broadcast(P)).then_inc(loaded, 16)

            def load_expert(e):
                if later(e):
                    sp.wait_ge(l_made, G * e)
                sp.dma_start(snT_hi[:].bitcast(F32), scratch["snT_hi"][:, :, bass.ds(e * P, P)].bitcast(F32)).then_inc(sn_in, 16)
                sp.dma_start(snT_lo[:].bitcast(F32), scratch["snT_lo"][:, :, bass.ds(e * P, P)].bitcast(F32)).then_inc(sn_in, 16)

            def load_weights(e):
                if later(e):
                    sp.wait_ge(w1_split, e)
                    sp.wait_ge(w1_lost, e)
                sp.dma_start(w1_raw[:], p["w1"][e]).then_inc(w1_in, 16)
                if later(e):
                    sp.wait_ge(w2_split, e)
                    sp.wait_ge(w2_lost, e)
                sp.dma_start(w2_raw[:], p["w2"][e]).then_inc(w2_in, 16)

            def load_tokens(e, g):
                u = e * G + g
                if later(u):
                    sp.wait_ge(c_shifted, u)
                sp.dma_start(nmax[:].rearrange("p (b s) -> p b s", b=GB),
                             scratch["nmax"][bass.ds(g * GB, GB), :].partition_broadcast(P)).then_inc(nmax_in, 16)
                if later(u):
                    sp.wait_ge(slots_made, DC * u)
                sp.dma_start(xn[:], scratch["xn_units"][:, bass.ds(g * GB, GB), :]).then_inc(xn_in, 16)

            load_expert(0)
            load_tokens(0, 0)
            load_weights(0)

            def unit(e, g, e2, g2):
                if isinstance(g, int) and g == 0:
                    load_weights(e + 1)
                if isinstance(g2, int) and g2 == 0:
                    load_expert(e2)
                load_tokens(e2, g2)

            unit(0, 0, 0, 1)
            with sp.Fori(1, G - 1) as g:
                unit(0, g, 0, g + 1)
            unit(0, G - 1, 1, 0)
            with sp.Fori(1, E - 1) as e:
                load_weights(e + 1)
                with sp.Fori(0, G - 1) as g:
                    unit(e, g, e, g + 1)
                unit(e, G - 1, e + 1, 0)
            with sp.Fori(0, G - 1) as g:
                unit(E - 1, g, E - 1, g + 1)
            sp.wait_ge(loaded, 32)

        @block.tensor
        def _(pe):
            def logits(e, g):
                u = e * G + g
                pe.wait_ge(sn_in, 32 * (e + 1))
                if later(u):
                    pe.wait_ge(slots_left, DC * u)
                    pe.wait_ge(slots_rounded, DC * u)
                n = 0
                for c in range(DC):
                    for a, t in ((snT_hi, xnT_hi), (snT_lo, xnT_hi), (snT_hi, xnT_lo)):
                        mm = pe.matmul(p_l[:, 0:N], a[:, c, :], t[:, c, bass.ds(g * N, N)], start=n == 0, stop=n == 3 * DC - 1)
                        n += 1
                mm.then_inc(l_made, 1)

            def transpose_dispatch(e, g):
                u = e * G + g
                pe.wait_ge(d_ready, u + 1)
                pe.wait_ge(c_shifted, u + 1)
                for b in range(GB):
                    mm = pe.transpose(p_l[0:S, b * P:(b + 1) * P], dispatch[:, b, :], ident[:])
                mm.then_inc(dT_made, 1)

            def fill_slots(e, g, c):
                u = e * G + g
                if c == 0:
                    pe.wait_ge(dT_ready, u + 1)
                    pe.wait_ge(xn_in, 16 * (u + 1))
                    if later(u):
                        pe.wait_ge(slots_left, DC * (u - 1) + 1)
                to = p_x if c == 0 else p_l
                for b in range(GB):
                    mm = pe.matmul(to[:, b * P:(b + 1) * P], xn[:, b, c * P:(c + 1) * P], dispatchT[:, b, :],
                                   start=True, stop=True)
                mm.then_inc(slots_made, 1)

            def layer_1(e, g, m):
                u = e * G + g
                if m == 0:
                    pe.wait_ge(slots_left, DC * (u + 1))
                    pe.wait_ge(slots_rounded, DC * (u + 1))
                    pe.wait_ge(w1_split, e + 1)
                    pe.wait_ge(w1_lost, e + 1)
                if m >= 3:
                    pe.wait_ge(h_ready, HC * u + m - 2)
                elif later(u):
                    pe.wait_ge(h_ready, HC * (u - 1) + M3[m])
                cols = slice(m * P, (m + 1) * P)
                n = 0
                for c in range(DC):
                    for w, a in ((w1_hi, slots_hi), (w1_lo, slots_hi), (w1_hi, slots_lo)):
                        mm = pe.matmul(p_h[m % 3][:, 0:R], w[:, c, cols], a[:, c, :], start=n == 0, stop=n == 3 * DC - 1)
                        n += 1
                mm.then_inc(h_made, 1)

            def layer_2(e, g, b):
                u = e * G + g
                if b == 0:
                    pe.wait_ge(w2_split, e + 1)
                    pe.wait_ge(w2_lost, e + 1)
                if b >= 2:
                    pe.wait_ge(e_ready, GB * u + b - 1)
                elif later(u):
                    pe.wait_ge(e_ready, GB * u + b - 1)
                rows = slice(b * P, (b + 1) * P)
                for m in range(HC):
                    if b == 0:
                        pe.wait_ge(h_left, HC * u + m + 1)
                    for n, (a, w) in enumerate(((h_hi, w2_hi), (h_lo, w2_hi), (h_hi, w2_lo))):
                        mm = pe.matmul(p_e[b % 2][:, 0:D], a[:, m, rows], w[:, m, :], start=m == 0 and n == 0,
                                       stop=m == HC - 1 and n == 2)
                mm.then_inc(e_made, 1)

            def combine_batch(e, g, b):
                u = e * G + g
                pe.wait_ge(e_ready, GB * u + b + 1)
                if b == 0:
                    pe.wait_ge(c_ready, u + 1)
                if b > 0 or later(u):
                    pe.wait_ge(x_added, GB * u + b)
                pe.matmul(p_c[0:S, 0:D], combine[:, b, :], eo[:, b, :], start=True, stop=True).then_inc(c_made, 1)

            def unit(e, g, e2, g2):
                more = e2 is not None
                if more:
                    logits(e2, g2)
                for m in range(HC):
                    layer_1(e, g, m)
                if more:
                    transpose_dispatch(e2, g2)
                layer_2(e, g, 0)
                if more:
                    fill_slots(e2, g2, 0)
                layer_2(e, g, 1)
                combine_batch(e, g, 0)
                if more:
                    fill_slots(e2, g2, 1)
                layer_2(e, g, 2)
                combine_batch(e, g, 1)
                layer_2(e, g, 3)
                combine_batch(e, g, 2)
                combine_batch(e, g, 3)

            def first():
                logits(0, 0)
                transpose_dispatch(0, 0)
                fill_slots(0, 0, 0)
                fill_slots(0, 0, 1)

            first()
            over_units(pe, unit)

        @block.vector
        def _(dve):
            dve.wait_ge(loaded, 32)

            def shift(e, g):
                u = e * G + g
                dve.wait_ge(l_made, u + 1)
                rows = p_l[:, 0:N].rearrange("p (b s) -> p b s", b=GB)
                dve.tensor_reduce(over[:], rows, X, ALU.max).then_inc(over_ready, 1)
                dve.wait_ge(over_ready, u + 1)
                if later(u):
                    dve.wait_ge(dT_made, u)
                dve.tensor_tensor(dispatch[:], rows, over[:].unsqueeze(2).broadcast_to([P, GB, S]),
                                  ALU.subtract).then_inc(d_shifted, 1)
                dve.wait_ge(nmax_in, 16 * (u + 1))
                if later(u):
                    dve.wait_ge(c_ready, u)
                dve.tensor_tensor(lag_c[:], p_l[:, 0:N], nmax[:], ALU.add).then_inc(c_shifted, 1)

            def sum_dispatch(e, g):
                u = e * G + g
                dve.wait_ge(d_exp, u + 1)
                dve.tensor_reduce(dsum[:], dispatch[:], X, ALU.add).then_inc(dsum_ready, 1)
                dve.wait_ge(dsum_ready, 2 * u + 1)
                dve.reciprocal(dsum[:], dsum[:]).then_inc(dsum_ready, 1)
                dve.wait_ge(dsum_ready, 2 * u + 2)
                dve.tensor_tensor(dispatch[:], dispatch[:], dsum[:].unsqueeze(2).broadcast_to([P, GB, S]),
                                  ALU.mult).then_inc(d_ready, 1)

            def leave_slots(e, g, c):
                u = e * G + g
                dve.wait_ge(slots_rounded, DC * u + c + 1)
                frm = p_x if c == 0 else p_l
                dve.tensor_tensor(slots_lo[:, c, :], frm[:, 0:R], slots_hi[:, c, :].bitcast(F32),
                                  ALU.subtract).then_inc(slots_left, 1)

            def leave_h(e, g, m):
                u = e * G + g
                dve.wait_ge(h_rounded, HC * u + m + 1)
                dve.tensor_tensor(h_lo[:, m, :], h[:, m % 2, :], h_hi[:, m, :].bitcast(F32), ALU.subtract).then_inc(h_left, 1)

            def leave_w(e, raw, hi, lo, split, lost):
                dve.wait_ge(split, e + 1)
                dve.tensor_tensor(lo[:].rearrange("p a b -> p (a b)"), raw[:].rearrange("p a b -> p (a b)"),
                                  hi[:].rearrange("p a b -> p (a b)").bitcast(F32), ALU.subtract).then_inc(lost, 1)

            def add_bias(e, g, b):
                u = e * G + g
                dve.wait_ge(e_made, GB * u + b + 1)
                if later(u):
                    dve.wait_ge(c_made, GB * (u - 1) + b + 1)
                dve.tensor_tensor(eo[:, b, :], p_e[b % 2][:, 0:D], b2[:, bass.ds(e, 1), :].squeeze(1) if not isinstance(e, int) else b2[:, e, :],
                                  ALU.add).then_inc(e_ready, 1)

            def add_to_x(e, g, b):
                u = e * G + g
                dve.wait_ge(c_made, GB * u + b + 1)
                at = g * GB + b
                dve.scalar_tensor_tensor(out=x_all[:, at, :], in0=p_c[0:S, 0:D], scalar=inv_sum[:, bass.ds(at, 1)],
                                         in1=x_all[:, at, :], op0=ALU.mult, op1=ALU.add).then_inc(x_added, 1)

            def unit(e, g, e2, g2):
                more = e2 is not None
                if more:
                    shift(e2, g2)
                for m in range(HC):
                    leave_h(e, g, m)
                    if m == 2 and more:
                        sum_dispatch(e2, g2)
                if isinstance(g2, int) and g2 == 0:
                    leave_w(e2, w1_raw, w1_hi, w1_lo, w1_split, w1_lost)
                add_bias(e, g, 0)
                if more:
                    leave_slots(e2, g2, 0)
                add_bias(e, g, 1)
                add_to_x(e, g, 0)
                if more:
                    leave_slots(e2, g2, 1)
                add_bias(e, g, 2)
                add_to_x(e, g, 1)
                add_bias(e, g, 3)
                add_to_x(e, g, 2)
                add_to_x(e, g, 3)
                if isinstance(g2, int) and g2 == 0:
                    leave_w(e2, w2_raw, w2_hi, w2_lo, w2_split, w2_lost)

            def first():
                shift(0, 0)
                sum_dispatch(0, 0)
                leave_w(0, w1_raw, w1_hi, w1_lo, w1_split, w1_lost)
                leave_w(0, w2_raw, w2_hi, w2_lo, w2_split, w2_lost)
                leave_slots(0, 0, 0)
                leave_slots(0, 0, 1)

            first()
            over_units(dve, unit)

        @block.scalar
        def _(act):
            act.wait_ge(loaded, 32)

            def exp_dispatch(e, g):
                u = e * G + g
                act.wait_ge(d_shifted, u + 1)
                act.activation(dispatch[:], dispatch[:], ACT.Exp).then_inc(d_exp, 1)

            def copy_dispatch(e, g):
                u = e * G + g
                act.wait_ge(dT_made, u + 1)
                if later(u):
                    act.wait_ge(slots_made, DC * u)
                act.copy(dispatchT[:].rearrange("s b p -> s (b p)"), p_l[0:S, 0:R]).then_inc(dT_ready, 1)

            def exp_combine(e, g):
                u = e * G + g
                act.wait_ge(c_shifted, u + 1)
                if later(u):
                    act.wait_ge(c_made, GB * u)
                act.activation(combine[:].rearrange("p b s -> p (b s)"), lag_c[:], ACT.Exp).then_inc(c_ready, 1)

            def round_slots(e, g, c):
                u = e * G + g
                act.wait_ge(slots_made, DC * u + c + 1)
                if c == 0 and later(u):
                    act.wait_ge(h_made, HC * u)
                act.copy(slots_hi[:, c, :], (p_x if c == 0 else p_l)[:, 0:R]).then_inc(slots_rounded, 1)

            def gelu(e, g, m):
                u = e * G + g
                act.wait_ge(h_made, HC * u + m + 1)
                if m >= 2 or later(u):
                    act.wait_ge(h_left, HC * u + m - 1)
                act.activation(h[:, m % 2, :], p_h[m % 3][:, 0:R], ACT.Gelu, bias=b1[:, e, m:m + 1]).then_inc(h_ready, 1)
                act.wait_ge(h_ready, HC * u + m + 1)
                if m == 0 and later(u):
                    act.wait_ge(e_made, GB * u)
                act.copy(h_hi[:, m, :], h[:, m % 2, :]).then_inc(h_rounded, 1)

            def split_w(e, raw, hi, arrived, split):
                act.wait_ge(arrived, 16 * (e + 1))
                act.copy(hi[:].rearrange("p a b -> p (a b)"), raw[:].rearrange("p a b -> p (a b)")).then_inc(split, 1)

            def unit(e, g, e2, g2):
                more = e2 is not None
                exp_combine(e, g)
                if more:
                    exp_dispatch(e2, g2)
                for m in range(HC):
                    gelu(e, g, m)
                if more:
                    copy_dispatch(e2, g2)
                    if isinstance(g2, int) and g2 == 0:
                        split_w(e2, w1_raw, w1_hi, w1_in, w1_split)
                    round_slots(e2, g2, 0)
                    round_slots(e2, g2, 1)
                    if isinstance(g2, int) and g2 == 0:
                        act.wait_ge(e_made, GB * (e * G + g) + GB)
                        split_w(e2, w2_raw, w2_hi, w2_in, w2_split)

            def first():
                exp_dispatch(0, 0)
                copy_dispatch(0, 0)
                split_w(0, w1_raw, w1_hi, w1_in, w1_split)
                split_w(0, w2_raw, w2_hi, w2_in, w2_split)
                round_slots(0, 0, 0)
                round_slots(0, 0, 1)

            first()
            over_units(act, unit)


def decoder_layer(nc, x, wqkv, wo, cos, sin, causal, ident_f32, ident_bf16, ctx_t, shift_mask, xw_q, xw_k, xw_v, xw_o,
                  xb_q, xb_k, xb_v, xb_o, is_low, gamma, slot_gamma, slots, w1, w2, b1, b2, out):
    with ExitStack() as ctx:
        sb = lambda n, shape, dt=F32: ctx.enter_context(nc.sbuf_tensor(n, shape, dt))
        dram = lambda n, shape, dt=F32: nc.dram_tensor(n, shape, dt, kind="Internal").ap()
        x_all = sb("x_all", [S, B, D])
        mv = sb("mv", [S, B, 2])
        rstd = sb("rstd", [S, B])
        stats = sb("stats", [S, B, 6])
        ident = sb("ident", [P, P])
        ident16 = sb("ident16", [P, P], BF16)
        x_in = ctx.enter_context(nc.semaphore("x_in"))
        x_out = ctx.enter_context(nc.semaphore("x_out"))

        with nc.Block() as block:
            @block.sync
            def _(sp):
                sp.dma_start(x_all[:], x.rearrange("b s d -> s b d")).then_inc(x_in, 16)
                sp.dma_start(ident[:], ident_f32).then_inc(x_in, 16)
                sp.dma_start(ident16[:], ident_bf16).then_inc(x_in, 16)
                sp.wait_ge(x_in, 48)

        norm_statistics(nc, x_all, mv, rstd, stats, "ln1", True)
        self_attention(nc, x_all, mv, rstd, stats, ident, wqkv, wo, cos, sin, causal)
        norm_statistics(nc, x_all, mv, rstd, stats, "ln2", False)
        cross_attention(nc, x_all, mv, rstd, stats, ident, ident16, ctx_t,
                        dict(w_q=xw_q, w_k=xw_k, w_v=xw_v, w_o=xw_o, b_q=xb_q, b_k=xb_k, b_v=xb_v, b_o=xb_o,
                             is_low=is_low), shift_mask)
        norm_statistics(nc, x_all, mv, rstd, stats, "ln3", False)

        ffn = dict(gamma=gamma, slot_gamma=slot_gamma, slots=slots, w1=w1, w2=w2, b1=b1, b2=b2)
        xn = dram("xn_tokens", (B, S, D))
        scratch = dict(snT_hi=dram("sn_t_hi", (P, DC, E * P), F32R), snT_lo=dram("sn_t_lo", (P, DC, E * P), F32R),
                       xn=xn, xn_units=xn.rearrange("b s d -> s b d"), nmax=dram("token_nmax", (B, S)))
        xnT_hi = sb("xnT_hi", [P, DC, B * S], F32R)
        xnT_lo = sb("xnT_lo", [P, DC, B * S], F32R)
        inv_sum = sb("inv_sum", [S, B])
        route(nc, x_all, mv, rstd, ident, ffn, xnT_hi, xnT_lo, inv_sum, scratch)
        experts(nc, x_all, ident, ffn, xnT_hi, xnT_lo, inv_sum, scratch)

        with nc.Block() as block:
            @block.sync
            def _(sp):
                sp.dma_start(out.rearrange("b s d -> s b d"), x_all[:]).then_inc(x_out, 16)
                sp.wait_ge(x_out, 16)


def constants():
    inv_freq = (np.float32(10000.0) ** (-np.arange(DK // 2, dtype=np.float32) * np.float32(2.0) / DK)).astype(np.float32)
    angle = np.arange(S, dtype=np.float32)[:, None] * inv_freq[None, :]
    cos, sin = np.cos(angle).astype(np.float32), np.sin(angle).astype(np.float32)
    shift_mask = np.zeros((ROWS, 2 * DK, HP, S), np.float32)
    for hp in range(HP):
        shift_mask[:, [hp, HP + hp], hp] = 1.0
    return dict(
        cos=np.tile(np.repeat(cos, 2, axis=1), (1, 2 * H)),
        sin=np.tile(np.stack([-sin, sin], axis=-1).reshape(S, DK), (1, 2 * H)),
        causal=np.where(np.tril(np.ones((S, S), bool)), 0.0, -3e38).astype(np.float32),
        ident_f32=np.eye(P, dtype=np.float32),
        ident_bf16=np.eye(P).astype(mybir.dt.np(BF16)),
        is_low=np.tile(np.repeat(np.array([0.0, 1.0], np.float32), DK), HP).reshape(P, 1),
        shift_mask=shift_mask.reshape(P, HP, S))


def kernel(**inputs):
    import concourse.bacc as _bacc
    from concourse.bass_utils import run_bass_kernel_spmd as _run

    given = {name: np.asarray(a) for name, a in inputs.items()}
    attn = lambda n: given["L0_attn_" + n]
    xattn = lambda n: given["L0_xattn_" + n]
    ffn = lambda n: given["L0_ffn_" + n]
    rows = lambda w: w.reshape(DC, P, -1).transpose(1, 0, 2)

    twice = lambda a: np.repeat(a.reshape(-1, H, 1, DK), 2, axis=2).reshape(-1, 2 * D)
    context = np.zeros((B, P, DC, SCP), given["ctx_1024"].dtype)
    context[..., 0:SC] = given["ctx_1024"].transpose(0, 2, 1).reshape(B, DC, P, SC).transpose(0, 2, 1, 3)

    arrays = dict(
        x=given["x"],
        wqkv=rows(np.concatenate([attn("Wq").T, attn("Wk").T, attn("Wv").T], axis=1)),
        wo=rows(attn("Wo").T),
        ctx_t=context, xw_q=rows(twice(xattn("Wq"))), xw_k=rows(twice(xattn("Wk"))),
        xw_v=rows(xattn("Wv")), xw_o=rows(xattn("Wo")),
        xb_q=twice(xattn("bq")).reshape(-1, P).T, xb_k=twice(xattn("bk")).reshape(-1, P).T,
        xb_v=xattn("bv"), xb_o=xattn("bo"),
        gamma=ffn("norm_gamma"), slot_gamma=ffn("slot_norm_gamma"), slots=ffn("slot_embeds").transpose(1, 0, 2),
        w1=ffn("w1").reshape(E, DC, P, HID).transpose(0, 2, 1, 3),
        w2=ffn("w2").reshape(E, HC, P, D).transpose(0, 2, 1, 3),
        b1=ffn("b1").reshape(E, HC, P).transpose(2, 0, 1), b2=ffn("b2").reshape(-1),
        **constants())

    nc = _bacc.Bacc("TRN2", target_bir_lowering=False, num_devices=1)
    feeds, args = {}, {}
    for name, a in arrays.items():
        feeds[f"in_{name}_dram"] = a = np.ascontiguousarray(a)
        args[name] = nc.dram_tensor(f"in_{name}_dram", a.shape, mybir.dt.from_np(a.dtype), kind="ExternalInput").ap()
    out = nc.dram_tensor("out_0_dram", (B, S, D), F32, kind="ExternalOutput").ap()
    decoder_layer(nc, out=out, **args)
    return _run(nc, [feeds], core_ids=[0]).results[0]["out_0_dram"]
```

```python
from contextlib import ExitStack

import numpy as np

import concourse.bass as bass
from concourse import mybir

ALU = mybir.AluOpType
ACT = mybir.ActivationFunctionType
F32 = mybir.dt.float32
F32R = mybir.dt.float32r
BF16 = mybir.dt.bfloat16
X = mybir.AxisListType.X

B, S, D = 32, 100, 256
SC = 361
SCP = 362
H, DK = 16, 16
P = 128
DC = D // P
HP = P // (2 * DK)
NT = H // HP
KEYS = [121, 120, 120]
KEY0 = [0, 121, 241]
ER = 3
E, HID = 8, 1024
HC = HID // P
GB = 4
G = B // GB
M3 = [7, 8, 6]
EPS = 1e-5


class Stages:

    def __init__(self, engine, stages, count):
        lags = [lag for _, lag in stages]
        least, deepest = min(lags), max(lags)
        begin = deepest + 1 + (deepest + 1) % 2
        end = count + least - (count + least) % 2

        def step(i, turn):
            for stage, lag in stages:
                b = i - lag
                if not isinstance(b, int) or 0 <= b < count:
                    stage(b, (turn - lag) % 2)

        for i in range(least, begin):
            step(i, i)
        with engine.Fori(begin // 2, end // 2) as pair:
            step(2 * pair, 0)
            step(2 * pair + 1, 1)
        for i in range(end, count + deepest):
            step(i, i)


def later(b, n=1):
    return not isinstance(b, int) or b >= n


def norm_semaphores(nc, ctx):
    return {n: ctx.enter_context(nc.semaphore(f"ln_{n}")) for n in (
        "stats_done", "aggr_done", "eps_added", "root_done", "rstd_done")}


def norm_on_vector(dve, x_all, mv, rstd, stats, norms, use):
    for b in range(B):
        dve.bn_aggr(mv[:, b, :], stats[:, b, :]).then_inc(norms["aggr_done"], 1)
    dve.wait_ge(norms["aggr_done"], B * (use + 1))
    dve.tensor_scalar(rstd[:], mv[:, :, 1], EPS, None, ALU.add).then_inc(norms["eps_added"], 1)
    dve.wait_ge(norms["root_done"], use + 1)
    dve.reciprocal(rstd[:], rstd[:]).then_inc(norms["rstd_done"], 1)
    dve.wait_ge(norms["rstd_done"], use + 1)


def norm_on_scalar(act, rstd, norms, use):
    act.wait_ge(norms["eps_added"], use + 1)
    act.activation(rstd[:], rstd[:], ACT.Sqrt).then_inc(norms["root_done"], 1)


def self_attention(nc, x, x_all, mv, rstd, stats, norms, ident, ident16, ident_dram, ident16_dram, wqkv_dram, wo_dram, cos_dram, sin_dram, mask_dram,
                   maskT_dram, is_low_dram, shift_mask_dram):
    with ExitStack() as ctx:
        sb = lambda n, shape, dt=F32: ctx.enter_context(nc.sbuf_tensor(f"sa_{n}", shape, dt))
        pb = lambda n, shape, dt=F32: ctx.enter_context(nc.psum_tensor(f"sa_{n}", shape, dt))
        sem = lambda n: ctx.enter_context(nc.semaphore(f"sa_{n}"))
        V2 = 2 * DK

        w_qkv_raw = sb("w_qkv_raw", [P, DC, 3 * D])
        w_o_raw = sb("w_o_raw", [P, DC, D])
        w_qkv_hi = sb("w_qkv_hi", [P, DC, 3 * D], F32R)
        w_qkv_lo = sb("w_qkv_lo", [P, DC, 3 * D], F32R)
        w_o_hi = sb("w_o_hi", [P, DC, D], F32R)
        w_o_lo = sb("w_o_lo", [P, DC, D], F32R)
        XG = 4
        weights = ((w_qkv_raw, w_qkv_hi, w_qkv_lo), (w_o_raw, w_o_hi, w_o_lo))
        cos_t = sb("cos_t", [S, 2 * D])
        sin_t = sb("sin_t", [S, 2 * D])
        mask = sb("mask", [S, HP, S], BF16)
        maskT = sb("maskT", [S, HP, S], BF16)
        is_low = sb("is_low", [P, 1])
        shift_mask = sb("shift_mask", [P, HP, S])
        ones = sb("ones", [P, S], BF16)
        xn = sb("xn", [S, D])
        xnT_hi = sb("xnT_hi", [P, DC, S], F32R)
        xnT_lo = sb("xnT_lo", [P, DC, S], F32R)
        t_cos = sb("t_cos", [S, 2 * D])
        t_sin = sb("t_sin", [S, 2 * D])
        q_rot = sb("q_rot", [S, H, 2, DK])
        k_rot = sb("k_rot", [S, H, 2, DK])
        q_hi = sb("q_hi", [P, NT, S], F32R)
        q_lo = sb("q_lo", [P, NT, S], F32R)
        qm_hi = sb("qm_hi", [P, 2, NT, HP, S], F32R)
        qm_lo = sb("qm_lo", [P, 2, NT, HP, S], F32R)
        k_low = sb("k_low", [P, NT, S], F32R)
        kT = sb("kT", [P, 2, NT, S], F32R)
        v_aug = sb("v_aug", [S, 2, H, V2])
        nmax = sb("nmax", [S, NT, HP])
        nmax2 = sb("nmax2", [S, NT, V2], BF16)
        shift = sb("shift", [P, HP, S], BF16)
        eT = sb("eT", [S, NT, HP, S])
        o_raw = sb("o_raw", [P, NT, S])
        rsum = sb("rsum", [S, H])
        o = sb("o", [S, D])
        oT_hi = sb("oT_hi", [P, DC, S], F32R)
        oT_lo = sb("oT_lo", [P, DC, S], F32R)

        p_s = [pb(f"p_s{i}", [P, 512]) for i in range(2)]
        p_e = [pb(f"p_e{i}", [P, 512]) for i in range(2)]
        p_o = pb("p_o", [P, 512])
        p_qk = pb("p_qk", [P, 512])
        p_t = pb("p_t", [P, 512])
        p_x = pb("p_x", [P, 512])

        x_in = [sem(f"x_in{g}") for g in range(XG)]
        qkv_in = sem("qkv_in")
        loaded = sem("loaded")
        cleared = sem("cleared")
        w_rounded = sem("w_rounded")
        w_left = sem("w_left")
        xn_ready = sem("xn_ready")
        xnT_made = sem("xnT_made")
        xnT_rounded = sem("xnT_rounded")
        xnT_left = sem("xnT_left")
        qk_made = sem("qk_made")
        rot_terms = sem("rot_terms")
        q_rotated = sem("q_rotated")
        k_rotated = sem("k_rotated")
        qT_made = sem("qT_made")
        q_rounded = sem("q_rounded")
        q_left = sem("q_left")
        q_hi_placed = [sem("q_hi_placed0"), sem("q_hi_placed1")]
        q_lo_placed = [sem("q_lo_placed0"), sem("q_lo_placed1")]
        kT_made = sem("kT_made")
        k_rounded = sem("k_rounded")
        k_ready = sem("k_ready")
        v_made = sem("v_made")
        v_ready = sem("v_ready")
        s_made = sem("s_made")
        max_ready = sem("max_ready")
        max_split = sem("max_split")
        maxT_made = sem("maxT_made")
        shift_ready = sem("shift_ready")
        sT_made = sem("sT_made")
        e_ready = sem("e_ready")
        pv_made = sem("pv_made")
        o_raw_ready = sem("o_raw_ready")
        back_made = sem("back_made")
        divided = sem("divided")
        oT_made = sem("oT_made")
        oT_rounded = sem("oT_rounded")
        oT_left = sem("oT_left")
        out_made = sem("out_made")
        x_added = sem("x_added")

        block = ctx.enter_context(nc.Block())
        N_LOADS = 9
        N_CLEARED = 5

        def in_turn(b):
            return b // 2 + 1

        def at_most(b, n):
            return min(b + n, B) if isinstance(b, int) else b + n

        def term(t, which):
            heads = t[:, which * D:(which + 1) * D].rearrange("s (h d) -> s h d", h=H)
            return heads.unsqueeze(2).broadcast_to([S, H, 2, DK])

        @block.sync
        def _(sp):
            for g in range(XG):
                group = slice(g * B // XG, (g + 1) * B // XG)
                sp.dma_start(x_all[:, group, :], x[group].rearrange("b s d -> s b d")).then_inc(x_in[g], 16)
                if g == 0:
                    sp.dma_start(w_qkv_raw[:], wqkv_dram).then_inc(qkv_in, 16)
            for dst, src in ((ident, ident_dram), (ident16, ident16_dram), (w_o_raw, wo_dram), (cos_t, cos_dram), (sin_t, sin_dram),
                             (mask, mask_dram), (maskT, maskT_dram), (is_low, is_low_dram), (shift_mask, shift_mask_dram)):
                sp.dma_start(dst[:], src).then_inc(loaded, 16)
            sp.wait_ge(cleared, N_CLEARED)

            def place_q(b, slot):
                sp.wait_ge(q_rounded, b + 1)
                for a in range(HP):
                    rows = slice(32 * a, 32 * a + 32)
                    sp.dma_start(qm_hi[rows, slot, :, a, :].bitcast(F32), q_hi[rows].bitcast(F32)).then_inc(q_hi_placed[slot], 16)
                sp.wait_ge(q_left, b + 1)
                for a in range(HP):
                    rows = slice(32 * a, 32 * a + 32)
                    sp.dma_start(qm_lo[rows, slot, :, a, :].bitcast(F32), q_lo[rows].bitcast(F32)).then_inc(q_lo_placed[slot], 16)

            Stages(sp, [(place_q, 0)], B)

        @block.tensor
        def _(pe):
            def transpose_xn(b, slot):
                pe.wait_ge(xn_ready, b + 1)
                if later(b):
                    pe.wait_ge(k_ready, b)
                for c in range(DC):
                    mm = pe.transpose(p_x[:, c * S:(c + 1) * S], xn[:, c * P:(c + 1) * P], ident[0:S, 0:S])
                mm.then_inc(xnT_made, 1)

            def product(to, w, cols):
                n = 0
                for c in range(DC):
                    for a, x in ((xnT_hi, w[0]), (xnT_lo, w[0]), (xnT_hi, w[1])):
                        mm = pe.matmul(to, a[:, c, :], x[:, c, cols], start=n == 0, stop=n == 3 * DC - 1)
                        n += 1
                return mm

            def project_qk(b, slot):
                pe.wait_ge(xnT_rounded, b + 1)
                pe.wait_ge(xnT_left, b + 1)
                if later(b):
                    pe.wait_ge(v_ready, b)
                product(p_qk[0:S, 0:2 * D], (w_qkv_hi, w_qkv_lo), slice(0, 2 * D)).then_inc(qk_made, 1)

            def project_v(b, slot):
                pe.wait_ge(rot_terms, 3 * b + 3)
                product(p_qk[0:S, 0:D], (w_qkv_hi, w_qkv_lo), slice(2 * D, 3 * D)).then_inc(v_made, 1)

            def transpose_q(b, slot):
                pe.wait_ge(q_rotated, b + 1)
                if later(b, 3):
                    pe.wait_ge(x_added, b - 2)
                for t in range(NT):
                    mm = pe.transpose(p_t[:, t * S:(t + 1) * S],
                                      q_rot[:, HP * t:HP * t + HP].rearrange("s a r d -> s (a r d)"), ident[0:S, 0:S])
                mm.then_inc(qT_made, 1)

            def transpose_k(b, slot):
                pe.wait_ge(k_rotated, b + 1)
                for t in range(NT):
                    mm = pe.transpose(p_x[:, t * S:(t + 1) * S],
                                      k_rot[:, HP * t:HP * t + HP].rearrange("s a r d -> s (a r d)"), ident[0:S, 0:S])
                mm.then_inc(kT_made, 1)

            def transpose_max(b, slot):
                pe.wait_ge(max_split, 2 * b + 2)
                if later(b):
                    pe.wait_ge(o_raw_ready, b)
                pe.transpose(p_o[:, :].bitcast(BF16)[:, 0:S], nmax2[:].rearrange("s r f -> s (r f)"),
                             ident16[0:S, 0:S]).then_inc(maxT_made, 1)

            def scores(b, slot, t):
                if t == 0:
                    pe.wait_ge(q_hi_placed[slot], HP * 16 * in_turn(b))
                    pe.wait_ge(k_ready, b + 1)
                if t >= 2 or later(b):
                    pe.wait_ge(max_ready, NT * b + t - 1)
                pe.matmul(p_s[t % 2][0:S, 0:HP * S], ident16[0:S, 0:S], mask[:].rearrange("q a k -> q (a k)"),
                          start=True, stop=False, skip_group_check=True)
                for a in range(HP):
                    mm = pe.matmul(p_s[t % 2][0:S, a * S:(a + 1) * S], qm_hi[:, slot, t, a, :], kT[:, slot, t, :],
                                   start=False, stop=True, skip_group_check=True)
                mm.then_inc(s_made, 1)

            def scores_t(b, slot, t):
                if t == 0:
                    pe.wait_ge(shift_ready, b + 1)
                    pe.wait_ge(q_lo_placed[slot], HP * 16 * in_turn(b))
                if t >= 2 or later(b):
                    pe.wait_ge(e_ready, NT * b + t - 1)
                rows = slice(32 * t, 32 * t + 32)
                to = p_e[t % 2][0:S, 0:HP * S]
                pe.matmul(to, ident16[0:S, 0:S], maskT[:].rearrange("k a q -> k (a q)"), start=True, stop=False)
                pe.matmul(to, ones[rows, :], shift[rows].rearrange("h r q -> h (r q)"), start=False, stop=False)
                for q in (qm_hi, qm_lo):
                    mm = pe.matmul(to, kT[:, slot, t, :], q[:, slot, t].rearrange("p a s -> p (a s)"),
                                   start=False, stop=q is qm_lo)
                mm.then_inc(sT_made, 1)

            def weigh_values(b, slot, t):
                pe.wait_ge(e_ready, NT * b + t + 1)
                if t == 0:
                    pe.wait_ge(v_ready, b + 1)
                    pe.wait_ge(shift_ready, b + 1)
                for a in range(HP):
                    mm = pe.matmul(p_o[32 * a:32 * a + 32, t * S:(t + 1) * S], v_aug[:, slot, HP * t + a, :],
                                   eT[:, t, a, :], start=True, stop=True)
                mm.then_inc(pv_made, 1)

            def transpose_back(b, slot):
                pe.wait_ge(o_raw_ready, b + 1)
                pe.wait_ge(q_left, at_most(b, 3))
                if later(b):
                    pe.wait_ge(x_added, b)
                for t in range(NT):
                    mm = pe.transpose(p_t[0:S, t * P:(t + 1) * P], o_raw[:, t, :], ident[:])
                mm.then_inc(back_made, 1)

            def transpose_o(b, slot):
                pe.wait_ge(divided, 2 * b + 2)
                for c in range(DC):
                    mm = pe.transpose(p_t[:, c * S:(c + 1) * S], o[:, c * P:(c + 1) * P], ident[0:S, 0:S])
                mm.then_inc(oT_made, 1)

            def project_out(b, slot):
                pe.wait_ge(oT_rounded, b + 1)
                pe.wait_ge(oT_left, b + 1)
                n = 0
                for c in range(DC):
                    for a, x in ((oT_hi, w_o_hi), (oT_lo, w_o_hi), (oT_hi, w_o_lo)):
                        mm = pe.matmul(p_t[0:S, 0:D], a[:, c, :], x[:, c, :], start=n == 0, stop=n == 3 * DC - 1)
                        n += 1
                mm.then_inc(out_made, 1)

            pe.wait_ge(w_left, len(weights))
            pe.wait_ge(cleared, N_CLEARED)
            pe.wait_ge(loaded, 16 * N_LOADS)
            part = lambda f, *a: (lambda b, slot: f(b, slot, *a))
            st = lambda t: (part(scores_t, t), 1)
            pv = lambda t: (part(weigh_values, t), 1)
            mx = lambda t: (part(scores, t), 0)
            Stages(pe, [
                (project_v, 0), (transpose_q, 0), (transpose_max, 1), (transpose_k, 0), st(0), (transpose_back, 2),
                (transpose_xn, -1), st(1), pv(0), (transpose_o, 2), (project_qk, -1), st(2), pv(1),
                (project_out, 2), mx(0), mx(1), st(3), pv(2), mx(2), mx(3), pv(3),
            ], B)

        @block.vector
        def _(dve):
            dve.memset(v_aug[:], 1.0).then_inc(cleared, 1)
            dve.memset(nmax2[:], 0.0).then_inc(cleared, 1)
            dve.memset(ones[:], 1.0).then_inc(cleared, 1)
            for b in range(B):
                if b % (B // XG) == 0:
                    dve.wait_ge(x_in[b * XG // B], 16)
                dve.bn_stats(stats[:, b, :], x_all[:, b, :]).then_inc(norms["stats_done"], 1)
            dve.wait_ge(norms["stats_done"], B)
            norm_on_vector(dve, x_all, mv, rstd, stats, norms, 0)
            for i, (raw, hi, lo) in enumerate(weights):
                dve.wait_ge(w_rounded, i + 1)
                dve.tensor_tensor(lo[:], raw[:], hi[:].bitcast(F32), ALU.subtract).then_inc(w_left, 1)
            dve.wait_ge(cleared, N_CLEARED)
            dve.wait_ge(loaded, 16 * N_LOADS)

            def normalise(b, slot):
                if later(b):
                    dve.wait_ge(xnT_made, b)
                dve.tensor_scalar(xn[:], x_all[:, b, :], mv[:, b, 0:1], rstd[:, bass.ds(b, 1)],
                                  ALU.subtract, ALU.mult).then_inc(xn_ready, 1)

            def leave_xnT(b, slot):
                dve.wait_ge(xnT_rounded, b + 1)
                if later(b):
                    dve.wait_ge(v_made, b)
                dve.tensor_tensor(xnT_lo[:].rearrange("p c s -> p (c s)"), p_x[:, 0:DC * S],
                                  xnT_hi[:].rearrange("p c s -> p (c s)").bitcast(F32), ALU.subtract).then_inc(xnT_left, 1)

            def rotate(b, slot):
                dve.wait_ge(qk_made, b + 1)
                if later(b):
                    dve.wait_ge(q_rotated, b)
                    dve.wait_ge(k_rotated, b)
                dve.tensor_tensor(t_cos[:], p_qk[0:S, :], cos_t[:], ALU.mult).then_inc(rot_terms, 1)
                dve.tensor_tensor(t_sin[:, 0::2], p_qk[0:S, 1::2], sin_t[:, 0::2], ALU.mult).then_inc(rot_terms, 1)
                dve.tensor_tensor(t_sin[:, 1::2], p_qk[0:S, 0::2], sin_t[:, 1::2], ALU.mult).then_inc(rot_terms, 1)

            def sum_q(b, slot):
                dve.wait_ge(rot_terms, 3 * b + 3)
                if later(b):
                    dve.wait_ge(qT_made, b)
                dve.tensor_tensor(q_rot[:], term(t_cos, 0), term(t_sin, 0), ALU.add).then_inc(q_rotated, 1)

            def leave_q(b, slot):
                dve.wait_ge(q_rounded, b + 1)
                if later(b):
                    dve.wait_ge(q_lo_placed[1 - slot], HP * 16 * in_turn(b - 1))
                dve.scalar_tensor_tensor(out=q_lo[:].rearrange("p t s -> p (t s)"), in0=p_t[:, 0:NT * S], scalar=DK ** -0.5,
                                         in1=q_hi[:].rearrange("p t s -> p (t s)").bitcast(F32), op0=ALU.mult,
                                         op1=ALU.subtract).then_inc(q_left, 1)

            def stack_k(b, slot):
                dve.wait_ge(k_rounded, b + 1)
                if later(b, 2):
                    dve.wait_ge(sT_made, NT * (b - 1))
                dve.tensor_tensor(kT[:, slot].rearrange("p t s -> p (t s)"), p_x[:, 0:NT * S],
                                  k_low[:].rearrange("p t s -> p (t s)").bitcast(F32), ALU.subtract).then_inc(k_ready, 1)

            def find_max(b, slot, t):
                dve.wait_ge(s_made, NT * b + t + 1)
                if t == 0 and later(b):
                    dve.wait_ge(max_split, 2 * b)
                dve.tensor_reduce(nmax[:, t, :], p_s[t % 2][0:S, 0:HP * S].rearrange("q (a k) -> q a k", a=HP), X, ALU.max,
                                  negate=True).then_inc(max_ready, 1)

            def split_max(b, slot):
                dve.wait_ge(max_ready, NT * (b + 1))
                if later(b):
                    dve.wait_ge(maxT_made, b)
                high, low = nmax2[:, :, 0:HP], nmax2[:, :, HP:2 * HP]
                dve.tensor_copy(high, nmax[:]).then_inc(max_split, 1)
                dve.wait_ge(max_split, 2 * b + 1)
                dve.tensor_tensor(low, nmax[:], high, ALU.subtract).then_inc(max_split, 1)

            def make_shift(b, slot):
                dve.wait_ge(maxT_made, b + 1)
                if later(b):
                    dve.wait_ge(sT_made, NT * b)
                dve.tensor_tensor(shift[:], p_o[:, :].bitcast(BF16)[:, 0:S].unsqueeze(1).broadcast_to([P, HP, S]),
                                  shift_mask[:], ALU.mult).then_inc(shift_ready, 1)

            def divide(b, slot):
                dve.wait_ge(back_made, b + 1)
                if later(b):
                    dve.wait_ge(oT_made, b)
                    dve.wait_ge(divided, 2 * b)
                pv = p_t[0:S, 0:H * V2].rearrange("q (h d) -> q h d", h=H)
                dve.reciprocal(rsum[:], pv[:, :, DK]).then_inc(divided, 1)
                dve.wait_ge(divided, 2 * b + 1)
                dve.tensor_tensor(o[:].rearrange("q (h d) -> q h d", h=H), pv[:, :, 0:DK],
                                  rsum[:].unsqueeze(2).broadcast_to([S, H, DK]), ALU.mult).then_inc(divided, 1)

            def leave_oT(b, slot):
                dve.wait_ge(oT_rounded, b + 1)
                if later(b):
                    dve.wait_ge(out_made, b)
                dve.tensor_tensor(oT_lo[:].rearrange("p c s -> p (c s)"), p_t[:, 0:DC * S],
                                  oT_hi[:].rearrange("p c s -> p (c s)").bitcast(F32), ALU.subtract).then_inc(oT_left, 1)

            def add_to_x(b, slot):
                dve.wait_ge(out_made, b + 1)
                dve.tensor_tensor(x_all[:, b, :], p_t[0:S, 0:D], x_all[:, b, :], ALU.add).then_inc(x_added, 1)

            def keep_stats(b, slot):
                dve.wait_ge(x_added, b + 1)
                dve.bn_stats(stats[:, b, :], x_all[:, b, :])

            part = lambda f, *a: (lambda b, slot: f(b, slot, *a))
            mx = lambda t: (part(find_max, t), 0)
            Stages(dve, [
                (make_shift, 1), (leave_q, 0), (stack_k, 0), (divide, 2), (leave_xnT, -1), (normalise, -2),
                (leave_oT, 2), (rotate, -1), (sum_q, -1), (add_to_x, 2), mx(0), mx(1), mx(2), mx(3),
                (split_max, 0), (keep_stats, 2),
            ], B)

        @block.scalar
        def _(act):
            act.wait_ge(qkv_in, 16)
            act.copy(w_qkv_hi[:], w_qkv_raw[:]).then_inc(w_rounded, 1)
            act.wait_ge(loaded, 16 * N_LOADS)
            act.copy(w_o_hi[:], w_o_raw[:]).then_inc(w_rounded, 1)
            norm_on_scalar(act, rstd, norms, 0)
            act.wait_ge(cleared, N_CLEARED)

            def round_xnT(b, slot):
                act.wait_ge(xnT_made, b + 1)
                if later(b):
                    act.wait_ge(v_made, b)
                act.copy(xnT_hi[:].rearrange("p c s -> p (c s)"), p_x[:, 0:DC * S]).then_inc(xnT_rounded, 1)

            def round_q(b, slot):
                act.wait_ge(qT_made, b + 1)
                if later(b):
                    act.wait_ge(q_hi_placed[1 - slot], HP * 16 * in_turn(b - 1))
                act.activation(q_hi[:].rearrange("p t s -> p (t s)"), p_t[:, 0:NT * S], ACT.Copy,
                               scale=DK ** -0.5).then_inc(q_rounded, 1)

            def round_k(b, slot):
                act.wait_ge(kT_made, b + 1)
                if later(b):
                    act.wait_ge(k_ready, b)
                act.activation(k_low[:].rearrange("p t s -> p (t s)"), p_x[:, 0:NT * S], ACT.Copy,
                               scale=is_low[:, 0:1]).then_inc(k_rounded, 1)

            def copy_v(b, slot):
                act.wait_ge(v_made, b + 1)
                if later(b, 2):
                    act.wait_ge(pv_made, NT * (b - 1))
                act.copy(v_aug[:, slot, :, 0:DK], p_qk[0:S, 0:D].rearrange("k (h d) -> k h d", h=H)).then_inc(v_ready, 1)

            def exponentiate(b, slot, t):
                act.wait_ge(sT_made, NT * b + t + 1)
                if later(b):
                    act.wait_ge(pv_made, NT * (b - 1) + t + 1)
                act.activation(eT[:, t].rearrange("k a q -> k (a q)"), p_e[t % 2][0:S, 0:HP * S], ACT.Exp).then_inc(e_ready, 1)

            def copy_o_raw(b, slot):
                act.wait_ge(pv_made, NT * (b + 1))
                if later(b):
                    act.wait_ge(back_made, b)
                act.copy(o_raw[:].rearrange("p t s -> p (t s)"), p_o[:, 0:NT * S]).then_inc(o_raw_ready, 1)

            def round_oT(b, slot):
                act.wait_ge(oT_made, b + 1)
                if later(b):
                    act.wait_ge(out_made, b)
                act.copy(oT_hi[:].rearrange("p c s -> p (c s)"), p_t[:, 0:DC * S]).then_inc(oT_rounded, 1)

            part = lambda f, *a: (lambda b, slot: f(b, slot, *a))
            ex = lambda t: (part(exponentiate, t), 1)
            Stages(act, [
                (copy_v, 0), (round_q, 0), (round_k, 0), ex(0), (round_xnT, -1), ex(1), (round_oT, 2), ex(2),
                ex(3), (copy_o_raw, 1),
            ], B)

        @block.gpsimd
        def _(pool):
            pool.memset(qm_hi[:].bitcast(F32), 0.0).then_inc(cleared, 1)
            pool.memset(qm_lo[:].bitcast(F32), 0.0).then_inc(cleared, 1)

            def sum_k(b, slot):
                pool.wait_ge(rot_terms, 3 * b + 3)
                if later(b):
                    pool.wait_ge(kT_made, b)
                pool.tensor_tensor(k_rot[:], term(t_cos, 1), term(t_sin, 1), ALU.add).then_inc(k_rotated, 1)

            Stages(pool, [(sum_k, -1)], B)


def cross_attention(nc, x_all, mv, rstd, stats, norms, ident, ident16, ctx_dram, w, shift_mask_dram):
    with ExitStack() as ctx:
        sb = lambda n, shape, dt=F32: ctx.enter_context(nc.sbuf_tensor(f"xa_{n}", shape, dt))
        pb = lambda n, shape, dt=F32: ctx.enter_context(nc.psum_tensor(f"xa_{n}", shape, dt))
        sem = lambda n: ctx.enter_context(nc.semaphore(f"xa_{n}"))
        NK = len(KEYS)
        UNITS = NT * NK
        V2 = 2 * DK

        names = ("w_q", "w_k", "w_v", "w_o")
        widths = dict(w_q=D, w_k=NT * P, w_v=D, w_o=D)
        raw = {n: sb(f"{n}_raw", [P, DC, widths[n]]) for n in names}
        w_hi = {n: sb(f"{n}_hi", [P, DC, widths[n]], F32R) for n in names}
        w_lo = {n: sb(f"{n}_lo", [P, DC, widths[n]], F32R) for n in names}
        b_q = sb("b_q", [S, D])
        b_k = sb("b_k", [P, NT])
        b_v = sb("b_v", [S, D])
        b_o = sb("b_o", [S, D])
        is_low = sb("is_low", [P, 1])
        low_b_k = sb("low_b_k", [P, NT])
        shift_mask = sb("shift_mask", [P, HP, S])
        ones = sb("ones", [P, KEYS[0]], BF16)
        context = sb("context", [P, 2, DC, SCP])
        ctx_hi = sb("ctx_hi", [P, DC, SCP], F32R)
        ctx_lo = sb("ctx_lo", [P, DC, SCP], F32R)
        xn = sb("xn", [S, D])
        xnT_hi = sb("xnT_hi", [P, DC, S], F32R)
        xnT_lo = sb("xnT_lo", [P, DC, S], F32R)
        q_full = sb("q_full", [S, H, 2, DK])
        q_hi = sb("q_hi", [P, NT, S], F32R)
        q_lo = sb("q_lo", [P, NT, S], F32R)
        qm_hi = sb("qm_hi", [P, 2, NT, HP, S], F32R)
        qm_lo = sb("qm_lo", [P, 2, NT, HP, S], F32R)
        k_low = sb("k_low", [P, 2, SCP], F32R)
        kT = sb("kT", [P, 2, NT, SCP], F32R)
        v_aug = sb("v_aug", [KEYS[0], 2, NK, H, V2])
        nmax = sb("nmax", [S, NT, HP])
        nmax2 = sb("nmax2", [S, NT, V2], BF16)
        shift = sb("shift", [P, HP, S], BF16)
        eT = sb("eT", [KEYS[0], ER, HP, S])
        o_raw = sb("o_raw", [P, NT, S])
        rsum = sb("rsum", [S, H])
        o = sb("o", [S, D])
        oT_hi = sb("oT_hi", [P, DC, S], F32R)
        oT_lo = sb("oT_lo", [P, DC, S], F32R)

        p_s = [pb(f"p_s{i}", [P, 512]) for i in range(2)]
        p_e = [pb(f"p_e{i}", [P, 512]) for i in range(2)]
        p_o = pb("p_o", [P, 512])
        p_k = [pb(f"p_k{i}", [P, 512]) for i in range(2)]
        p_x = pb("p_x", [P, 512])

        loaded = sem("loaded")
        cleared = sem("cleared")
        raw_in = sem("raw_in")
        w_rounded = sem("w_rounded")
        w_left = sem("w_left")
        biases = sem("biases")
        context_in = [sem("context_in0"), sem("context_in1")]
        ctx_rounded = sem("ctx_rounded")
        ctx_left = sem("ctx_left")
        xn_ready = sem("xn_ready")
        xnT_made = sem("xnT_made")
        xnT_rounded = sem("xnT_rounded")
        xnT_left = sem("xnT_left")
        q_made = sem("q_made")
        q_ready = sem("q_ready")
        qT_made = sem("qT_made")
        q_rounded = sem("q_rounded")
        q_left = sem("q_left")
        q_hi_placed = [sem("q_hi_placed0"), sem("q_hi_placed1")]
        q_lo_placed = [sem("q_lo_placed0"), sem("q_lo_placed1")]
        k_made = sem("k_made")
        k_rounded = sem("k_rounded")
        k_ready = sem("k_ready")
        v_made = sem("v_made")
        v_ready = sem("v_ready")
        s_made = sem("s_made")
        max_ready = sem("max_ready")
        max_split = sem("max_split")
        maxT_made = sem("maxT_made")
        shift_ready = sem("shift_ready")
        sT_made = sem("sT_made")
        e_ready = sem("e_ready")
        pv_unit = sem("pv_unit")
        o_raw_ready = sem("o_raw_ready")
        back_made = sem("back_made")
        divided = sem("divided")
        oT_made = sem("oT_made")
        oT_rounded = sem("oT_rounded")
        oT_left = sem("oT_left")
        out_made = sem("out_made")
        x_added = sem("x_added")
        bo_added = sem("bo_added")

        block = ctx.enter_context(nc.Block())
        N_LOADS = 6
        N_CLEARED = 5

        def in_turn(b):
            return b // 2 + 1

        def at_most(b, n):
            return min(b + n, B) if isinstance(b, int) else b + n

        @block.sync
        def _(sp):
            for n in names:
                sp.dma_start(raw[n][:], w[n]).then_inc(raw_in, 16)
            for dst, src in ((b_k, w["b_k"]), (is_low, w["is_low"]), (shift_mask, shift_mask_dram)):
                sp.dma_start(dst[:], src).then_inc(loaded, 16)
            for dst, src in ((b_q, w["b_q"]), (b_v, w["b_v"]), (b_o, w["b_o"])):
                sp.dma_start(dst[:], src.partition_broadcast(S)).then_inc(loaded, 16)

            def load_context(b, slot):
                if later(b, 2):
                    sp.wait_ge(ctx_left, b - 1)
                    sp.wait_ge(ctx_rounded, b - 1)
                sp.dma_start(context[:, slot], ctx_dram[b]).then_inc(context_in[slot], 16)

            def place_q(b, slot):
                if later(b, 2):
                    sp.wait_ge(sT_made, UNITS * (b - 1))
                if isinstance(b, int) and b < 2:
                    sp.wait_ge(cleared, N_CLEARED)
                sp.wait_ge(q_rounded, b + 1)
                for a in range(HP):
                    rows = slice(32 * a, 32 * a + 32)
                    sp.dma_start(qm_hi[rows, slot, :, a, :].bitcast(F32), q_hi[rows].bitcast(F32)).then_inc(q_hi_placed[slot], 16)
                sp.wait_ge(q_left, b + 1)
                for a in range(HP):
                    rows = slice(32 * a, 32 * a + 32)
                    sp.dma_start(qm_lo[rows, slot, :, a, :].bitcast(F32), q_lo[rows].bitcast(F32)).then_inc(q_lo_placed[slot], 16)

            Stages(sp, [(load_context, -2), (place_q, -1)], B)

        @block.tensor
        def _(pe):
            def transpose_xn(b, slot):
                pe.wait_ge(xn_ready, b + 1)
                if later(b):
                    pe.wait_ge(q_left, b)
                if later(b, 2):
                    pe.wait_ge(shift_ready, b - 1)
                if later(b, 3):
                    pe.wait_ge(x_added, b - 2)
                for c in range(DC):
                    mm = pe.transpose(p_x[:, c * S:(c + 1) * S], xn[:, c * P:(c + 1) * P], ident[0:S, 0:S])
                mm.then_inc(xnT_made, 1)

            def project_q(b, slot):
                pe.wait_ge(xnT_rounded, b + 1)
                pe.wait_ge(xnT_left, b + 1)
                n = 0
                for c in range(DC):
                    for a, x in ((xnT_hi, w_hi["w_q"]), (xnT_lo, w_hi["w_q"]), (xnT_hi, w_lo["w_q"])):
                        mm = pe.matmul(p_x[0:S, 0:D], a[:, c, :], x[:, c, :], start=n == 0, stop=n == 3 * DC - 1)
                        n += 1
                mm.then_inc(q_made, 1)

            def transpose_q(b, slot):
                pe.wait_ge(q_ready, b + 1)
                for t in range(NT):
                    mm = pe.transpose(p_x[:, t * S:(t + 1) * S],
                                      q_full[:, HP * t:HP * t + HP].rearrange("s a r d -> s (a r d)"), ident[0:S, 0:S])
                mm.then_inc(qT_made, 1)

            def transpose_max(b, slot):
                pe.wait_ge(max_split, 2 * b + 2)
                pe.wait_ge(q_left, at_most(b, 2))
                if later(b, 2):
                    pe.wait_ge(x_added, b - 1)
                pe.transpose(p_x[:, :].bitcast(BF16)[:, 0:S], nmax2[:].rearrange("s r f -> s (r f)"),
                             ident16[0:S, 0:S]).then_inc(maxT_made, 1)

            def project_k(b, slot, t):
                if t == 0:
                    pe.wait_ge(ctx_rounded, b + 1)
                    pe.wait_ge(ctx_left, b + 1)
                if t >= 2:
                    pe.wait_ge(k_ready, NT * b + t - 1)
                elif later(b):
                    pe.wait_ge(v_ready, NK * b - 1 + t)
                cols = slice(t * P, (t + 1) * P)
                n = 0
                for d in range(DC):
                    for a, x in ((w_hi["w_k"], ctx_hi), (w_lo["w_k"], ctx_hi), (w_hi["w_k"], ctx_lo)):
                        mm = pe.matmul(p_k[(slot + t) % 2][:, 0:SCP], a[:, d, cols], x[:, d, :],
                                       start=n == 0, stop=n == 3 * DC - 1)
                        n += 1
                mm.then_inc(k_made, 1)

            def project_v(b, slot, j):
                if j < 2:
                    pe.wait_ge(k_ready, NT * b + NT - 1 + j)
                else:
                    pe.wait_ge(v_ready, NK * b + 1)
                keys = slice(KEY0[j], KEY0[j] + KEYS[j])
                n = 0
                for d in range(DC):
                    for a, x in ((ctx_hi, w_hi["w_v"]), (ctx_lo, w_hi["w_v"]), (ctx_hi, w_lo["w_v"])):
                        mm = pe.matmul(p_k[(slot + NT + j) % 2][0:KEYS[j], 0:D], a[:, d, keys], x[:, d, :],
                                       start=n == 0, stop=n == 3 * DC - 1)
                        n += 1
                mm.then_inc(v_made, 1)

            def scores(b, slot, h):
                if h == 0:
                    pe.wait_ge(q_hi_placed[slot], HP * 16 * in_turn(b))
                if h % HP == 0:
                    pe.wait_ge(k_ready, NT * b + h // HP + 1)
                if h >= 2:
                    pe.wait_ge(max_ready, H * b + h - 1)
                elif later(b):
                    pe.wait_ge(max_ready, H * b + h - 1)
                t, a = divmod(h, HP)
                pe.matmul(p_s[h % 2][0:S, 0:SCP], qm_hi[:, slot, t, a, :], kT[:, slot, t, :],
                          start=True, stop=True).then_inc(s_made, 1)

            def scores_t(b, slot, u):
                t, n = divmod(u, NK)
                if u == 0:
                    pe.wait_ge(shift_ready, b + 1)
                    pe.wait_ge(q_lo_placed[slot], HP * 16 * in_turn(b))
                if u >= 2 or later(b):
                    pe.wait_ge(e_ready, UNITS * b + u - 1)
                keys = slice(KEY0[n], KEY0[n] + KEYS[n])
                rows = slice(32 * t, 32 * t + 32)
                to = p_e[u % 2][0:KEYS[n], 0:HP * S]
                pe.matmul(to, ones[rows, 0:KEYS[n]], shift[rows].rearrange("h r q -> h (r q)"), start=True, stop=False)
                for q in (qm_hi, qm_lo):
                    mm = pe.matmul(to, kT[:, slot, t, keys], q[:, slot, t].rearrange("p a s -> p (a s)"),
                                   start=False, stop=q is qm_lo)
                mm.then_inc(sT_made, 1)

            def weigh_values(b, slot, u):
                t, n = divmod(u, NK)
                pe.wait_ge(e_ready, UNITS * b + u + 1)
                if u == 0:
                    pe.wait_ge(v_ready, NK * (b + 1))
                    if later(b):
                        pe.wait_ge(o_raw_ready, b)
                for a in range(HP):
                    mm = pe.matmul(p_o[32 * a:32 * a + 32, t * S:(t + 1) * S], v_aug[0:KEYS[n], slot, n, HP * t + a, :],
                                   eT[0:KEYS[n], u % ER, a, :], start=u == 0, stop=n == NK - 1, skip_group_check=True)
                mm.then_inc(pv_unit, 1)

            def transpose_back(b, slot):
                pe.wait_ge(o_raw_ready, b + 1)
                pe.wait_ge(shift_ready, at_most(b, 2))
                if later(b):
                    pe.wait_ge(x_added, b)
                for t in range(NT):
                    mm = pe.transpose(p_x[0:S, t * P:(t + 1) * P], o_raw[:, t, :], ident[:])
                mm.then_inc(back_made, 1)

            def transpose_o(b, slot):
                pe.wait_ge(divided, 3 * b + 3)
                for c in range(DC):
                    mm = pe.transpose(p_x[:, c * S:(c + 1) * S], o[:, c * P:(c + 1) * P], ident[0:S, 0:S])
                mm.then_inc(oT_made, 1)

            def project_out(b, slot):
                pe.wait_ge(oT_rounded, b + 1)
                pe.wait_ge(oT_left, b + 1)
                n = 0
                for c in range(DC):
                    for a, x in ((oT_hi, w_hi["w_o"]), (oT_lo, w_hi["w_o"]), (oT_hi, w_lo["w_o"])):
                        mm = pe.matmul(p_x[0:S, 0:D], a[:, c, :], x[:, c, :], start=n == 0, stop=n == 3 * DC - 1)
                        n += 1
                mm.then_inc(out_made, 1)

            pe.wait_ge(w_left, len(names))
            pe.wait_ge(cleared, N_CLEARED)
            part = lambda f, *a: (lambda b, slot: f(b, slot, *a))
            st = lambda u: (part(scores_t, u), 1)
            pv = lambda u: (part(weigh_values, u), 1)
            mx = lambda h: (part(scores, h), 0)
            k = lambda t: (part(project_k, t), 0)
            v = lambda j: (part(project_v, j), 0)
            Stages(pe, [
                k(0), (transpose_max, 1), (part(weigh_values, UNITS - 1), 2), k(1), st(0), k(2), st(1), pv(0),
                (transpose_back, 2), mx(0), k(3), mx(1), st(2), pv(1), mx(2), v(0), mx(3), st(3), pv(2), mx(4),
                mx(5), (transpose_o, 2), v(1), mx(6), st(4), pv(3), mx(7), mx(8), st(5), pv(4), v(2), mx(9),
                (project_out, 2), st(6), pv(5), mx(10), (transpose_xn, -1), st(7), pv(6), mx(11), st(8),
                (project_q, -1), pv(7), mx(12), st(9), (transpose_q, -1), pv(8), mx(13), mx(14), st(10), pv(9),
                st(11), mx(15), pv(10),
            ], B)

        @block.vector
        def _(dve):
            norm_on_vector(dve, x_all, mv, rstd, stats, norms, 1)
            dve.memset(v_aug[:], 1.0).then_inc(cleared, 1)
            dve.memset(nmax2[:], 0.0).then_inc(cleared, 1)
            dve.memset(ones[:], 1.0).then_inc(cleared, 1)
            for i, n in enumerate(names):
                dve.wait_ge(w_rounded, i + 1)
                dve.tensor_tensor(w_lo[n][:], raw[n][:], w_hi[n][:].bitcast(F32), ALU.subtract).then_inc(w_left, 1)
            dve.wait_ge(cleared, N_CLEARED)
            dve.wait_ge(loaded, 16 * N_LOADS)
            dve.tensor_scalar(low_b_k[:], b_k[:], is_low[:, 0:1], None, ALU.mult).then_inc(biases, 1)
            dve.wait_ge(biases, 1)

            def normalise(b, slot):
                if later(b):
                    dve.wait_ge(xnT_made, b)
                dve.tensor_scalar(xn[:], x_all[:, b, :], mv[:, b, 0:1], rstd[:, bass.ds(b, 1)],
                                  ALU.subtract, ALU.mult).then_inc(xn_ready, 1)

            def leave_xnT(b, slot):
                dve.wait_ge(xnT_rounded, b + 1)
                if later(b):
                    dve.wait_ge(q_made, b)
                dve.tensor_tensor(xnT_lo[:].rearrange("p c s -> p (c s)"), p_x[:, 0:DC * S],
                                  xnT_hi[:].rearrange("p c s -> p (c s)").bitcast(F32), ALU.subtract).then_inc(xnT_left, 1)

            def bias_q(b, slot):
                dve.wait_ge(q_made, b + 1)
                if later(b):
                    dve.wait_ge(qT_made, b)
                twice = lambda t: t.rearrange("s (h d) -> s h d", h=H).unsqueeze(2).broadcast_to([S, H, 2, DK])
                dve.tensor_tensor(q_full[:], twice(p_x[0:S, 0:D]), twice(b_q[:]), ALU.add).then_inc(q_ready, 1)

            def leave_q(b, slot):
                dve.wait_ge(q_rounded, b + 1)
                if later(b):
                    dve.wait_ge(q_lo_placed[1 - slot], HP * 16 * in_turn(b - 1))
                dve.scalar_tensor_tensor(out=q_lo[:].rearrange("p t s -> p (t s)"), in0=p_x[:, 0:NT * S], scalar=DK ** -0.5,
                                         in1=q_hi[:].rearrange("p t s -> p (t s)").bitcast(F32), op0=ALU.mult,
                                         op1=ALU.subtract).then_inc(q_left, 1)

            def stack_k(b, slot, t):
                dve.wait_ge(k_rounded, NT * b + t + 1)
                if t == 0 and later(b, 2):
                    dve.wait_ge(sT_made, UNITS * (b - 1))
                dve.scalar_tensor_tensor(out=kT[:, slot, t, :], in0=p_k[(slot + t) % 2][:, 0:SCP], scalar=b_k[:, t:t + 1],
                                         in1=k_low[:, t % 2, :].bitcast(F32), op0=ALU.add,
                                         op1=ALU.subtract).then_inc(k_ready, 1)

            def find_max(b, slot, h):
                dve.wait_ge(s_made, H * b + h + 1)
                if h == 0 and later(b):
                    dve.wait_ge(max_split, 2 * b)
                t, a = divmod(h, HP)
                dve.tensor_reduce(nmax[:, t, a:a + 1], p_s[h % 2][0:S, 0:SC], X, ALU.max, negate=True).then_inc(max_ready, 1)

            def split_max(b, slot):
                dve.wait_ge(max_ready, H * (b + 1))
                if later(b):
                    dve.wait_ge(maxT_made, b)
                high, low = nmax2[:, :, 0:HP], nmax2[:, :, HP:2 * HP]
                dve.tensor_copy(high, nmax[:]).then_inc(max_split, 1)
                dve.wait_ge(max_split, 2 * b + 1)
                dve.tensor_tensor(low, nmax[:], high, ALU.subtract).then_inc(max_split, 1)

            def make_shift(b, slot):
                dve.wait_ge(maxT_made, b + 1)
                if later(b):
                    dve.wait_ge(sT_made, UNITS * b)
                dve.tensor_tensor(shift[:], p_x[:, :].bitcast(BF16)[:, 0:S].unsqueeze(1).broadcast_to([P, HP, S]),
                                  shift_mask[:], ALU.mult).then_inc(shift_ready, 1)

            def divide(b, slot):
                dve.wait_ge(back_made, b + 1)
                if later(b):
                    dve.wait_ge(oT_made, b)
                    dve.wait_ge(divided, 3 * b)
                pv = p_x[0:S, 0:H * V2].rearrange("q (h d) -> q h d", h=H)
                dve.reciprocal(rsum[:], pv[:, :, DK]).then_inc(divided, 1)
                dve.wait_ge(divided, 3 * b + 1)
                dve.tensor_tensor(o[:].rearrange("q (h d) -> q h d", h=H), pv[:, :, 0:DK],
                                  rsum[:].unsqueeze(2).broadcast_to([S, H, DK]), ALU.mult).then_inc(divided, 1)
                dve.wait_ge(divided, 3 * b + 2)
                dve.tensor_tensor(o[:], o[:], b_v[:], ALU.add).then_inc(divided, 1)

            def leave_oT(b, slot):
                dve.wait_ge(oT_rounded, b + 1)
                if later(b):
                    dve.wait_ge(out_made, b)
                dve.tensor_tensor(oT_lo[:].rearrange("p c s -> p (c s)"), p_x[:, 0:DC * S],
                                  oT_hi[:].rearrange("p c s -> p (c s)").bitcast(F32), ALU.subtract).then_inc(oT_left, 1)

            def add_to_x(b, slot):
                dve.wait_ge(out_made, b + 1)
                dve.wait_ge(bo_added, b + 1)
                dve.tensor_tensor(x_all[:, b, :], p_x[0:S, 0:D], x_all[:, b, :], ALU.add).then_inc(x_added, 1)

            def keep_stats(b, slot):
                dve.wait_ge(x_added, b + 1)
                dve.bn_stats(stats[:, b, :], x_all[:, b, :])

            part = lambda f, *a: (lambda b, slot: f(b, slot, *a))
            k = lambda t: (part(stack_k, t), 0)
            mx = lambda h: (part(find_max, h), 0)
            Stages(dve, [
                (make_shift, 1), k(0), k(1), k(2), (divide, 2), mx(0), k(3), mx(1), mx(2), mx(3), mx(4), mx(5),
                (leave_oT, 2), mx(6), mx(7), mx(8), mx(9), (add_to_x, 2), mx(10), (leave_xnT, -1), mx(11),
                (bias_q, -1), mx(12), mx(13), (leave_q, -1), (keep_stats, 2), mx(14), mx(15), (split_max, 0),
                (normalise, -2),
            ], B)

        @block.scalar
        def _(act):
            act.wait_ge(raw_in, 16 * len(names))
            for n in names:
                act.copy(w_hi[n][:], raw[n][:]).then_inc(w_rounded, 1)
            norm_on_scalar(act, rstd, norms, 1)
            act.wait_ge(cleared, N_CLEARED)
            act.wait_ge(biases, 1)

            def round_context(b, slot):
                act.wait_ge(context_in[slot], 16 * in_turn(b))
                if later(b):
                    act.wait_ge(v_made, NK * b)
                    act.wait_ge(ctx_left, b)
                act.copy(ctx_hi[:], context[:, slot]).then_inc(ctx_rounded, 1)

            def round_xnT(b, slot):
                act.wait_ge(xnT_made, b + 1)
                if later(b):
                    act.wait_ge(q_made, b)
                act.copy(xnT_hi[:].rearrange("p c s -> p (c s)"), p_x[:, 0:DC * S]).then_inc(xnT_rounded, 1)

            def round_q(b, slot):
                act.wait_ge(qT_made, b + 1)
                if later(b):
                    act.wait_ge(q_hi_placed[1 - slot], HP * 16 * in_turn(b - 1))
                act.activation(q_hi[:].rearrange("p t s -> p (t s)"), p_x[:, 0:NT * S], ACT.Copy, scale=DK ** -0.5).then_inc(q_rounded, 1)

            def round_k(b, slot, t):
                act.wait_ge(k_made, NT * b + t + 1)
                if t >= 2 or later(b):
                    act.wait_ge(k_ready, NT * b + t - 1)
                act.activation(k_low[:, t % 2, :], p_k[(slot + t) % 2][:, 0:SCP], ACT.Identity, bias=low_b_k[:, t:t + 1],
                               scale=is_low[:, 0:1]).then_inc(k_rounded, 1)

            def copy_v(b, slot, j):
                act.wait_ge(v_made, NK * b + j + 1)
                if j == 0 and later(b, 2):
                    act.wait_ge(pv_unit, UNITS * (b - 1))
                act.copy(v_aug[0:KEYS[j], slot, j, :, 0:DK],
                         p_k[(slot + NT + j) % 2][0:KEYS[j], 0:D].rearrange("k (h d) -> k h d", h=H)).then_inc(v_ready, 1)

            def exponentiate(b, slot, u):
                act.wait_ge(sT_made, UNITS * b + u + 1)
                if u >= ER or later(b):
                    act.wait_ge(pv_unit, UNITS * b + u + 1 - ER)
                nk = KEYS[u % NK]
                act.activation(eT[0:nk, u % ER].rearrange("k h q -> k (h q)"), p_e[u % 2][0:nk, 0:HP * S],
                               ACT.Exp).then_inc(e_ready, 1)

            def copy_o_raw(b, slot):
                act.wait_ge(pv_unit, UNITS * (b + 1))
                if later(b):
                    act.wait_ge(back_made, b)
                act.copy(o_raw[:].rearrange("p t s -> p (t s)"), p_o[:, 0:NT * S]).then_inc(o_raw_ready, 1)

            def round_oT(b, slot):
                act.wait_ge(oT_made, b + 1)
                if later(b):
                    act.wait_ge(out_made, b)
                act.copy(oT_hi[:].rearrange("p c s -> p (c s)"), p_x[:, 0:DC * S]).then_inc(oT_rounded, 1)

            part = lambda f, *a: (lambda b, slot: f(b, slot, *a))
            ex = lambda u: (part(exponentiate, u), 1)
            k = lambda t: (part(round_k, t), 0)
            v = lambda j: (part(copy_v, j), 0)
            Stages(act, [
                k(0), (copy_o_raw, 2), k(1), ex(0), k(2), ex(1), k(3), ex(2), v(0), ex(3), (round_oT, 2), v(1),
                ex(4), ex(5), v(2), ex(6), (round_xnT, -1), ex(7), (round_context, -1), ex(8), ex(9),
                (round_q, -1), ex(10), ex(11),
            ], B)

        @block.gpsimd
        def _(pool):
            pool.memset(qm_hi[:].bitcast(F32), 0.0).then_inc(cleared, 1)
            pool.memset(qm_lo[:].bitcast(F32), 0.0).then_inc(cleared, 1)

            def leave_context(b, slot):
                pool.wait_ge(ctx_rounded, b + 1)
                if later(b):
                    pool.wait_ge(v_made, NK * b)
                pool.tensor_tensor(ctx_lo[:], context[:, slot], ctx_hi[:].bitcast(F32), ALU.subtract).then_inc(ctx_left, 1)

            def add_bias_to_x(b, slot):
                pool.wait_ge(xn_ready, b + 1)
                pool.tensor_tensor(x_all[:, b, :], x_all[:, b, :], b_o[:], ALU.add).then_inc(bo_added, 1)

            pool.wait_ge(loaded, 16 * N_LOADS)
            Stages(pool, [(add_bias_to_x, 0), (leave_context, -1)], B)


def route(nc, x_all, mv, rstd, stats, norms, ident, p, first, xnT_hi, xnT_lo, scratch):
    with ExitStack() as ctx:
        sb = lambda n, shape, dt=F32: ctx.enter_context(nc.sbuf_tensor(f"rt_{n}", shape, dt))
        pb = lambda n, shape, dt=F32: ctx.enter_context(nc.psum_tensor(f"rt_{n}", shape, dt))
        sem = lambda n: ctx.enter_context(nc.semaphore(f"rt_{n}"))

        quads = [(c, range(e, e + 4)) for e in range(0, E, 4) for c in range(DC)]

        gamma = sb("gamma", [S, D])
        slot_gamma = sb("slot_gamma", [P, D])
        slots = sb("slots", [P, E, D])
        squares = sb("squares", [P, D])
        norm = sb("norm", [P, E])
        sn = sb("sn", [P, E, D])
        snT_hi = sb("snT_hi", [P, DC, E * P], F32R)
        snT_lo = sb("snT_lo", [P, DC, E * P], F32R)
        scale = sb("scale", [S, B])
        scaled = sb("scaled", [S, 2, D])
        xn = sb("xn", [S, 2, D])
        cur_hi = sb("cur_hi", [P, 2, DC, S], F32R)
        nmax = sb("nmax", [S, B])
        nmaxT = sb("nmaxT", [B, S])

        p_t = [pb(f"p_t{i}", [P, 512]) for i in range(2)]
        p_sn = [pb(f"p_sn{i}", [P, 512]) for i in range(2)]
        p_l = [pb(f"p_l{i}", [P, 2, 512]) for i in range(2)]

        loaded = sem("loaded")
        kept = sem("kept")
        squared = sem("squared")
        steps = sem("steps")
        rooted = sem("rooted")
        sn_ready = sem("sn_ready")
        snT_made = sem("snT_made")
        snT_rounded = sem("snT_rounded")
        snT_left = sem("snT_left")
        scaled_ready = sem("scaled_ready")
        xn_ready = sem("xn_ready")
        xn_kept = [sem("xn_kept0"), sem("xn_kept1")]
        xnT_made = sem("xnT_made")
        xnT_rounded = sem("xnT_rounded")
        xnT_kept = sem("xnT_kept")
        xnT_left = sem("xnT_left")
        logits_made = sem("logits_made")
        max_ready = sem("max_ready")
        maxT_made = sem("maxT_made")
        maxT_ready = sem("maxT_ready")
        block = ctx.enter_context(nc.Block())

        @block.sync
        def _(sp):
            sp.dma_start(slots[:], p["slots"]).then_inc(loaded, 16)
            sp.dma_start(gamma[:], p["gamma"].partition_broadcast(S)).then_inc(loaded, 16)
            sp.dma_start(slot_gamma[:], p["slot_gamma"].partition_broadcast(P)).then_inc(loaded, 16)
            sp.dma_start(scratch["x"], x_all[:]).then_inc(kept, 16)
            sp.dma_start(first["w1_raw"][:], p["w1"][0]).then_inc(first["w1_in"], 16)
            sp.dma_start(first["b1"][:], p["b1"]).then_inc(first["b1_in"], 16)
            sp.dma_start(first["b2"][:, 0, :], p["b2"][0:1, :].partition_broadcast(P)).then_inc(first["b2_in"], 16)
            sp.dma_start(first["w2_raw"][:], p["w2"][0]).then_inc(first["w2_in"], 16)

            sp.wait_ge(snT_rounded, len(quads))
            sp.dma_start(scratch["snT_hi"].bitcast(F32), snT_hi[:].bitcast(F32)).then_inc(kept, 16)
            sp.wait_ge(snT_left, len(quads))
            sp.dma_start(scratch["snT_lo"].bitcast(F32), snT_lo[:].bitcast(F32)).then_inc(kept, 16)

            def keep_xn(b, slot):
                sp.wait_ge(xn_ready, b + 1)
                sp.dma_start(scratch["xn"][b], xn[:, slot]).then_inc(xn_kept[slot], 16)

            Stages(sp, [(keep_xn, 0)], B)
            sp.wait_ge(maxT_ready, 1)
            sp.dma_start(scratch["nmax"], nmaxT[:]).then_inc(kept, 16)
            sp.wait_ge(kept, 64)
            sp.wait_ge(xn_kept[0], 16 * (B // 2))
            sp.wait_ge(xn_kept[1], 16 * (B // 2))

        @block.tensor
        def _(pe):
            pe.wait_ge(sn_ready, E)
            for n, (c, experts_of) in enumerate(quads):
                if n >= 2:
                    pe.wait_ge(snT_left, n - 1)
                for i, e in enumerate(experts_of):
                    mm = pe.transpose(p_sn[n % 2][:, i * P:(i + 1) * P], sn[:, e, c * P:(c + 1) * P], ident[:])
                mm.then_inc(snT_made, 1)
            pe.wait_ge(snT_rounded, len(quads))

            def transpose_xn(b, slot):
                pe.wait_ge(xn_ready, b + 1)
                if later(b, 2):
                    pe.wait_ge(xnT_left, b - 1)
                    pe.wait_ge(xnT_rounded, b - 1)
                for c in range(DC):
                    mm = pe.transpose(p_t[slot][:, c * S:(c + 1) * S], xn[:, slot, c * P:(c + 1) * P], ident[0:S, 0:S])
                mm.then_inc(xnT_made, 1)

            def logits(b, slot):
                pe.wait_ge(xnT_rounded, b + 1)
                if later(b, 2):
                    pe.wait_ge(max_ready, b - 1)
                for half in range(2):
                    cols = slice(half * 512, half * 512 + 512)
                    for c in range(DC):
                        mm = pe.matmul(p_l[slot][0:S, half, :], cur_hi[:, slot, c, :], snT_hi[:, c, cols],
                                       start=c == 0, stop=c == DC - 1)
                mm.then_inc(logits_made, 1)

            Stages(pe, [(transpose_xn, 0), (logits, 1)], B)
            pe.wait_ge(max_ready, B)
            pe.wait_ge(xnT_left, B)
            pe.transpose(p_t[0][0:B, 0:S], nmax[:], ident[0:S, 0:S]).then_inc(maxT_made, 1)

        @block.vector
        def _(dve):
            dve.wait_ge(squared, E)
            dve.wait_ge(rooted, 1)
            dve.tensor_scalar(norm[:], norm[:], 1e-12, None, ALU.max).then_inc(steps, 1)
            dve.wait_ge(steps, 1)
            dve.reciprocal(norm[:], norm[:]).then_inc(steps, 1)
            dve.wait_ge(steps, 2)
            dve.tensor_scalar(norm[:], norm[:], float(D) ** 0.5, None, ALU.mult).then_inc(steps, 1)
            dve.wait_ge(steps, 3)
            for e in range(E):
                dve.scalar_tensor_tensor(out=sn[:, e, :], in0=slots[:, e, :], scalar=norm[:, e:e + 1], in1=slot_gamma[:],
                                         op0=ALU.mult, op1=ALU.mult).then_inc(sn_ready, 1)

            norm_on_vector(dve, x_all, mv, rstd, stats, norms, 2)
            dve.tensor_tensor(scale[:], mv[:, :, 1], rstd[:], ALU.mult).then_inc(steps, 1)
            dve.wait_ge(steps, 4)
            dve.tensor_tensor(scale[:], scale[:], rstd[:], ALU.mult).then_inc(steps, 1)
            dve.wait_ge(steps, 5)
            dve.tensor_scalar(scale[:], scale[:], float(D), None, ALU.mult).then_inc(steps, 1)
            dve.wait_ge(rooted, 2)
            dve.tensor_scalar(scale[:], scale[:], 1e-12, None, ALU.max).then_inc(steps, 1)
            dve.wait_ge(steps, 7)
            dve.reciprocal(scale[:], scale[:]).then_inc(steps, 1)
            dve.wait_ge(steps, 8)
            dve.tensor_tensor(scale[:], scale[:], rstd[:], ALU.mult).then_inc(steps, 1)
            dve.wait_ge(steps, 9)
            dve.tensor_scalar(scale[:], scale[:], float(D) ** 0.5, None, ALU.mult).then_inc(steps, 1)
            dve.wait_ge(steps, 10)

            for n, (c, experts_of) in enumerate(quads):
                dve.wait_ge(snT_rounded, n + 1)
                cols = slice(experts_of[0] * P, (experts_of[-1] + 1) * P)
                dve.tensor_tensor(snT_lo[:, c, cols], p_sn[n % 2][:, :], snT_hi[:, c, cols].bitcast(F32),
                                  ALU.subtract).then_inc(snT_left, 1)

            def normalise(b, slot):
                if later(b, 2):
                    dve.wait_ge(xn_ready, b - 1)
                dve.tensor_scalar(scaled[:, slot], x_all[:, b, :], mv[:, b, 0:1], scale[:, bass.ds(b, 1)],
                                  ALU.subtract, ALU.mult).then_inc(scaled_ready, 1)

            def leave_xnT(b, slot):
                dve.wait_ge(xnT_rounded, b + 1)
                dve.tensor_tensor(xnT_lo[:, :, bass.ds(b * S, S)], p_t[slot][:, 0:DC * S].rearrange("p (c s) -> p c s", c=DC),
                                  cur_hi[:, slot].bitcast(F32), ALU.subtract).then_inc(xnT_left, 1)

            def find_max(b, slot):
                dve.wait_ge(logits_made, b + 1)
                dve.tensor_reduce(nmax[:, bass.ds(b, 1)], p_l[slot][0:S].rearrange("s a n -> s (a n)"), X, ALU.max,
                                  negate=True).then_inc(max_ready, 1)

            Stages(dve, [(normalise, -2), (leave_xnT, 0), (find_max, 1)], B)
            dve.wait_ge(maxT_made, 1)
            dve.tensor_copy(nmaxT[:], p_t[0][0:B, 0:S]).then_inc(maxT_ready, 1)

        @block.scalar
        def _(act):
            act.wait_ge(loaded, 48)
            for e in range(E):
                if e:
                    act.wait_ge(squared, e)
                act.activation(squares[:], slots[:, e, :], ACT.Square, accum_out=norm[:, e:e + 1]).then_inc(squared, 1)
            act.wait_ge(squared, E)
            act.activation(norm[:], norm[:], ACT.Sqrt).then_inc(rooted, 1)
            norm_on_scalar(act, rstd, norms, 2)
            act.wait_ge(steps, 6)
            act.activation(scale[:], scale[:], ACT.Sqrt).then_inc(rooted, 1)
            for n, (c, experts_of) in enumerate(quads):
                act.wait_ge(snT_made, n + 1)
                cols = slice(experts_of[0] * P, (experts_of[-1] + 1) * P)
                act.copy(snT_hi[:, c, cols], p_sn[n % 2][:, :]).then_inc(snT_rounded, 1)

            def round_xnT(b, slot):
                act.wait_ge(xnT_made, b + 1)
                if later(b, 2):
                    act.wait_ge(logits_made, b - 1)
                    act.wait_ge(xnT_left, b - 1)
                    act.wait_ge(xnT_kept, b - 1)
                act.copy(cur_hi[:, slot].rearrange("p c s -> p (c s)"), p_t[slot][:, 0:DC * S]).then_inc(xnT_rounded, 1)
                act.wait_ge(xnT_rounded, b + 1)
                act.copy(xnT_hi[:, :, bass.ds(b * S, S)], cur_hi[:, slot].bitcast(F32)).then_inc(xnT_kept, 1)

            Stages(act, [(round_xnT, 0)], B)

        @block.gpsimd
        def _(pool):
            pool.wait_ge(loaded, 48)

            def apply_gamma(b, slot):
                pool.wait_ge(scaled_ready, b + 1)
                if later(b, 2):
                    pool.wait_ge(xn_kept[slot], 16 * (b // 2))
                    pool.wait_ge(xnT_made, b - 1)
                pool.tensor_tensor(xn[:, slot], scaled[:, slot], gamma[:], ALU.mult).then_inc(xn_ready, 1)

            Stages(pool, [(apply_gamma, -1)], B)


def experts(nc, y_all, ident, p, first, xnT_hi, xnT_lo, scratch, out_rows):
    with ExitStack() as ctx:
        sb = lambda n, shape, dt=F32: ctx.enter_context(nc.sbuf_tensor(f"ex_{n}", shape, dt))
        pb = lambda n, shape, dt=F32: ctx.enter_context(nc.psum_tensor(f"ex_{n}", shape, dt))
        sem = lambda n: ctx.enter_context(nc.semaphore(f"ex_{n}"))
        N = GB * S
        R = GB * P

        w1_raw, w2_raw, b1, b2 = (first[n] for n in ("w1_raw", "w2_raw", "b1", "b2"))
        w1_hi = sb("w1_hi", [P, DC, HID], F32R)
        w1_lo = sb("w1_lo", [P, DC, HID], F32R)
        w2_hi = sb("w2_hi", [P, HC, D], F32R)
        w2_lo = sb("w2_lo", [P, HC, D], F32R)
        b1_now = sb("b1_now", [P, HC])
        snT_hi = sb("snT_hi", [P, DC, P], F32R)
        snT_lo = sb("snT_lo", [P, DC, P], F32R)
        nmax = sb("nmax", [P, N])
        xn = sb("xn", [S, GB, D])
        x = sb("x", [S, GB, D])
        over = sb("over", [P, GB])
        dispatch = sb("dispatch", [P, GB, S])
        dsum = sb("dsum", [P, GB])
        dispatchT = sb("dispatchT", [S, GB, P])
        lag_c = sb("lag_c", [P, 2, N])
        combine = sb("combine", [P, GB, S])
        slots_hi = sb("slots_hi", [P, DC, R], F32R)
        slots_lo = sb("slots_lo", [P, DC, R], F32R)
        h = sb("h", [P, 2, R])
        h_hi = sb("h_hi", [P, HC, R], F32R)
        h_lo = sb("h_lo", [P, HC, R], F32R)
        eo = sb("eo", [P, GB, D + 1])
        inv = sb("inv", [S, GB])

        p_h = [pb(f"p_h{i}", [P, 512]) for i in range(3)]
        p_e = [pb(f"p_e{i}", [P, 512]) for i in range(2)]
        p_c = pb("p_c", [P, 512])
        p_l = pb("p_l", [P, 512])
        p_x = pb("p_x", [P, 512])

        cleared = sem("cleared")
        b1_in, b2_in, w1_in, w2_in = (first[n] for n in ("b1_in", "b2_in", "w1_in", "w2_in"))
        b1_ready = sem("b1_ready")
        sn_in = sem("sn_in")
        nmax_in = sem("nmax_in")
        xn_in = sem("xn_in")
        x_in = sem("x_in")
        out_kept = sem("out_kept")
        w1_split = sem("w1_split")
        w1_lost = sem("w1_lost")
        w2_split = sem("w2_split")
        w2_lost = sem("w2_lost")
        l_made = sem("l_made")
        over_ready = sem("over_ready")
        d_shifted = sem("d_shifted")
        c_shifted = sem("c_shifted")
        d_exp = sem("d_exp")
        dsum_ready = sem("dsum_ready")
        d_ready = sem("d_ready")
        dT_made = sem("dT_made")
        dT_ready = sem("dT_ready")
        c_ready = sem("c_ready")
        slots_made = sem("slots_made")
        slots_rounded = sem("slots_rounded")
        slots_left = sem("slots_left")
        h_made = sem("h_made")
        h_ready = sem("h_ready")
        h_rounded = sem("h_rounded")
        h_left = sem("h_left")
        e_made = sem("e_made")
        e_ready = sem("e_ready")
        c_made = sem("c_made")
        y_added = sem("y_added")
        inv_ready = sem("inv_ready")
        out_ready = sem("out_ready")

        block = ctx.enter_context(nc.Block())

        def over_units(engine, unit):
            for e in (0, None, E - 1):
                with ExitStack() as loop:
                    if e is None:
                        e = loop.enter_context(engine.Fori(1, E - 1))
                    unit(e, 0, e, 1)
                    with engine.Fori(1, G - 1) as g:
                        unit(e, g, e, g + 1)
                    last = isinstance(e, int) and e == E - 1
                    unit(e, G - 1, None if last else e + 1, None if last else 0)

        def starts(g):
            return isinstance(g, int) and g == 0

        def ends(e):
            return isinstance(e, int) and e == E - 1

        def group_before(g):
            return G - 1 if starts(g) else g - 1

        @block.sync
        def _(sp):
            def load_slots(e):
                if later(e):
                    sp.wait_ge(l_made, G * e)
                sp.dma_start(snT_hi[:].bitcast(F32), scratch["snT_hi"][:, :, bass.ds(e * P, P)].bitcast(F32)).then_inc(sn_in, 16)
                sp.dma_start(snT_lo[:].bitcast(F32), scratch["snT_lo"][:, :, bass.ds(e * P, P)].bitcast(F32)).then_inc(sn_in, 16)

            def load_w1(e):
                sp.wait_ge(w1_split, e)
                sp.wait_ge(w1_lost, e)
                sp.dma_start(w1_raw[:], p["w1"][e]).then_inc(w1_in, 16)

            def load_w2(e):
                sp.wait_ge(w2_split, e)
                sp.wait_ge(w2_lost, e)
                sp.dma_start(w2_raw[:], p["w2"][e]).then_inc(w2_in, 16)

            def load_b2(e):
                if later(e, 2):
                    sp.wait_ge(e_ready, GB * G * (e - 1))
                sp.dma_start(b2[:, e % 2, :], p["b2"][bass.ds(e, 1), :].partition_broadcast(P)).then_inc(b2_in, 16)

            def load_tokens(e, g):
                u = e * G + g
                if later(u):
                    sp.wait_ge(c_shifted, u)
                sp.dma_start(nmax[:].rearrange("p (b s) -> p b s", b=GB),
                             scratch["nmax"][bass.ds(g * GB, GB), :].partition_broadcast(P)).then_inc(nmax_in, 16)
                if later(u):
                    sp.wait_ge(slots_made, DC * u)
                sp.dma_start(xn[:], scratch["xn_units"][:, bass.ds(g * GB, GB), :]).then_inc(xn_in, 16)

            def load_x(g):
                if later(g):
                    sp.wait_ge(out_ready, GB * g)
                sp.dma_start(x[:], scratch["x"][:, bass.ds(g * GB, GB), :]).then_inc(x_in, 16)

            def keep_out(g):
                sp.wait_ge(out_ready, GB * (g + 1))
                sp.dma_start(out_rows[:, bass.ds(g * GB, GB), :],
                             y_all[:, bass.ds(g * GB, GB), 0:D]).then_inc(out_kept, 16)

            load_slots(0)
            load_tokens(0, 0)

            def unit(e, g, e2, g2):
                if starts(g) and not ends(e):
                    load_w1(e + 1)
                    load_b2(e + 1)
                if starts(g2):
                    load_slots(e2)
                if e2 is not None:
                    load_tokens(e2, g2)
                if starts(g) and not ends(e):
                    load_w2(e + 1)
                if ends(e):
                    if not starts(g):
                        keep_out(g - 1)
                    load_x(g)

            over_units(sp, unit)
            keep_out(G - 1)
            sp.wait_ge(out_kept, 16 * G)

        @block.tensor
        def _(pe):
            def logits(e, g):
                u = e * G + g
                pe.wait_ge(sn_in, 32 * (e + 1))
                if later(u):
                    pe.wait_ge(slots_left, DC * u)
                    pe.wait_ge(slots_rounded, DC * u)
                n = 0
                for c in range(DC):
                    for a, t in ((snT_hi, xnT_hi), (snT_lo, xnT_hi), (snT_hi, xnT_lo)):
                        mm = pe.matmul(p_l[:, 0:N], a[:, c, :], t[:, c, bass.ds(g * N, N)], start=n == 0, stop=n == 3 * DC - 1)
                        n += 1
                mm.then_inc(l_made, 1)

            def transpose_dispatch(e, g):
                u = e * G + g
                pe.wait_ge(d_ready, u + 1)
                pe.wait_ge(c_shifted, u + 1)
                for b in range(GB):
                    mm = pe.transpose(p_l[0:S, b * P:(b + 1) * P], dispatch[:, b, :], ident[:])
                mm.then_inc(dT_made, 1)

            def fill_slots(e, g, c):
                u = e * G + g
                if c == 0:
                    pe.wait_ge(dT_ready, u + 1)
                    pe.wait_ge(xn_in, 16 * (u + 1))
                    if later(u):
                        pe.wait_ge(slots_left, DC * (u - 1) + 1)
                to = p_x if c == 0 else p_l
                for b in range(GB):
                    mm = pe.matmul(to[:, b * P:(b + 1) * P], xn[:, b, c * P:(c + 1) * P], dispatchT[:, b, :],
                                   start=True, stop=True)
                mm.then_inc(slots_made, 1)

            def layer_1(e, g, m):
                u = e * G + g
                if m == 0:
                    pe.wait_ge(slots_left, DC * (u + 1))
                    pe.wait_ge(slots_rounded, DC * (u + 1))
                    pe.wait_ge(w1_split, e + 1)
                    pe.wait_ge(w1_lost, e + 1)
                if m >= 3:
                    pe.wait_ge(h_ready, HC * u + m - 2)
                elif later(u):
                    pe.wait_ge(h_ready, HC * (u - 1) + M3[m])
                cols = slice(m * P, (m + 1) * P)
                n = 0
                for c in range(DC):
                    for w, a in ((w1_hi, slots_hi), (w1_lo, slots_hi), (w1_hi, slots_lo)):
                        mm = pe.matmul(p_h[m % 3][:, 0:R], w[:, c, cols], a[:, c, :], start=n == 0, stop=n == 3 * DC - 1)
                        n += 1
                mm.then_inc(h_made, 1)

            def layer_2(e, g, b):
                u = e * G + g
                if b == 0:
                    pe.wait_ge(w2_split, e + 1)
                    pe.wait_ge(w2_lost, e + 1)
                if b >= 2 or later(u):
                    pe.wait_ge(e_ready, GB * u + b - 1)
                rows = slice(b * P, (b + 1) * P)
                for m in range(HC):
                    if b == 0:
                        pe.wait_ge(h_left, HC * u + m + 1)
                    for n, (a, w) in enumerate(((h_hi, w2_hi), (h_lo, w2_hi), (h_hi, w2_lo))):
                        mm = pe.matmul(p_e[b % 2][:, 0:D], a[:, m, rows], w[:, m, :], start=m == 0 and n == 0,
                                       stop=m == HC - 1 and n == 2)
                mm.then_inc(e_made, 1)

            def combine_batch(u, b):
                pe.wait_ge(e_ready, GB * u + b + 1)
                if b == 0:
                    pe.wait_ge(c_ready, u + 1)
                if b > 0 or later(u):
                    pe.wait_ge(y_added, GB * u + b)
                pe.matmul(p_c[0:S, 0:D + 1], combine[:, b, :], eo[:, b, :], start=True, stop=True).then_inc(c_made, 1)

            def unit(e, g, e2, g2):
                u = e * G + g
                more = e2 is not None
                if more:
                    logits(e2, g2)
                if later(u):
                    combine_batch(u - 1, GB - 1)
                for m in range(HC):
                    layer_1(e, g, m)
                layer_2(e, g, 0)
                layer_2(e, g, 1)
                if more:
                    transpose_dispatch(e2, g2)
                layer_2(e, g, 2)
                combine_batch(u, 0)
                if more:
                    fill_slots(e2, g2, 0)
                    fill_slots(e2, g2, 1)
                combine_batch(u, 1)
                layer_2(e, g, 3)
                combine_batch(u, 2)

            logits(0, 0)
            transpose_dispatch(0, 0)
            fill_slots(0, 0, 0)
            fill_slots(0, 0, 1)
            over_units(pe, unit)
            combine_batch(E * G - 1, GB - 1)

        @block.vector
        def _(dve):
            dve.memset(eo[:, :, D], 1.0).then_inc(cleared, 1)

            def shift(e, g):
                u = e * G + g
                dve.wait_ge(l_made, u + 1)
                rows = p_l[:, 0:N].rearrange("p (b s) -> p b s", b=GB)
                dve.tensor_reduce(over[:], rows, X, ALU.max).then_inc(over_ready, 1)
                dve.wait_ge(nmax_in, 16 * (u + 1))
                if later(u, 2):
                    dve.wait_ge(c_ready, u - 1)
                dve.tensor_tensor(lag_c[:, u % 2, :], p_l[:, 0:N], nmax[:], ALU.add).then_inc(c_shifted, 1)
                dve.wait_ge(over_ready, u + 1)
                if later(u):
                    dve.wait_ge(dT_made, u)
                dve.tensor_tensor(dispatch[:], rows, over[:].unsqueeze(2).broadcast_to([P, GB, S]),
                                  ALU.subtract).then_inc(d_shifted, 1)

            def sum_dispatch(e, g):
                u = e * G + g
                dve.wait_ge(d_exp, u + 1)
                dve.tensor_reduce(dsum[:], dispatch[:], X, ALU.add).then_inc(dsum_ready, 1)
                dve.wait_ge(dsum_ready, 2 * u + 1)
                dve.reciprocal(dsum[:], dsum[:]).then_inc(dsum_ready, 1)
                dve.wait_ge(dsum_ready, 2 * u + 2)
                dve.tensor_tensor(dispatch[:], dispatch[:], dsum[:].unsqueeze(2).broadcast_to([P, GB, S]),
                                  ALU.mult).then_inc(d_ready, 1)

            def leave_slots(e, g, c):
                u = e * G + g
                dve.wait_ge(slots_rounded, DC * u + c + 1)
                frm = p_x if c == 0 else p_l
                dve.tensor_tensor(slots_lo[:, c, :], frm[:, 0:R], slots_hi[:, c, :].bitcast(F32),
                                  ALU.subtract).then_inc(slots_left, 1)

            def split_h(e, g, m):
                u = e * G + g
                dve.wait_ge(h_ready, HC * u + m + 1)
                if m == 0 and later(u):
                    dve.wait_ge(e_made, GB * u)
                dve.tensor_copy(h_hi[:, m, :], h[:, m % 2, :]).then_inc(h_rounded, 1)
                dve.wait_ge(h_rounded, HC * u + m + 1)
                dve.tensor_tensor(h_lo[:, m, :], h[:, m % 2, :], h_hi[:, m, :].bitcast(F32), ALU.subtract).then_inc(h_left, 1)

            def leave_w1(e):
                dve.wait_ge(w1_split, e + 1)
                dve.tensor_tensor(w1_lo[:].rearrange("p a b -> p (a b)"), w1_raw[:].rearrange("p a b -> p (a b)"),
                                  w1_hi[:].rearrange("p a b -> p (a b)").bitcast(F32), ALU.subtract).then_inc(w1_lost, 1)

            def add_bias(e, g, b):
                u = e * G + g
                dve.wait_ge(e_made, GB * u + b + 1)
                if b == 0:
                    dve.wait_ge(b2_in, 16 * (e + 1))
                if later(u):
                    dve.wait_ge(c_made, GB * (u - 1) + b + 1)
                dve.tensor_tensor(eo[:, b, 0:D], p_e[b % 2][:, 0:D], b2[:, e % 2, :], ALU.add).then_inc(e_ready, 1)

            def add_to_y(u, g, b):
                dve.wait_ge(c_made, GB * u + b + 1)
                at = g * GB + b
                dve.tensor_tensor(y_all[:, at, :], p_c[0:S, 0:D + 1], y_all[:, at, :], ALU.add).then_inc(y_added, 1)

            def finish(g):
                dve.wait_ge(y_added, GB * ((E - 1) * G + g + 1))
                if later(g):
                    dve.wait_ge(out_ready, GB * g)
                dve.reciprocal(inv[:], y_all[:, bass.ds(g * GB, GB), D]).then_inc(inv_ready, 1)
                dve.wait_ge(inv_ready, g + 1)
                dve.wait_ge(x_in, 16 * (g + 1))
                for b in range(GB):
                    at = g * GB + b
                    dve.scalar_tensor_tensor(out=y_all[:, at, 0:D], in0=y_all[:, at, 0:D], scalar=inv[:, b:b + 1],
                                             in1=x[:, b, :], op0=ALU.mult, op1=ALU.add).then_inc(out_ready, 1)

            def unit(e, g, e2, g2):
                u = e * G + g
                more = e2 is not None
                if starts(g):
                    if later(e):
                        dve.wait_ge(h_ready, HC * G * e)
                    dve.tensor_copy(b1_now[:], b1[:, e, :]).then_inc(b1_ready, 1)
                if more:
                    shift(e2, g2)
                if later(u):
                    add_to_y(u - 1, group_before(g), GB - 1)
                for m in range(HC):
                    split_h(e, g, m)
                    if m == 3 and ends(e) and not starts(g):
                        finish(g - 1)
                add_bias(e, g, 0)
                if more:
                    sum_dispatch(e2, g2)
                add_bias(e, g, 1)
                if more and starts(g2):
                    leave_w1(e2)
                add_bias(e, g, 2)
                add_to_y(u, g, 0)
                if more:
                    leave_slots(e2, g2, 0)
                    leave_slots(e2, g2, 1)
                add_to_y(u, g, 1)
                add_bias(e, g, 3)
                add_to_y(u, g, 2)

            dve.wait_ge(b1_in, 16)
            shift(0, 0)
            sum_dispatch(0, 0)
            leave_w1(0)
            leave_slots(0, 0, 0)
            leave_slots(0, 0, 1)
            dve.wait_ge(cleared, 2)
            over_units(dve, unit)
            add_to_y(E * G - 1, G - 1, GB - 1)
            finish(G - 1)

        @block.scalar
        def _(act):
            def exp_dispatch(e, g):
                u = e * G + g
                act.wait_ge(d_shifted, u + 1)
                act.activation(dispatch[:], dispatch[:], ACT.Exp).then_inc(d_exp, 1)

            def copy_dispatch(e, g):
                u = e * G + g
                act.wait_ge(dT_made, u + 1)
                if later(u):
                    act.wait_ge(slots_made, DC * u)
                act.copy(dispatchT[:].rearrange("s b p -> s (b p)"), p_l[0:S, 0:R]).then_inc(dT_ready, 1)

            def exp_combine(e, g):
                u = e * G + g
                act.wait_ge(c_shifted, u + 1)
                if later(u):
                    act.wait_ge(c_made, GB * u)
                act.activation(combine[:].rearrange("p b s -> p (b s)"), lag_c[:, u % 2, :], ACT.Exp).then_inc(c_ready, 1)

            def round_slots(e, g, c):
                u = e * G + g
                act.wait_ge(slots_made, DC * u + c + 1)
                if c == 0 and later(u):
                    act.wait_ge(h_made, HC * u)
                act.copy(slots_hi[:, c, :], (p_x if c == 0 else p_l)[:, 0:R]).then_inc(slots_rounded, 1)

            def gelu(e, g, m):
                u = e * G + g
                act.wait_ge(h_made, HC * u + m + 1)
                if m == 0:
                    act.wait_ge(b1_ready, e + 1)
                if m >= 2 or later(u):
                    act.wait_ge(h_left, HC * u + m - 1)
                act.activation(h[:, m % 2, :], p_h[m % 3][:, 0:R], ACT.Gelu, bias=b1_now[:, m:m + 1]).then_inc(h_ready, 1)

            def round_w(e, raw, hi, arrived, split):
                act.wait_ge(arrived, 16 * (e + 1))
                act.copy(hi[:].rearrange("p a b -> p (a b)"), raw[:].rearrange("p a b -> p (a b)")).then_inc(split, 1)

            def unit(e, g, e2, g2):
                u = e * G + g
                more = e2 is not None
                for m in range(HC):
                    gelu(e, g, m)
                    if m == 1 and starts(g):
                        if later(u):
                            act.wait_ge(e_made, GB * u)
                        round_w(e, w2_raw, w2_hi, w2_in, w2_split)
                if more:
                    exp_dispatch(e2, g2)
                exp_combine(e, g)
                if more:
                    if starts(g2):
                        round_w(e2, w1_raw, w1_hi, w1_in, w1_split)
                    copy_dispatch(e2, g2)
                    round_slots(e2, g2, 0)
                    round_slots(e2, g2, 1)

            exp_dispatch(0, 0)
            round_w(0, w1_raw, w1_hi, w1_in, w1_split)
            copy_dispatch(0, 0)
            round_slots(0, 0, 0)
            round_slots(0, 0, 1)
            over_units(act, unit)

        @block.gpsimd
        def _(pool):
            pool.memset(y_all[:], 0.0).then_inc(cleared, 1)

            def leave_w2(e):
                pool.wait_ge(w2_split, e + 1)
                pool.tensor_tensor(w2_lo[:].rearrange("p a b -> p (a b)"), w2_raw[:].rearrange("p a b -> p (a b)"),
                                   w2_hi[:].rearrange("p a b -> p (a b)").bitcast(F32), ALU.subtract).then_inc(w2_lost, 1)

            with pool.Fori(0, E) as e:
                leave_w2(e)


def decoder_layer(nc, x, wqkv, wo, cos, sin, causal, causal_t, ident_f32, ident_bf16, ctx_t, shift_mask, xw_q, xw_k, xw_v, xw_o,
                  xb_q, xb_k, xb_v, xb_o, is_low, gamma, slot_gamma, slots, w1, w2, b1, b2, out):
    with ExitStack() as ctx:
        sb = lambda n, shape, dt=F32: ctx.enter_context(nc.sbuf_tensor(n, shape, dt))
        dram = lambda n, shape, dt=F32: nc.dram_tensor(n, shape, dt, kind="Internal").ap()
        y_all = sb("y_all", [S, B, D + 1])
        x_all = y_all[:, :, 0:D]
        mv = sb("mv", [S, B, 2])
        rstd = sb("rstd", [S, B])
        stats = sb("stats", [S, B, 6])
        ident = sb("ident", [P, P])
        ident16 = sb("ident16", [P, P], BF16)
        norms = norm_semaphores(nc, ctx)

        self_attention(nc, x, x_all, mv, rstd, stats, norms, ident, ident16, ident_f32, ident_bf16, wqkv, wo, cos, sin,
                       causal, causal_t, is_low, shift_mask)
        cross_attention(nc, x_all, mv, rstd, stats, norms, ident, ident16, ctx_t,
                        dict(w_q=xw_q, w_k=xw_k, w_v=xw_v, w_o=xw_o, b_q=xb_q, b_k=xb_k, b_v=xb_v, b_o=xb_o,
                             is_low=is_low), shift_mask)

        ffn = dict(gamma=gamma, slot_gamma=slot_gamma, slots=slots, w1=w1, w2=w2, b1=b1, b2=b2)
        xn = dram("xn_tokens", (B, S, D))
        scratch = dict(snT_hi=dram("sn_t_hi", (P, DC, E * P), F32R), snT_lo=dram("sn_t_lo", (P, DC, E * P), F32R),
                       x=dram("x_tokens", (S, B, D)), xn=xn, xn_units=xn.rearrange("b s d -> s b d"),
                       nmax=dram("token_nmax", (B, S)))
        xnT_hi = sb("xnT_hi", [P, DC, B * S], F32R)
        xnT_lo = sb("xnT_lo", [P, DC, B * S], F32R)
        first = dict(w1_raw=sb("w1_raw", [P, DC, HID]), w2_raw=sb("w2_raw", [P, HC, D]), b1=sb("b1", [P, E, HC]),
                     b2=sb("b2", [P, 2, D]))
        for n in ("w1_in", "w2_in", "b1_in", "b2_in"):
            first[n] = ctx.enter_context(nc.semaphore(n))
        route(nc, x_all, mv, rstd, stats, norms, ident, ffn, first, xnT_hi, xnT_lo, scratch)
        experts(nc, y_all, ident, ffn, first, xnT_hi, xnT_lo, scratch, out.rearrange("b s d -> s b d"))


def constants():
    inv_freq = (np.float32(10000.0) ** (-np.arange(DK // 2, dtype=np.float32) * np.float32(2.0) / DK)).astype(np.float32)
    angle = np.arange(S, dtype=np.float32)[:, None] * inv_freq[None, :]
    cos, sin = np.cos(angle).astype(np.float32), np.sin(angle).astype(np.float32)
    bf16 = mybir.dt.np(BF16)
    causal = np.where(np.tril(np.ones((S, S), bool)), 0.0, -3e38)
    heads = lambda a: np.repeat(a[:, None, :], HP, axis=1).astype(bf16)
    shift_mask = np.zeros((NT, 2 * DK, HP, S), np.float32)
    for hp in range(HP):
        shift_mask[:, [hp, HP + hp], hp] = 1.0
    return dict(
        cos=np.tile(np.repeat(cos, 2, axis=1), (1, 2 * H)),
        sin=np.tile(np.stack([-sin, sin], axis=-1).reshape(S, DK), (1, 2 * H)),
        causal=heads(causal), causal_t=heads(causal.T),
        ident_f32=np.eye(P, dtype=np.float32),
        ident_bf16=np.eye(P).astype(bf16),
        is_low=np.tile(np.repeat(np.array([0.0, 1.0], np.float32), DK), HP).reshape(P, 1),
        shift_mask=shift_mask.reshape(P, HP, S))


def kernel(**inputs):
    import concourse.bacc as _bacc
    from concourse.bass_utils import run_bass_kernel_spmd as _run

    given = {name: np.asarray(a) for name, a in inputs.items()}
    attn = lambda n: given["L0_attn_" + n]
    xattn = lambda n: given["L0_xattn_" + n]
    ffn = lambda n: given["L0_ffn_" + n]
    rows = lambda w: w.reshape(DC, P, -1).transpose(1, 0, 2)

    twice = lambda a: np.repeat(a.reshape(-1, H, 1, DK), 2, axis=2).reshape(-1, 2 * D)
    context = np.zeros((B, P, DC, SCP), given["ctx_1024"].dtype)
    context[..., 0:SC] = given["ctx_1024"].transpose(0, 2, 1).reshape(B, DC, P, SC).transpose(0, 2, 1, 3)

    arrays = dict(
        x=given["x"],
        wqkv=rows(np.concatenate([attn("Wq").T, attn("Wk").T, attn("Wv").T], axis=1)),
        wo=rows(attn("Wo").T),
        ctx_t=context, xw_q=rows(xattn("Wq")), xw_k=rows(twice(xattn("Wk"))),
        xw_v=rows(xattn("Wv")), xw_o=rows(xattn("Wo")),
        xb_q=xattn("bq"), xb_k=twice(xattn("bk")).reshape(-1, P).T,
        xb_v=xattn("bv"), xb_o=xattn("bo"),
        gamma=ffn("norm_gamma"), slot_gamma=ffn("slot_norm_gamma"), slots=ffn("slot_embeds").transpose(1, 0, 2),
        w1=ffn("w1").reshape(E, DC, P, HID).transpose(0, 2, 1, 3),
        w2=ffn("w2").reshape(E, HC, P, D).transpose(0, 2, 1, 3),
        b1=ffn("b1").reshape(E, HC, P).transpose(2, 0, 1), b2=ffn("b2"),
        **constants())

    nc = _bacc.Bacc("TRN2", target_bir_lowering=False, num_devices=1)
    feeds, args = {}, {}
    for name, a in arrays.items():
        feeds[f"in_{name}_dram"] = a = np.ascontiguousarray(a)
        args[name] = nc.dram_tensor(f"in_{name}_dram", a.shape, mybir.dt.from_np(a.dtype), kind="ExternalInput").ap()
    out = nc.dram_tensor("out_0_dram", (B, S, D), F32, kind="ExternalOutput").ap()
    decoder_layer(nc, out=out, **args)
    return _run(nc, [feeds], core_ids=[0]).results[0]["out_0_dram"]
```
